# Optimizing a Trainium2 kernel written in Bass

```python
import numpy as np
import jax
import jax.numpy as jnp

def _softmax(x, axis=-1):
    return jax.nn.softmax(x, axis=axis)

def _gelu(x):
    return jax.nn.gelu(x, approximate=True)

def _silu(x):
    return jax.nn.silu(x)

def _sigmoid(x):
    return jax.nn.sigmoid(x)

def _layernorm(x, axis=-1, eps=1e-05):
    m = jnp.mean(x, axis=axis, keepdims=True)
    v = jnp.var(x, axis=axis, keepdims=True)
    return (x - m) / jnp.sqrt(v + eps)

def _scatter_add(tgt, idx, src, axis=0):
    return tgt.at[idx].add(src)

def _segment_sum(src, seg, n):
    return jax.ops.segment_sum(src, seg, n)
kernel_name = 'mk_prb_d2_jaxref_r4_1c6bb7'

def setup_inputs(seed: int=0):
    np.random.seed(seed)
    _w = jnp.asarray

    def _L0_attn_setup():
        import jax, jax.numpy as jnp
        import numpy as np
        B, S, D, H, FACTOR = (1, 512, 256, 16, 16)
        HD = D // H
        key = jax.random.key(seed)
        ks = jax.random.split(key, 9)
        s = 1.0 / np.sqrt(D)
        u = lambda k, shape: jax.random.uniform(k, shape, jnp.float32, -s, s)
        return {'x': jax.random.normal(ks[0], (B, S, D), jnp.float32), 'Wq': u(ks[1], (D, D)), 'bq': u(ks[2], (D,)), 'Wk': u(ks[3], (D, D)), 'bk': u(ks[4], (D,)), 'Wv': u(ks[5], (D, D)), 'bv': u(ks[6], (D,)), 'Wo': u(ks[7], (D, D)), 'bo': u(ks[8], (D,))}
    _L0_attn_in = _L0_attn_setup()

    def _L0_ffn_setup():
        import jax, jax.numpy as jnp
        import numpy as np
        D_MODEL = 256
        NUM_HEADS = 4
        NUM_EXPERTS = 8
        TOP_K = 2
        D_FF = 256
        EPS = 1e-06

        def _rmsnorm(x, g):
            return x * jax.lax.rsqrt(jnp.mean(x * x, axis=-1, keepdims=True) + EPS) * g

        def _swiglu(x, w1, w2, w3):
            return jax.nn.silu(x @ w1.T) * (x @ w3.T) @ w2.T
        key = jax.random.key(seed)
        ks = jax.random.split(key, 16)
        d, e, f = (D_MODEL, NUM_EXPERTS, D_FF)
        dc = d // 4
        s = 0.02
        return {'X': jax.random.normal(ks[0], (2, 256, d), dtype=jnp.float32), 'g1': jnp.ones((d,), jnp.float32), 'g2': jnp.ones((d,), jnp.float32), 'Wq': jax.random.normal(ks[1], (d, d), jnp.float32) * s, 'Wkc': jax.random.normal(ks[2], (dc, d), jnp.float32) * s, 'Wvc': jax.random.normal(ks[3], (dc, d), jnp.float32) * s, 'Wo': jax.random.normal(ks[4], (d, d), jnp.float32) * s, 'Wr': jax.random.normal(ks[5], (e, d), jnp.float32) * s, 'expert_bias': jnp.zeros((e,), jnp.float32), 'sW1': jax.random.normal(ks[6], (f, d), jnp.float32) * s, 'sW2': jax.random.normal(ks[7], (d, f), jnp.float32) * s, 'sW3': jax.random.normal(ks[8], (f, d), jnp.float32) * s, 'eW1': jax.random.normal(ks[9], (e, f, d), jnp.float32) * s, 'eW2': jax.random.normal(ks[10], (e, d, f), jnp.float32) * s, 'eW3': jax.random.normal(ks[11], (e, f, d), jnp.float32) * s}
    _L0_ffn_in = _L0_ffn_setup()

    def _L1_attn_setup():
        import jax, jax.numpy as jnp
        import numpy as np
        DIM = 256
        key = jax.random.key(seed)
        k1, k2, k3, k4 = jax.random.split(key, 4)
        x = jax.random.normal(k1, (4, 512, DIM), dtype=jnp.float32)
        wk = jax.random.normal(k2, (DIM, DIM), dtype=jnp.float32) * 0.02
        wq = jax.random.normal(k3, (DIM, DIM), dtype=jnp.float32) * 0.02
        wv = jax.random.normal(k4, (DIM, DIM), dtype=jnp.float32) * 0.02
        return {'x': x, 'wk': wk, 'wq': wq, 'wv': wv}
    _L1_attn_in = _L1_attn_setup()

    def _L1_ffn_setup():
        import jax, jax.numpy as jnp
        import numpy as np
        HIDDEN = 256
        NUM_EXPERTS = 8
        EXPERT = 512
        TOP_K = 2
        key = jax.random.key(seed)
        ks = jax.random.split(key, 8)
        s_h = 1.0 / np.sqrt(HIDDEN)
        s_e = 1.0 / np.sqrt(EXPERT)
        x = jax.random.normal(ks[0], (4, 512, HIDDEN), dtype=jnp.float32)
        gate_w = jax.random.uniform(ks[1], (HIDDEN, NUM_EXPERTS), jnp.float32, -s_h, s_h)
        gate_b = jax.random.uniform(ks[2], (NUM_EXPERTS,), jnp.float32, -s_h, s_h)
        w1 = jax.random.uniform(ks[3], (NUM_EXPERTS, HIDDEN, EXPERT), jnp.float32, -s_h, s_h)
        b1 = jax.random.uniform(ks[4], (NUM_EXPERTS, EXPERT), jnp.float32, -s_h, s_h)
        w2 = jax.random.uniform(ks[5], (NUM_EXPERTS, EXPERT, HIDDEN), jnp.float32, -s_e, s_e)
        b2 = jax.random.uniform(ks[6], (NUM_EXPERTS, HIDDEN), jnp.float32, -s_e, s_e)
        return {'x': x, 'gate_w': gate_w, 'gate_b': gate_b, 'w1': w1, 'b1': b1, 'w2': w2, 'b2': b2}
    _L1_ffn_in = _L1_ffn_setup()
    _d = {'L0_attn_x': _L0_attn_in['x'], 'L0_attn_Wq': _L0_attn_in['Wq'], 'L0_attn_bq': _L0_attn_in['bq'], 'L0_attn_Wk': _L0_attn_in['Wk'], 'L0_attn_bk': _L0_attn_in['bk'], 'L0_attn_Wv': _L0_attn_in['Wv'], 'L0_attn_bv': _L0_attn_in['bv'], 'L0_attn_Wo': _L0_attn_in['Wo'], 'L0_attn_bo': _L0_attn_in['bo'], 'L0_ffn_g1': _L0_ffn_in['g1'], 'L0_ffn_g2': _L0_ffn_in['g2'], 'L0_ffn_Wq': _L0_ffn_in['Wq'], 'L0_ffn_Wkc': _L0_ffn_in['Wkc'], 'L0_ffn_Wvc': _L0_ffn_in['Wvc'], 'L0_ffn_Wo': _L0_ffn_in['Wo'], 'L0_ffn_Wr': _L0_ffn_in['Wr'], 'L0_ffn_expert_bias': _L0_ffn_in['expert_bias'], 'L0_ffn_sW1': _L0_ffn_in['sW1'], 'L0_ffn_sW2': _L0_ffn_in['sW2'], 'L0_ffn_sW3': _L0_ffn_in['sW3'], 'L0_ffn_eW1': _L0_ffn_in['eW1'], 'L0_ffn_eW2': _L0_ffn_in['eW2'], 'L0_ffn_eW3': _L0_ffn_in['eW3'], 'L1_attn_wk': _L1_attn_in['wk'], 'L1_attn_wq': _L1_attn_in['wq'], 'L1_attn_wv': _L1_attn_in['wv'], 'L1_ffn_gate_w': _L1_ffn_in['gate_w'], 'L1_ffn_gate_b': _L1_ffn_in['gate_b'], 'L1_ffn_w1': _L1_ffn_in['w1'], 'L1_ffn_b1': _L1_ffn_in['b1'], 'L1_ffn_w2': _L1_ffn_in['w2'], 'L1_ffn_b2': _L1_ffn_in['b2']}
    _x0 = _d['L0_attn_x']
    _d['L0_attn_x'] = jax.random.normal(jax.random.fold_in(jax.random.key(seed), 1), (4, 1024, 256), dtype=_x0.dtype)
    del _x0
    return _d

def reference(L0_attn_x, L0_attn_Wq, L0_attn_bq, L0_attn_Wk, L0_attn_bk, L0_attn_Wv, L0_attn_bv, L0_attn_Wo, L0_attn_bo, L0_ffn_g1, L0_ffn_g2, L0_ffn_Wq, L0_ffn_Wkc, L0_ffn_Wvc, L0_ffn_Wo, L0_ffn_Wr, L0_ffn_expert_bias, L0_ffn_sW1, L0_ffn_sW2, L0_ffn_sW3, L0_ffn_eW1, L0_ffn_eW2, L0_ffn_eW3, L1_attn_wk, L1_attn_wq, L1_attn_wv, L1_ffn_gate_w, L1_ffn_gate_b, L1_ffn_w1, L1_ffn_b1, L1_ffn_w2, L1_ffn_b2):

    def _L0_attn_ref(x, Wq, bq, Wk, bk, Wv, bv, Wo, bo):
        import jax, jax.numpy as jnp
        import numpy as np
        B, S, D, H, FACTOR = (1, 512, 256, 16, 16)
        HD = D // H
        b, s, d = x.shape
        h, hd = (H, HD)
        q = (x @ Wq + bq).reshape(b, s, h, hd).transpose(0, 2, 1, 3)
        k = (x @ Wk + bk).reshape(b, s, h, hd).transpose(0, 2, 1, 3)
        v = (x @ Wv + bv).reshape(b, s, h, hd).transpose(0, 2, 1, 3)
        scores = jnp.einsum('bhqd,bhkd->bhqk', q, k) / np.sqrt(hd).astype(np.float32)
        vals, idx = jax.lax.top_k(scores, FACTOR)
        flat_scores = scores.reshape(-1, s)
        rows = jnp.arange(flat_scores.shape[0])[:, None]
        sparse = jnp.zeros_like(flat_scores).at[rows, idx.reshape(-1, FACTOR)].set(vals.reshape(-1, FACTOR)).reshape(scores.shape)
        attn = jax.nn.softmax(sparse, axis=-1)
        out = jnp.einsum('bhqk,bhkd->bhqd', attn, v)
        out = out.transpose(0, 2, 1, 3).reshape(b, s, d)
        return out @ Wo + bo

    def _L0_ffn_ref(X, g1, g2, Wq, Wkc, Wvc, Wo, Wr, expert_bias, sW1, sW2, sW3, eW1, eW2, eW3):
        import jax, jax.numpy as jnp
        import numpy as np
        D_MODEL = 256
        NUM_HEADS = 4
        NUM_EXPERTS = 8
        TOP_K = 2
        D_FF = 256
        EPS = 1e-06

        def _rmsnorm(x, g):
            return x * jax.lax.rsqrt(jnp.mean(x * x, axis=-1, keepdims=True) + EPS) * g

        def _swiglu(x, w1, w2, w3):
            return jax.nn.silu(x @ w1.T) * (x @ w3.T) @ w2.T
        B, S, d = X.shape
        H = NUM_HEADS
        dk = d // H
        scale = 1.0 / jnp.sqrt(jnp.float32(dk))
        nx = _rmsnorm(X, g1)
        Q = (nx @ Wq.T).reshape(B, S, H, dk).transpose(0, 2, 1, 3)
        Kc = nx @ Wkc.T
        Vc = nx @ Wvc.T
        scores = jnp.einsum('bhsd,btd->bhst', Q, Kc) * scale
        attn = jax.nn.softmax(scores, axis=-1)
        out = jnp.einsum('bhst,btd->bhsd', attn, Vc)
        out = out.transpose(0, 2, 1, 3).reshape(B, S, d) @ Wo.T
        X = X + out
        nx = _rmsnorm(X, g2)
        xf = nx.reshape(-1, d)
        logits = xf @ Wr.T + expert_bias
        rw = jax.nn.softmax(logits, axis=-1)
        topw, topi = jax.lax.top_k(rw, TOP_K)
        topw = jax.nn.softmax(topw, axis=-1)
        combine = jnp.sum(jax.nn.one_hot(topi, NUM_EXPERTS, dtype=xf.dtype) * topw[..., None], axis=1)
        shared = _swiglu(xf, sW1, sW2, sW3)
        h = jax.nn.silu(jnp.einsum('td,efd->etf', xf, eW1)) * jnp.einsum('td,efd->etf', xf, eW3)
        eo = jnp.einsum('etf,edf->etd', h, eW2)
        specialist = jnp.einsum('te,etd->td', combine, eo)
        moe_out = (shared + specialist).reshape(B, S, d)
        return X + moe_out

    def _L1_attn_ref(x, wk, wq, wv):
        import jax, jax.numpy as jnp
        import numpy as np
        DIM = 256
        B, N, d = x.shape
        scale = N ** (-0.5)
        wv_stoch = (jax.nn.softmax(wv, axis=0) * (1.0 / d)).T
        query = x @ wq
        key_t = jnp.swapaxes(x @ wk, -1, -2)
        value = x @ wv_stoch
        scores = jnp.einsum('bnd,bdm->bnm', query, key_t) * scale
        attn = jax.nn.softmax(scores, axis=1) - jnp.eye(N, dtype=x.dtype)
        return attn @ value

    def _L1_ffn_ref(x, gate_w, gate_b, w1, b1, w2, b2):
        import jax, jax.numpy as jnp
        import numpy as np
        HIDDEN = 256
        NUM_EXPERTS = 8
        EXPERT = 512
        TOP_K = 2
        probs = jax.nn.softmax(x @ gate_w + gate_b, axis=-1)
        top_s, top_i = jax.lax.top_k(probs, TOP_K)
        top_s = top_s / jnp.sum(top_s, axis=-1, keepdims=True)
        comb = jnp.sum(jax.nn.one_hot(top_i, NUM_EXPERTS, dtype=x.dtype) * top_s[..., None], axis=-2)
        out = jnp.zeros_like(x)
        for j in range(NUM_EXPERTS):
            h = jax.nn.relu(jnp.einsum('bsh,hf->bsf', x, w1[j]) + b1[j])
            y = jnp.einsum('bsf,fh->bsh', h, w2[j]) + b2[j]
            out = out + comb[..., j:j + 1] * y
        return out
    x = L0_attn_x
    xn = _layernorm(x, axis=-1)
    x = x + _L0_attn_ref(xn, L0_attn_Wq, L0_attn_bq, L0_attn_Wk, L0_attn_bk, L0_attn_Wv, L0_attn_bv, L0_attn_Wo, L0_attn_bo) + _L0_ffn_ref(xn, L0_ffn_g1, L0_ffn_g2, L0_ffn_Wq, L0_ffn_Wkc, L0_ffn_Wvc, L0_ffn_Wo, L0_ffn_Wr, L0_ffn_expert_bias, L0_ffn_sW1, L0_ffn_sW2, L0_ffn_sW3, L0_ffn_eW1, L0_ffn_eW2, L0_ffn_eW3)
    xn = _layernorm(x, axis=-1)
    x = x + _L1_attn_ref(xn, L1_attn_wk, L1_attn_wq, L1_attn_wv) + _L1_ffn_ref(xn, L1_ffn_gate_w, L1_ffn_gate_b, L1_ffn_w1, L1_ffn_b1, L1_ffn_w2, L1_ffn_b2)
    return x

_drawn_inputs = setup_inputs


def setup_inputs(seed=0):
    import zlib

    import numpy as np

    out = dict(_drawn_inputs(seed))
    spreads = {'L0_ffn_g1': (1.0, 0.6), 'L0_ffn_g2': (1.0, 0.6), 'L0_ffn_expert_bias': (0.0, 0.8)}
    factors = {'L0_attn_Wq': 8.0,
     'L0_attn_bq': 8.0,
     'L0_attn_Wk': 8.0,
     'L0_attn_bk': 200.0,
     'L0_attn_Wv': 8.0,
     'L0_attn_bv': 4.68,
     'L0_attn_Wo': 4.06,
     'L0_attn_bo': 23.912,
     'L0_ffn_Wq': 8.0,
     'L0_ffn_Wkc': 8.0,
     'L0_ffn_Wvc': 8.0,
     'L0_ffn_Wo': 8.0,
     'L0_ffn_Wr': 7.67,
     'L0_ffn_sW1': 5.12,
     'L0_ffn_sW2': 5.005,
     'L0_ffn_sW3': 5.164,
     'L0_ffn_eW1': 6.684,
     'L0_ffn_eW2': 6.54,
     'L0_ffn_eW3': 6.695,
     'L1_attn_wk': 200.0,
     'L1_attn_wq': 200.0,
     'L1_attn_wv': 200.0,
     'L1_ffn_gate_b': 26.672,
     'L1_ffn_b1': 64.0,
     'L1_ffn_b2': 48.512,
     'L1_ffn_gate_w': 5.404,
     'L1_ffn_w1': 7.277,
     'L1_ffn_w2': 5.487}
    for name, (base, spread) in spreads.items():
        noise = np.random.default_rng([zlib.crc32(name.encode()), seed]).standard_normal(out[name].shape)
        drawn = base * np.exp(spread * noise) if base else spread * noise
        out[name] = jnp.asarray(drawn.astype(out[name].dtype))
    for name, factor in factors.items():
        out[name] = (out[name] * factor).astype(out[name].dtype)
    return out
```

```python
from contextlib import ExitStack

import concourse.bass as bass
from concourse import mybir

F32 = mybir.dt.float32
U32 = mybir.dt.uint32
ALU = mybir.AluOpType
ACT = mybir.ActivationFunctionType
AX_X = mybir.AxisListType.X

P = 128
BATCH, SEQ, DIM = 4, 1024, 256
TOK = BATCH * SEQ
TILES = TOK // P
CH = DIM // P
BLK = 512
BT = BLK // P
BLOCKS = TOK // BLK
BANK = 512
HEADS0, HD0 = 16, 16
GROUP = 4
GROUPS = HEADS0 // GROUP
TOPK = 16
HEADS1, HD1 = 4, 64
EXPERTS = 8
FF0, FF1 = 256, 512
NEG = -3.0e38
QT = SEQ // P
ROUNDS = QT // 2


class Stage:

    def __init__(self, nc, name):
        self.nc, self.name, self.ctx = nc, name, ExitStack()

    def __enter__(self):
        self.ctx.__enter__()
        return self

    def __exit__(self, *e):
        return self.ctx.__exit__(*e)

    def sb(self, name, shape, dt=F32):
        return self.ctx.enter_context(self.nc.sbuf_tensor(f"{self.name}_{name}", shape, dt))

    def ps(self, name, shape):
        return self.ctx.enter_context(self.nc.psum_tensor(f"{self.name}_{name}", shape, F32))

    def sem(self, name):
        return self.ctx.enter_context(self.nc.semaphore(f"{self.name}_{name}"))

    def block(self):
        return self.ctx.enter_context(self.nc.Block())


def tiled(ap, i, n=BT):
    return ap.rearrange("(t p) d -> p t d", p=P)[:, bass.ds(i * n, n), :]


def chunked(ap, c=CH):
    return ap.rearrange("(c p) n -> p c n", p=P)


def ticks(e, outer, rounds, units, steps):
    drain = max(lag for lag, _ in steps)
    assert drain <= units
    with e.Fori(0, outer) as b:
        for k in range(units):
            for lag, step in steps:
                if k >= lag:
                    step(b, 0, k - lag, True)
        with e.Fori(1, rounds) as r:
            for k in range(units):
                for lag, step in steps:
                    if k >= lag:
                        step(b, r, k - lag, False)
                    else:
                        step(b, r - 1, k - lag + units, False)
        for k in range(drain):
            for lag, step in steps:
                if k < lag:
                    step(b, rounds - 1, units + k - lag, False)


class Tally:

    def __init__(self, eng, sem, round_, per):
        self.eng, self.sem, self.base, self.per, self.n = eng, sem, round_ * per, per, 0

    def step(self, k=1):
        self.n += k

    def wait(self):
        self.eng.wait_ge(self.sem, self.base + self.n)

    def close(self):
        assert self.n == self.per, (self.n, self.per)



def project0(nc, I, scr, ident):
    with Stage(nc, "pj") as s:
        wq = s.sb("wq", [P, CH, GROUPS * P])
        wk = s.sb("wk", [P, CH, GROUPS * P])
        wv = s.sb("wv", [P, CH, DIM])
        wq2 = s.sb("wq2", [P, CH, DIM])
        wkc = s.sb("wkc", [P, CH, P])
        wvc = s.sb("wvc", [P, CH, HD1])
        bq = s.sb("bq", [P, GROUPS])
        bqs = s.sb("bqs", [P, GROUPS])
        bk = s.sb("bk", [P, GROUPS])
        bv = s.sb("bv", [P, DIM])
        g1 = s.sb("g1", [P, CH])
        x = s.sb("x", [P, BT, DIM])
        xn = s.sb("xn", [P, BT, DIM])
        nx = s.sb("nx", [P, BT, DIM])
        sq = s.sb("sq", [P, DIM])
        st = s.sb("st", [P, BT, 6])
        mv = s.sb("mv", [P, BT, 2])
        vs = s.sb("vs", [P, BT])
        ms = s.sb("ms", [P, BT])
        sd = s.sb("sd", [P, BT])
        rs = s.sb("rs", [P, BT])
        xnT = s.sb("xnT", [P, CH, BLK])
        nxT = s.sb("nxT", [P, CH, BLK])
        qT = s.sb("qT", [P, GROUPS, BLK])
        kT = s.sb("kT", [P, GROUPS, BLK])
        v = s.sb("v", [P, BT, DIM])
        q2T = s.sb("q2T", [P, CH, BLK])
        kcT = s.sb("kcT", [P, BLK])
        vc = s.sb("vc", [P, BT, HD1])
        pT = s.ps("pT", [P, CH, BLK])
        pP = s.ps("pP", [P, 4, BLK])
        pV = s.ps("pV", [P, BT, DIM])

        loaded = s.sem("loaded")
        x_in = s.sem("x_in")
        xn_ok = s.sem("xn_ok")
        nx_ok = s.sem("nx_ok")
        dve = s.sem("dve")
        var_ok = s.sem("var_ok")
        root_ok = s.sem("root_ok")
        sq_ok = s.sem("sq_ok")
        turned = s.sem("turned")
        xnT_ok = s.sem("xnT_ok")
        nxT_ok = s.sem("nxT_ok")
        proj = s.sem("proj")
        proj_out = s.sem("proj_out")
        pv_ok = s.sem("pv_ok")
        pv_out = s.sem("pv_out")
        stored = s.sem("stored")
        passed = s.sem("passed")
        NW, NP = 11, 2 * GROUPS + CH + 1
        NST = 5 + 2 * GROUP
        b = s.block()

        @b.sync
        def _(e):
            for dst, src in ((wq[:], chunked(I["wq"])), (wk[:], chunked(I["wk"])), (wv[:], chunked(I["wv"])),
                             (wq2[:], chunked(I["wq2"])), (wkc[:], chunked(I["wkc"])), (wvc[:], chunked(I["wvc"])),
                             (bq[:], I["bq"]), (bk[:], I["bk"]), (bv[:], I["bv"].partition_broadcast(P)),
                             (g1[:], I["g1"]), (ident[:], I["ident"])):
                e.dma_start(dst, src).then_inc(loaded, 16)
            e.sem_inc(stored, 16)
            with e.Fori(0, BLOCKS) as i:
                now = bass.ds(i * BLK, BLK)
                e.wait_ge(xn_ok, i + 1)
                e.dma_start(x[:], tiled(I["x"], i)).then_inc(x_in, 16)
                e.wait_ge(xn_ok, i + 2)
                e.dma_start(tiled(scr["xn"], i), xn[:]).then_inc(stored, 16)
                for t, name, after in ((qT, "qT", GROUPS), (kT, "kT", 2 * GROUPS)):
                    e.wait_ge(proj_out, NP * i + after + 4)
                    for j in range(GROUP):
                        e.dma_start(scr[name].rearrange("(j g r) n -> j r g n", j=GROUP, g=GROUPS)[j, :, :, now],
                                    t[32 * j:32 * j + HD0]).then_inc(stored, 16)
                e.wait_ge(pv_out, 2 * i + 2)
                e.dma_start(tiled(scr["v"], i), v[:]).then_inc(stored, 16)
                e.wait_ge(proj_out, NP * i + NP + 4)
                e.dma_start(chunked(scr["q2T"])[:, :, now], q2T[:]).then_inc(stored, 16)
                e.dma_start(scr["kcT"][:, now], kcT[:]).then_inc(stored, 16)
                e.wait_ge(pv_out, 2 * i + 3)
                e.dma_start(tiled(scr["vc"], i), vc[:]).then_inc(stored, 16)
            e.wait_ge(stored, 16 * NST * BLOCKS + 16)

        @b.vector
        def _(e):
            e.wait_ge(loaded, 16 * NW)
            e.sem_inc(xn_ok, 1)
            e.sem_inc(pv_out, 1)
            with e.Fori(0, BLOCKS) as i:
                d = Tally(e, dve, i, 2 * BT + 2)
                e.wait_ge(x_in, 16 * i + 16)
                for a in range(BT):
                    e.bn_stats(st[:, a, :], x[:, a, :]).then_inc(dve, 1)
                    d.step()
                d.wait()
                e.sem_inc(passed, 1)
                for a in range(BT):
                    e.bn_aggr(mv[:, a, :], st[:, a, :]).then_inc(dve, 1)
                    d.step()
                d.wait()
                e.tensor_scalar(vs[:], mv[:, :, 1], 1e-5, None, ALU.add).then_inc(var_ok, 1)
                e.wait_ge(root_ok, 2 * i + 1)
                e.reciprocal(rs[:], sd[:]).then_inc(dve, 1)
                d.step()
                e.wait_ge(turned, 2 * i + 1)
                e.wait_ge(stored, 16 * NST * i + 16)
                d.wait()
                for a in range(BT):
                    r = e.tensor_scalar(xn[:, a, :], x[:, a, :], mv[:, a, 0:1], rs[:, a:a + 1],
                                        ALU.subtract, ALU.mult)
                r.then_inc(xn_ok, 1)
                e.wait_ge(sq_ok, BT * i + BT)
                e.tensor_scalar(vs[:], ms[:], 1.0 / DIM, 1e-6, ALU.mult, ALU.add).then_inc(var_ok, 1)
                e.wait_ge(root_ok, 2 * i + 2)
                e.reciprocal(rs[:], sd[:]).then_inc(dve, 1)
                d.step()
                e.wait_ge(turned, 2 * i + 2)
                d.wait()
                for a in range(BT):
                    r = e.tensor_scalar(nx[:, a, :], xn[:, a, :], rs[:, a:a + 1], None, ALU.mult)
                r.then_inc(nx_ok, 1)
                e.wait_ge(turned, 2 * i + 4)
                for c in range(CH):
                    r = e.tensor_scalar(nxT[:, c, :], pT[:, c, :], g1[:, c:c + 1], None, ALU.mult)
                r.then_inc(nxT_ok, 1)
                e.wait_ge(pv_ok, 2 * i + 1)
                for a in range(BT):
                    r = e.tensor_tensor(v[:, a, :], pV[:, a, :], bv[:], ALU.add)
                r.then_inc(pv_out, 1)
                e.wait_ge(pv_ok, 2 * i + 2)
                e.tensor_copy(vc[:], pV[:, :, 0:HD1]).then_inc(pv_out, 1)
                d.close()

        @b.scalar
        def _(e):
            e.wait_ge(loaded, 16 * NW)
            e.sem_inc(proj_out, 4)
            e.activation(bqs[:], bq[:], ACT.Copy, scale=HD0 ** -0.5)
            with e.Fori(0, BLOCKS) as i:
                e.wait_ge(var_ok, 2 * i + 1)
                e.activation(sd[:], vs[:], ACT.Sqrt).then_inc(root_ok, 1)
                e.wait_ge(xn_ok, i + 2)
                for a in range(BT):
                    e.activation(sq[:], xn[:, a, :], ACT.Square, accum_out=ms[:, a:a + 1]).then_inc(sq_ok, 1)
                    e.wait_ge(sq_ok, BT * i + a + 1)
                e.wait_ge(var_ok, 2 * i + 2)
                e.activation(sd[:], vs[:], ACT.Sqrt).then_inc(root_ok, 1)
                e.wait_ge(turned, 2 * i + 3)
                for c in range(CH):
                    r = e.activation(xnT[:, c, :], pT[:, c, :], ACT.Copy)
                r.then_inc(xnT_ok, 1)
                e.wait_ge(stored, 16 * NST * i + 16)
                k = 0
                for g in range(GROUPS):
                    k += 1
                    e.wait_ge(proj, NP * i + k)
                    e.activation(qT[:, g, :], pP[:, (k - 1) % 4, :], ACT.Identity, bias=bqs[:, g:g + 1],
                                 scale=HD0 ** -0.5).then_inc(proj_out, 1)
                for g in range(GROUPS):
                    k += 1
                    e.wait_ge(proj, NP * i + k)
                    e.activation(kT[:, g, :], pP[:, (k - 1) % 4, :], ACT.Identity,
                                 bias=bk[:, g:g + 1]).then_inc(proj_out, 1)
                for c in range(CH):
                    k += 1
                    e.wait_ge(proj, NP * i + k)
                    e.activation(q2T[:, c, :], pP[:, (k - 1) % 4, :], ACT.Copy,
                                 scale=HD1 ** -0.5).then_inc(proj_out, 1)
                e.wait_ge(proj, NP * i + NP)
                e.activation(kcT[:], pP[:, k % 4, :], ACT.Copy).then_inc(proj_out, 1)

        @b.tensor
        def _(e):
            e.wait_ge(loaded, 16 * NW)
            e.sem_inc(turned, 2)

            def turn(src):
                for c in range(CH):
                    for a in range(BT):
                        r = e.transpose(pT[:, c, a * P:(a + 1) * P], src[:, a, c * P:(c + 1) * P], ident[:])
                return r

            with e.Fori(0, BLOCKS) as i:
                e.wait_ge(xn_ok, i + 2)
                turn(xn).then_inc(turned, 1)
                e.wait_ge(xnT_ok, i + 1)
                e.wait_ge(nx_ok, i + 1)
                turn(nx).then_inc(turned, 1)
                k = 0
                for w in (wq, wk):
                    for g in range(GROUPS):
                        e.wait_ge(proj_out, NP * i + k + 1)
                        for c in range(CH):
                            r = e.matmul(pP[:, k % 4, :], w[:, c, g * P:(g + 1) * P], xnT[:, c, :],
                                         start=(c == 0), stop=(c == CH - 1))
                        r.then_inc(proj, 1)
                        k += 1
                e.wait_ge(pv_out, 2 * i + 1)
                for a in range(BT):
                    for c in range(CH):
                        r = e.matmul(pV[:, a, :], xnT[:, c, a * P:(a + 1) * P], wv[:, c, :],
                                     start=(c == 0), stop=(c == CH - 1))
                r.then_inc(pv_ok, 1)
                e.wait_ge(nxT_ok, i + 1)
                for m in range(CH + 1):
                    e.wait_ge(proj_out, NP * i + k + 1)
                    w = wq2[:, :, m * P:(m + 1) * P] if m < CH else wkc[:, :, :]
                    for c in range(CH):
                        r = e.matmul(pP[:, k % 4, :], w[:, c, :], nxT[:, c, :], start=(c == 0), stop=(c == CH - 1))
                    r.then_inc(proj, 1)
                    k += 1
                e.wait_ge(pv_out, 2 * i + 2)
                for a in range(BT):
                    for c in range(CH):
                        r = e.matmul(pV[:, a, 0:HD1], nxT[:, c, a * P:(a + 1) * P], wvc[:, c, :],
                                     start=(c == 0), stop=(c == CH - 1))
                r.then_inc(pv_ok, 1)


def attend(nc, scr, ident, name, heads, hd, top):
    with Stage(nc, name) as s:
        units = 2 * heads
        per = 2 if hd == HD1 else GROUP
        step = P // per
        groups = heads // per
        kgroups = 1 if hd == HD1 else groups
        vcols = hd if hd == HD1 else heads * hd
        R = 4
        qs = s.sb("qs", [P, groups, P])
        kT = s.sb("kT", [P, kgroups, SEQ])
        v = s.sb("v", [P, QT, vcols])
        sb = s.sb("sb", [P, R, SEQ]) if top else None
        cut = s.sb("cut", [P, SEQ]) if top else None
        w = s.sb("w", [P, R, SEQ])
        wT = s.sb("wT", [P, 2, SEQ])
        m8 = s.sb("m8", [P, R, TOPK])
        negm = s.sb("negm", [P, R])
        sums = s.sb("sums", [P, 2, heads])
        rsum = s.sb("rsum", [P, 2, heads])
        o = s.sb("o", [P, 2, heads, hd])
        pS = s.ps("pS", [P, 2, SEQ])
        pT = s.ps("pT", [P, 2, BANK])
        pO = s.ps("pO", [P, 2, BANK])

        k_in = s.sem("k_in")
        v_in = s.sem("v_in")
        q_in = [s.sem(f"q_in{g}") for g in range(groups)]
        scored = s.sem("scored")
        copied = s.sem("copied")
        thr_ok = s.sem("thr_ok")
        dmask = s.sem("dmask")
        pmask = s.sem("pmask")
        exped = s.sem("exped")
        turned = s.sem("turned")
        wT_ok = [s.sem(f"wT_ok{j}") for j in range(2)]
        av = s.sem("av")
        o_ok = s.sem("o_ok")
        stored = [s.sem(f"stored{j}") for j in range(2)]
        divided = s.sem("divided")
        dve = s.sem("dve")
        passed = s.sem("passed")
        CUT = 320
        b = s.block()

        def unit(bi, r, k):
            return (bi * ROUNDS + r) * units + k

        def tile(bi, r, k):
            return (bi * ROUNDS + r) * 2 + k // heads

        @b.sync
        def _(e):
            with e.Fori(0, BATCH) as bi:
                keys = bass.ds(bi * SEQ, SEQ)
                e.wait_ge(scored, bi * QT * heads + heads)
                if hd == HD1:
                    e.dma_start(kT[:, 0, :], scr["kcT"][:, keys]).then_inc(k_in, 16)
                else:
                    for j in range(per):
                        e.dma_start(kT[step * j:step * j + hd],
                                    scr["kT"].rearrange("(j g r) n -> j r g n", j=per, g=groups)[j, :, :, keys]
                                    ).then_inc(k_in, 16)

                def load_q(qt, g):
                    at = bass.ds(qt * P, P)
                    e.wait_ge(scored, qt * heads + per * (g + 1))
                    if hd == HD1:
                        e.dma_start(qs[:, g, :], chunked(scr["q2T"])[:, g, at]).then_inc(q_in[g], 16)
                    else:
                        for j in range(per):
                            e.dma_start(qs[step * j:step * j + hd, g, :],
                                        scr["qT"].rearrange("(j g r) n -> j g r n", j=per, g=groups)[j, g, :, at]
                                        ).then_inc(q_in[g], 16)

                for g in range(groups):
                    load_q(bi * QT, g)
                e.wait_ge(av, bi * QT * heads + 2)
                e.dma_start(v[:], tiled(scr["v" if top else "vc"], bi, QT)).then_inc(v_in, 16)
                with e.Fori(1, QT) as t:
                    for g in range(groups):
                        load_q(bi * QT + t, g)

        q_step = 16 * (1 if hd == HD1 else per)

        @b.tensor
        def _(e):
            e.sem_inc(scored, heads)
            e.sem_inc(turned, 2 * R)
            e.sem_inc(av, 2)

            def scores(bi, r, k, opening):
                n, h = unit(bi, r, k), k % heads
                g, at = h // per, step * (h % per)
                if opening and k == 0:
                    e.wait_ge(k_in, q_step * (bi + 1))
                if h % per == 0:
                    e.wait_ge(q_in[g], q_step * (tile(bi, r, k) + 1))
                e.wait_ge(copied if top else exped, n + 1)
                for c in range(SEQ // BANK):
                    m = e.matmul(pS[:, k % 2, c * BANK:(c + 1) * BANK], qs[at:at + hd, g, :],
                                 kT[at:at + hd, g if kgroups > 1 else 0, c * BANK:(c + 1) * BANK],
                                 start=True, stop=True)
                m.then_inc(scored, 1)

            def turn(bi, r, k, opening):
                n = unit(bi, r, k)
                e.wait_ge(exped, n + 1 + 2)
                for j in range(2):
                    e.wait_ge(wT_ok[j], n + 1)
                    for c in range(4 * j, 4 * j + 4):
                        m = e.transpose(pT[:, j, (c % 4) * P:(c % 4 + 1) * P], w[:, k % R, c * P:(c + 1) * P],
                                        ident[:])
                    m.then_inc(turned, 1)

            def outputs(bi, r, k, opening):
                n, h = unit(bi, r, k), k % heads
                if opening and k == 0:
                    e.wait_ge(v_in, 16 * (bi + 1))
                if h == 0:
                    e.wait_ge(o_ok, tile(bi, r, k) + 1)
                e.wait_ge(wT_ok[1], n + 1 + 1)
                vat = h * hd if top else 0
                for c in range(QT):
                    m = e.matmul(pO[:, k // heads, h * hd:(h + 1) * hd], wT[:, k % 2, c * P:(c + 1) * P],
                                 v[:, c, vat:vat + hd], start=(c == 0), stop=(c == QT - 1))
                m.then_inc(av, 1)

            ticks(e, BATCH, ROUNDS, units, [(0, scores), (3, turn), (4, outputs)] if top else
                  [(0, scores), (2, turn), (3, outputs)])

        @b.scalar
        def _(e):
            if top:
                e.sem_inc(copied, 2)
            e.sem_inc(exped, 2)
            for j in range(2):
                e.sem_inc(wT_ok[j], 1)
                e.sem_inc(stored[j], 16)

            def copy(bi, r, k, opening):
                n = unit(bi, r, k)
                e.wait_ge(scored, n + 1 + heads)
                e.wait_ge(dmask, n + 1)
                e.wait_ge(pmask, 2 * n + 2)
                e.activation(sb[:, k % R, :], pS[:, k % 2, :], ACT.Copy).then_inc(copied, 1)

            def exp(bi, r, k, opening):
                n, h = unit(bi, r, k), k % heads
                if top:
                    e.wait_ge(dmask, n + 1 + R)
                    e.wait_ge(pmask, 2 * n + 2 + 2 * R)
                else:
                    e.wait_ge(thr_ok, n + 1)
                    e.wait_ge(turned, 2 * n + 2)
                if h == 0:
                    e.wait_ge(o_ok, tile(bi, r, k) + 1)
                e.activation(w[:, k % R, :], w[:, k % R, :] if top else pS[:, k % 2, :], ACT.Exp,
                             bias=negm[:, k % R:k % R + 1],
                             accum_out=sums[:, k // heads, h:h + 1]).then_inc(exped, 1)

            def copy_turned(bi, r, k, opening):
                n = unit(bi, r, k)
                e.wait_ge(av, n + 1)
                for j in range(2):
                    e.wait_ge(turned, 2 * n + j + 1 + 2 * R)
                    e.activation(wT[:, k % 2, j * BANK:(j + 1) * BANK], pT[:, j, :],
                                 ACT.Copy).then_inc(wT_ok[j], 1)

            def store(bi, r, k, opening):
                if k % heads == heads - 1:
                    t = tile(bi, r, k)
                    e.wait_ge(o_ok, t + 1 + 2)
                    e.dma_start(scr["o0" if top else "o1"].rearrange("(t p) d -> p t d", p=P)[:, bass.ds(t, 1), :],
                                o[:, k // heads].rearrange("p h d -> p (h d)").unsqueeze(1)
                                ).then_inc(stored[k // heads], 16)

            ticks(e, BATCH, ROUNDS, units, [(0, copy), (2, exp), (3, copy_turned), (8, store)] if top else
                  [(1, exp), (2, copy_turned), (7, store)])
            for j in range(2):
                e.wait_ge(stored[j], 16 * (BATCH * ROUNDS + 1))

        @b.vector
        def _(e):
            if top:
                e.sem_inc(dmask, R)
            e.sem_inc(o_ok, 2)

            def largest(bi, r, k, opening):
                n, q = unit(bi, r, k), k % R
                e.wait_ge(copied, n + 1 + 2)
                e.sem_inc(passed, 1)
                e.max(m8[:, q, 0:8], sb[:, q, :]).then_inc(dve, 1)
                e.wait_ge(dve, 2 * n + 1)
                e.sem_inc(passed, 1)
                e.match_replace(cut[:], m8[:, q, 0:8], sb[:, q, :], NEG).then_inc(dve, 1)
                e.wait_ge(dve, 2 * n + 2)
                e.sem_inc(passed, 1)
                e.max(m8[:, q, 8:16], cut[:]).then_inc(thr_ok, 1)
                e.wait_ge(turned, 2 * n + 2)
                e.wait_ge(thr_ok, n + 1)
                e.tensor_scalar(negm[:, q:q + 1], m8[:, q, 0:1], 0.0, -1.0, ALU.max, ALU.mult)
                e.scalar_tensor_tensor(w[:, q, 0:CUT], sb[:, q, 0:CUT], m8[:, q, TOPK - 1:TOPK],
                                       sb[:, q, 0:CUT], ALU.is_ge, ALU.mult).then_inc(dmask, 1)

            def maximum(bi, r, k, opening):
                n, q = unit(bi, r, k), k % R
                e.wait_ge(scored, n + 1 + heads)
                e.reduce_max(m8[:, q, 0:1], pS[:, k % 2, :], AX_X).then_inc(dve, 1)
                e.wait_ge(exped, n + 1)
                e.wait_ge(dve, n + 1)
                e.tensor_scalar(negm[:, q:q + 1], m8[:, q, 0:1], -1.0, None, ALU.mult).then_inc(thr_ok, 1)

            def divide(bi, r, k, opening):
                if k % heads == heads - 1:
                    t, half = tile(bi, r, k), k // heads
                    e.wait_ge(av, unit(bi, r, k) + 1 + 2)
                    e.reciprocal(rsum[:, half, :], sums[:, half, :]).then_inc(divided, 1)
                    e.wait_ge(stored[half], 16 * (bi * ROUNDS + r + 1))
                    e.wait_ge(divided, t + 1)
                    e.tensor_tensor(o[:, half], pO[:, half, 0:heads * hd].rearrange("p (h d) -> p h d", h=heads),
                                    rsum[:, half, :].unsqueeze(2).to_broadcast([P, heads, hd]), ALU.mult).then_inc(o_ok, 1)

            ticks(e, BATCH, ROUNDS, units, [(0, largest), (6, divide)] if top else [(0, maximum), (5, divide)])

        if top:
            @b.gpsimd
            def _(e):
                e.sem_inc(pmask, 2 * R)

                def mask(bi, r, k, opening):
                    n, q = unit(bi, r, k), k % R
                    e.wait_ge(turned, 2 * n + 2)
                    e.wait_ge(thr_ok, n + 1)
                    e.sem_inc(passed, 1)
                    e.tensor_scalar(w[:, q, CUT:], sb[:, q, CUT:], m8[:, q, TOPK - 1:TOPK], None,
                                    ALU.is_ge).then_inc(pmask, 1)
                    e.wait_ge(pmask, 2 * n + 1 + 2 * R)
                    e.tensor_tensor(w[:, q, CUT:], w[:, q, CUT:], sb[:, q, CUT:], ALU.mult).then_inc(pmask, 1)

                ticks(e, BATCH, ROUNDS, units, [(0, mask)])


class Gate:

    def __init__(self, s, bias_in):
        t = [P, BT, EXPERTS]
        self.bias = s.sb("g_bias", [P, EXPERTS])
        self.bias_in = bias_in
        self.iota = s.sb("g_iota", [P, EXPERTS])
        self.lg, self.pr, self.oh = s.sb("g_lg", t), s.sb("g_pr", t), s.sb("g_oh", t)
        self.m8, self.ixf = s.sb("g_m8", t), s.sb("g_ixf", t)
        self.ix = s.sb("g_ix", t, U32)
        self.r = s.sb("g_r", [P, BT])
        self.c = s.sb("g_c", [P, 2, BT])
        self.exp_in = s.sem("g_exp_in")
        self.exp_out = s.sem("g_exp_out")

    def vector(self, e, i, d, passed, logits, comb, soft):
        t = [P, BT, EXPERTS]
        many = lambda a: a.unsqueeze(2).to_broadcast(t)
        n_exp = 2 if soft else 1
        def tt(out, a, b, op):
            e.tensor_tensor(out, a, b, op).then_inc(d.sem, 1)
            d.step()
            d.wait()
        tt(self.lg[:], logits, self.bias[:].unsqueeze(1).to_broadcast(t), ALU.add)
        e.reduce_max(self.r[:], self.lg[:], AX_X).then_inc(d.sem, 1)
        d.step()
        d.wait()
        e.tensor_tensor(self.lg[:], self.lg[:], many(self.r[:]), ALU.subtract).then_inc(self.exp_in, 1)
        e.wait_ge(self.exp_out, n_exp * i + 1)
        e.reduce_sum(self.r[:], self.pr[:], AX_X).then_inc(d.sem, 1)
        d.step()
        d.wait()
        e.reciprocal(self.r[:], self.r[:]).then_inc(d.sem, 1)
        d.step()
        d.wait()
        tt(self.pr[:], self.pr[:], many(self.r[:]), ALU.mult)
        e.sem_inc(passed, 1)
        for a in range(BT):
            e.max(self.m8[:, a, :], self.pr[:, a, :]).then_inc(d.sem, 1)
            d.step()
        d.wait()
        e.sem_inc(passed, 1)
        for a in range(BT):
            e.max_index(self.ix[:, a, :], self.m8[:, a, :], self.pr[:, a, :]).then_inc(d.sem, 1)
            d.step()
        d.wait()
        e.tensor_copy(self.ixf[:], self.ix[:]).then_inc(d.sem, 1)
        d.step()
        if soft:
            e.tensor_tensor(self.c[:, 1, :], self.m8[:, :, 1], self.m8[:, :, 0], ALU.subtract
                            ).then_inc(self.exp_in, 1)
            e.wait_ge(self.exp_out, n_exp * i + 2)
            e.tensor_scalar(self.r[:], self.c[:, 1, :], 1.0, None, ALU.add).then_inc(d.sem, 1)
            d.step()
        else:
            e.tensor_tensor(self.r[:], self.m8[:, :, 1], self.m8[:, :, 0], ALU.add).then_inc(d.sem, 1)
            d.step()
        d.wait()
        e.reciprocal(self.r[:], self.r[:]).then_inc(d.sem, 1)
        d.step()
        d.wait()
        if soft:
            e.tensor_copy(self.c[:, 0, :], self.r[:]).then_inc(d.sem, 1)
            d.step()
            tt(self.c[:, 1, :], self.c[:, 1, :], self.r[:], ALU.mult)
        else:
            for m in range(2):
                tt(self.c[:, m, :], self.m8[:, :, m], self.r[:], ALU.mult)
        iota = self.iota[:].unsqueeze(1).to_broadcast(t)
        tt(self.oh[:], iota, many(self.ixf[:, :, 0]), ALU.is_equal)
        tt(self.oh[:], self.oh[:], many(self.c[:, 0, :]), ALU.mult)
        tt(self.lg[:], iota, many(self.ixf[:, :, 1]), ALU.is_equal)
        tt(self.lg[:], self.lg[:], many(self.c[:, 1, :]), ALU.mult)
        tt(comb, self.lg[:], self.oh[:], ALU.add)

    STEPS = 1 + 1 + 1 + 1 + 1 + BT + BT + 1 + 1 + 1 + 2 + 5

    def scalar(self, e, i, soft):
        n = 2 if soft else 1
        e.wait_ge(self.exp_in, n * i + 1)
        e.activation(self.pr[:], self.lg[:], ACT.Exp).then_inc(self.exp_out, 1)
        if soft:
            e.wait_ge(self.exp_in, n * i + 2)
            e.activation(self.c[:, 1, :], self.c[:, 1, :], ACT.Exp).then_inc(self.exp_out, 1)


def route0(nc, I, scr, ident, acc, xT, comb):
    with Stage(nc, "rt") as s:
        wo = [s.sb(f"wo{j}", [P, CH, DIM]) for j in range(2)]
        wr = s.sb("wr", [P, CH, EXPERTS])
        bo = s.sb("bo", [P, DIM])
        g2 = s.sb("g2", [P, CH])
        o = [s.sb(f"o{j}", [P, BT, DIM]) for j in range(2)]
        x = s.sb("x", [P, BT, DIM])
        xn = s.sb("xn", [P, BT, DIM])
        nx = s.sb("nx", [P, BT, DIM])
        sq = s.sb("sq", [P, DIM])
        ms, vs, sd, rs = (s.sb(n, [P, BT]) for n in ("ms", "vs", "sd", "rs"))
        oT = [s.sb(f"oT{j}", [P, CH, BLK]) for j in range(2)]
        nxT = s.sb("nxT", [P, CH, BLK])
        pT = s.ps("pT", [P, CH, BLK])
        pP = s.ps("pP", [P, 2, BT, DIM])
        pL = s.ps("pL", [P, BT, EXPERTS])
        loaded = s.sem("loaded")
        o_in = s.sem("o_in")
        x_in = s.sem("x_in")
        turned = s.sem("turned")
        oT_ok = s.sem("oT_ok")
        proj = s.sem("proj")
        x2_ok = s.sem("x2_ok")
        sq_ok = s.sem("sq_ok")
        var_ok = s.sem("var_ok")
        root_ok = s.sem("root_ok")
        nx_ok = s.sem("nx_ok")
        nxT_ok = s.sem("nxT_ok")
        logit = s.sem("logit")
        xT_ok = s.sem("xT_ok")
        done = s.sem("done")
        dve = s.sem("dve")
        passed = s.sem("passed")
        gate = Gate(s, I["ebias"])
        b = s.block()
        NW = 7

        @b.sync
        def _(e):
            for dst, src in ((wo[0][:], chunked(I["wo"])), (wo[1][:], chunked(I["wo2"])), (wr[:], chunked(I["wr"])),
                             (bo[:], I["bo"].partition_broadcast(P)), (g2[:], I["g2"]),
                             (gate.bias[:], I["ebias"].partition_broadcast(P)),
                             (gate.iota[:], I["iota"].partition_broadcast(P))):
                e.dma_start(dst, src).then_inc(loaded, 16)
            with e.Fori(0, BLOCKS) as i:
                e.wait_ge(turned, 3 * i + 3)
                for j in range(2):
                    e.dma_start(o[j][:], tiled(scr[f"o{j}"], i)).then_inc(o_in, 16)
                e.wait_ge(done, i + 1)
                e.dma_start(x[:], tiled(I["x"], i)).then_inc(x_in, 16)
                e.dma_start(xn[:], tiled(scr["xn"], i)).then_inc(x_in, 16)

        @b.tensor
        def _(e):
            e.wait_ge(loaded, 16 * NW)
            e.sem_inc(turned, 3)

            def turn(src):
                for c in range(CH):
                    for a in range(BT):
                        r = e.transpose(pT[:, c, a * P:(a + 1) * P], src[:, a, c * P:(c + 1) * P], ident[:])
                return r

            with e.Fori(0, BLOCKS) as i:
                e.wait_ge(o_in, 32 * i + 32)
                e.wait_ge(nxT_ok, i + 1)
                turn(o[0]).then_inc(turned, 1)
                e.wait_ge(oT_ok, 2 * i + 1)
                turn(o[1]).then_inc(turned, 1)
                e.wait_ge(done, i + 1)
                for j in range(2):
                    e.wait_ge(oT_ok, 2 * i + j + 1)
                    for a in range(BT):
                        for c in range(CH):
                            r = e.matmul(pP[:, j, a, :], oT[j][:, c, a * P:(a + 1) * P], wo[j][:, c, :],
                                         start=(c == 0), stop=(c == CH - 1))
                    r.then_inc(proj, 1)
                e.wait_ge(nx_ok, i + 1)
                turn(nx).then_inc(turned, 1)
                e.wait_ge(nxT_ok, i + 2)
                for a in range(BT):
                    for c in range(CH):
                        r = e.matmul(pL[:, a, :], nxT[:, c, a * P:(a + 1) * P], wr[:, c, :],
                                     start=(c == 0), stop=(c == CH - 1))
                r.then_inc(logit, 1)

        @b.scalar
        def _(e):
            with e.Fori(0, BLOCKS) as i:
                for j in range(2):
                    e.wait_ge(turned, 3 * i + j + 1 + 3)
                    for c in range(CH):
                        r = e.activation(oT[j][:, c, :], pT[:, c, :], ACT.Copy)
                    r.then_inc(oT_ok, 1)
                e.wait_ge(x2_ok, i + 1)
                for a in range(BT):
                    e.activation(sq[:], xn[:, a, :], ACT.Square, accum_out=ms[:, a:a + 1]).then_inc(sq_ok, 1)
                    e.wait_ge(sq_ok, BT * i + a + 1)
                e.wait_ge(var_ok, i + 1)
                e.activation(sd[:], vs[:], ACT.Sqrt).then_inc(root_ok, 1)
                gate.scalar(e, i, True)

        @b.vector
        def _(e):
            e.wait_ge(loaded, 16 * NW)
            e.sem_inc(done, 1)
            e.sem_inc(nxT_ok, 1)
            with e.Fori(0, BLOCKS) as i:
                d = Tally(e, dve, i, 3 + Gate.STEPS)
                e.wait_ge(x_in, 32 * i + 32)
                for a in range(BT):
                    r = e.tensor_tensor(x[:, a, :], x[:, a, :], bo[:], ALU.add)
                r.then_inc(dve, 1)
                d.step()
                e.wait_ge(proj, 2 * i + 1)
                d.wait()
                e.tensor_tensor(x[:], x[:], pP[:, 0], ALU.add).then_inc(dve, 1)
                d.step()
                e.wait_ge(proj, 2 * i + 2)
                e.tensor_tensor(xn[:], xn[:], pP[:, 1], ALU.add).then_inc(x2_ok, 1)
                e.wait_ge(x2_ok, i + 1)
                d.wait()
                e.tensor_tensor(acc[:, bass.ds(i * BT, BT), :], x[:], xn[:], ALU.add)
                e.wait_ge(sq_ok, BT * i + BT)
                e.tensor_scalar(vs[:], ms[:], 1.0 / DIM, 1e-6, ALU.mult, ALU.add).then_inc(var_ok, 1)
                e.wait_ge(root_ok, i + 1)
                e.reciprocal(rs[:], sd[:]).then_inc(dve, 1)
                d.step()
                d.wait()
                for a in range(BT):
                    r = e.tensor_scalar(nx[:, a, :], xn[:, a, :], rs[:, a:a + 1], None, ALU.mult)
                r.then_inc(nx_ok, 1)
                e.wait_ge(nx_ok, i + 1)
                e.sem_inc(done, 1)
                e.wait_ge(xT_ok, i + 1)
                e.wait_ge(turned, 3 * i + 6)
                for c in range(CH):
                    r = e.tensor_scalar(nxT[:, c, :], pT[:, c, :], g2[:, c:c + 1], None, ALU.mult)
                r.then_inc(nxT_ok, 1)
                e.wait_ge(logit, i + 1)
                gate.vector(e, i, d, passed, pL[:], comb[:, bass.ds(i * BT, BT), 1:1 + EXPERTS], True)
                d.close()

        @b.gpsimd
        def _(e):
            e.memset(comb[:, :, 0:1], 1.0)
            e.sem_inc(xT_ok, 1)
            with e.Fori(0, BLOCKS) as i:
                e.wait_ge(nxT_ok, i + 2)
                e.sem_inc(passed, 1)
                e.tensor_copy(xT[:, :, bass.ds(i * BLK, BLK)], nxT[:]).then_inc(xT_ok, 1)


def experts(nc, I, name, acc, xT, comb, count, ff, swiglu, first, out=None):
    with Stage(nc, name) as s:
        FC = ff // P
        SIDES = 2 if swiglu else 1
        RH = 2 if swiglu else 4
        w1 = s.sb("w1", [P, SIDES, CH, ff])
        w2 = s.sb("w2", [P, FC, DIM])
        b1 = None if swiglu else s.sb("b1", [P, FC])
        sg = s.sb("sg", [P, 2, BLK]) if swiglu else None
        h = s.sb("h", [P, 2, FC, BLK])
        pH = s.ps("pH", [P, RH, SIDES, BLK])
        pY = s.ps("pY", [P, 2, BT, DIM])
        w1_in, w2_in = s.sem("w1_in"), s.sem("w2_in")
        b1_in = s.sem("b1_in")
        hid = s.sem("hid")
        sg_ok = s.sem("sg_ok")
        h_ok = s.sem("h_ok")
        y_ok = s.sem("y_ok")
        added = s.sem("added")
        stored = s.sem("stored")
        b = s.block()
        ROUNDS_T = BLOCKS // 2

        def unit(x, r, k):
            return (x * ROUNDS_T + r) * 2 + k

        @b.sync
        def _(e):
            with e.Fori(0, count) as x:
                if b1 is not None:
                    e.wait_ge(h_ok, x * (BLOCKS * FC) + RH)
                    e.dma_start(b1[:], I["b1"][:, bass.ds(x, 1), :].rearrange("p x f -> p (x f)")).then_inc(b1_in, 16)
                e.wait_ge(hid, x * (BLOCKS * FC) + 1)
                for side, wname in enumerate(("w1", "w3")[:SIDES]):
                    e.dma_start(w1[:, side], I[f"{name}_{wname}"].rearrange("(x c p) f -> p x c f", c=CH, p=P)
                                [:, bass.ds(x, 1), :, :].rearrange("p x c f -> p (x c) f")).then_inc(w1_in, 16)
                e.wait_ge(y_ok, x * BLOCKS + 2)
                e.dma_start(w2[:], I[f"{name}_w2"].rearrange("(x c p) d -> p x c d", c=FC, p=P)
                            [:, bass.ds(x, 1), :, :].rearrange("p x c d -> p (x c) d")).then_inc(w2_in, 16)
            if out is not None:
                e.wait_ge(added, count * BLOCKS + 2)
                e.dma_start(out.rearrange("(t p) d -> p t d", p=P), acc[:]).then_inc(stored, 16)
                e.wait_ge(stored, 16)

        @b.tensor
        def _(e):
            e.sem_inc(hid, 1)
            e.sem_inc(y_ok, 2)

            def hidden(x, r, k, opening):
                n = unit(x, r, k)
                if opening and k == 0:
                    e.wait_ge(w1_in, 16 * SIDES * (x + 1))
                for f in range(FC):
                    e.wait_ge(h_ok, n * FC + f + 1)
                    for side in range(SIDES):
                        for c in range(CH):
                            m = e.matmul(pH[:, (k * FC + f) % RH, side, :], w1[:, side, c, f * P:(f + 1) * P],
                                         xT[:, c, bass.ds((r * 2 + k) * BLK, BLK)], start=(c == 0), stop=(c == CH - 1))
                    m.then_inc(hid, 1)

            def output(x, r, k, opening):
                n = unit(x, r, k)
                if opening and k == 0:
                    e.wait_ge(w2_in, 16 * (x + 1))
                e.wait_ge(added, n + 1)
                e.wait_ge(h_ok, n * FC + FC + RH)
                for a in range(BT):
                    for f in range(FC):
                        m = e.matmul(pY[:, k, a, :], h[:, k, f, a * P:(a + 1) * P], w2[:, f, :],
                                     start=(f == 0), stop=(f == FC - 1))
                m.then_inc(y_ok, 1)

            ticks(e, count, ROUNDS_T, 2, [(0, hidden), (1, output)])

        @b.scalar
        def _(e):
            if not swiglu:
                e.sem_inc(h_ok, RH)

            def act(x, r, k, opening):
                n = unit(x, r, k)
                if not swiglu:
                    e.wait_ge(y_ok, n + 1)
                    if opening and k == 0:
                        e.wait_ge(b1_in, 16 * (x + 1))
                for f in range(FC):
                    e.wait_ge(hid, n * FC + f + 1 + 1)
                    if swiglu:
                        e.wait_ge(h_ok, n * FC + f + 1)
                        e.activation(sg[:, f % 2, :], pH[:, (k * FC + f) % RH, 0, :], ACT.Silu).then_inc(sg_ok, 1)
                    else:
                        e.activation(h[:, k, f, :], pH[:, (k * FC + f) % RH, 0, :], ACT.Relu,
                                     bias=b1[:, f:f + 1]).then_inc(h_ok, 1)

            ticks(e, count, ROUNDS_T, 2, [(0, act)])

        @b.vector
        def _(e):
            if swiglu:
                e.sem_inc(h_ok, RH)
            e.sem_inc(added, 2)

            def multiply(x, r, k, opening):
                n = unit(x, r, k)
                e.wait_ge(y_ok, n + 1)
                for f in range(FC):
                    e.wait_ge(sg_ok, n * FC + f + 1)
                    e.tensor_tensor(h[:, k, f, :], sg[:, f % 2, :], pH[:, (k * FC + f) % RH, 1, :],
                                    ALU.mult).then_inc(h_ok, 1)

            def add(x, r, k, opening):
                n = unit(x, r, k)
                e.wait_ge(y_ok, n + 1 + 2)
                if opening and k == 0:
                    e.wait_ge(added, x * BLOCKS + 2)
                for a in range(BT):
                    t = (r * 2 + k) * BT + a
                    now = acc[:, bass.ds(t, 1), :].rearrange("p t d -> p (t d)")
                    m = e.scalar_tensor_tensor(now, pY[:, k, a, :], comb[:, bass.ds(t, 1), bass.ds(x + first, 1)]
                                               .rearrange("p t x -> p (t x)"), now, ALU.mult, ALU.add)
                m.then_inc(added, 1)

            ticks(e, count, ROUNDS_T, 2, [(0, multiply), (1, add)] if swiglu else [(0, add)])


def project1(nc, I, scr, ident, acc, xT, comb):
    with Stage(nc, "p1") as s:
        wq = s.sb("wq", [P, CH, DIM])
        wk = s.sb("wk", [P, CH, DIM])
        wv = s.sb("wv", [P, CH, DIM])
        wg = s.sb("wg", [P, CH, EXPERTS])
        b2 = s.sb("b2", [EXPERTS, DIM])
        wm, wsum = s.sb("wm", [P, CH]), s.sb("wsum", [P, CH])
        xn = s.sb("xn", [P, BT, DIM])
        st, mv = s.sb("st", [P, BT, 6]), s.sb("mv", [P, BT, 2])
        vs, sd, rs = (s.sb(n, [P, BT]) for n in ("vs", "sd", "rs"))
        xnT = s.sb("xnT", [P, CH, BLK])
        qk = s.sb("qk", [P, 2 * CH, BLK])
        v = s.sb("v", [P, BT, DIM])
        cb = s.sb("cb", [P, BT, EXPERTS])
        cT = s.sb("cT", [EXPERTS, BLK])
        pT = s.ps("pT", [P, CH, BLK])
        pP = s.ps("pP", [P, 2 * CH, BLK])
        pV = s.ps("pV", [P, BT, DIM])
        loaded = s.sem("loaded")
        w_ok = s.sem("w_ok")
        var_ok, root_ok = s.sem("var_ok"), s.sem("root_ok")
        xn_ok = s.sem("xn_ok")
        turned = s.sem("turned")
        xnT_ok = s.sem("xnT_ok")
        xT_ok = s.sem("xT_ok")
        logit = s.sem("logit")
        proj = s.sem("proj")
        qk_ok = s.sem("qk_ok")
        v_ps = s.sem("v_ps")
        v_ok = s.sem("v_ok")
        cb_ok = s.sem("cb_ok")
        cb_T = s.sem("cb_T")
        cT_ok = s.sem("cT_ok")
        stored = s.sem("stored")
        dve = s.sem("dve")
        passed = s.sem("passed")
        gate = Gate(s, I["gate_b"])
        NW, NST = 7, 3
        b = s.block()

        @b.sync
        def _(e):
            for dst, src in ((wq[:], chunked(I["l1wq"])), (wk[:], chunked(I["l1wk"])), (wv[:], chunked(I["l1wvT"])),
                             (wg[:], chunked(I["gate_w"])), (b2[:], I["b2"]),
                             (gate.bias[:], I["gate_b"].partition_broadcast(P)),
                             (gate.iota[:], I["iota"].partition_broadcast(P))):
                e.dma_start(dst, src).then_inc(loaded, 16)
            e.sem_inc(stored, 16)
            with e.Fori(0, BLOCKS) as i:
                now = bass.ds(i * BLK, BLK)
                e.wait_ge(v_ok, 2 * i + 3)
                e.dma_start(tiled(scr["v1"], i), v[:]).then_inc(stored, 16)
                e.wait_ge(qk_ok, 4 * i + 8)
                e.dma_start(chunked(scr["q1T"])[:, :, now], qk[:, 0:CH, :]).then_inc(stored, 16)
                e.dma_start(chunked(scr["k1T"])[:, :, now], qk[:, CH:, :]).then_inc(stored, 16)
            e.wait_ge(stored, 16 * NST * BLOCKS + 16)

        @b.tensor
        def _(e):
            e.wait_ge(loaded, 16 * NW)
            e.wait_ge(w_ok, 2 * CH + 4)
            e.sem_inc(turned, 1)
            with e.Fori(0, BLOCKS) as i:
                e.wait_ge(xn_ok, i + 1)
                e.wait_ge(cT_ok, i + 1)
                for c in range(CH):
                    for a in range(BT):
                        r = e.transpose(pT[:, c, a * P:(a + 1) * P], xn[:, a, c * P:(c + 1) * P], ident[:])
                r.then_inc(turned, 1)
                e.wait_ge(xnT_ok, i + 1)
                for a in range(BT):
                    for c in range(CH):
                        r = e.matmul(pT[:, 0, a * EXPERTS:(a + 1) * EXPERTS], xnT[:, c, a * P:(a + 1) * P],
                                     wg[:, c, :], start=(c == 0), stop=(c == CH - 1))
                r.then_inc(logit, 1)
                e.wait_ge(v_ok, 2 * i + 2)
                for a in range(BT):
                    for c in range(CH):
                        r = e.matmul(pV[:, a, :], xnT[:, c, a * P:(a + 1) * P], wv[:, c, :],
                                     start=(c == 0), stop=(c == CH - 1))
                r.then_inc(v_ps, 1)
                k = 0
                for w in (wq, wk):
                    for m in range(CH):
                        e.wait_ge(qk_ok, 4 * i + k + 1)
                        for c in range(CH):
                            r = e.matmul(pP[:, k, :], w[:, c, m * P:(m + 1) * P], xnT[:, c, :],
                                         start=(c == 0), stop=(c == CH - 1))
                        r.then_inc(proj, 1)
                        k += 1
                e.wait_ge(cb_ok, i + 1)
                for a in range(BT):
                    r = e.transpose(pT[0:EXPERTS, 1, a * P:(a + 1) * P], cb[:, a, :], ident[:])
                r.then_inc(cb_T, 1)
                e.wait_ge(v_ok, 2 * i + 3)
                e.wait_ge(cT_ok, i + 2)
                for a in range(BT):
                    r = e.matmul(pV[:, a, :], cT[:, a * P:(a + 1) * P], b2[:], start=True, stop=True)
                r.then_inc(v_ps, 1)

        @b.scalar
        def _(e):
            e.sem_inc(qk_ok, 4)
            e.sem_inc(cT_ok, 1)
            e.wait_ge(w_ok, CH + 1)
            for c in range(CH):
                e.activation(wv[:, c, :], wv[:, c, :], ACT.Exp, bias=wm[:, c:c + 1],
                             accum_out=wsum[:, c:c + 1]).then_inc(w_ok, 1)
                e.wait_ge(w_ok, CH + 1 + c + 1)
            with e.Fori(0, BLOCKS) as i:
                e.wait_ge(var_ok, i + 1)
                e.activation(sd[:], vs[:], ACT.Sqrt).then_inc(root_ok, 1)
                e.wait_ge(turned, i + 2)
                e.wait_ge(xT_ok, i + 1)
                for c in range(CH):
                    r = e.activation(xnT[:, c, :], pT[:, c, :], ACT.Copy)
                r.then_inc(xnT_ok, 1)
                gate.scalar(e, i, False)
                e.wait_ge(stored, 16 * NST * i + 16)
                for k in range(2 * CH):
                    e.wait_ge(proj, 2 * CH * i + k + 1)
                    e.activation(qk[:, k, :], pP[:, k, :], ACT.Copy).then_inc(qk_ok, 1)
                e.wait_ge(cb_T, i + 1)
                e.activation(cT[:], pT[0:EXPERTS, 1, :], ACT.Copy).then_inc(cT_ok, 1)

        @b.vector
        def _(e):
            e.wait_ge(loaded, 16 * NW)
            e.sem_inc(v_ok, 2)
            for c in range(CH):
                e.reduce_max(wm[:, c:c + 1], wv[:, c, :], AX_X).then_inc(w_ok, 1)
            e.wait_ge(w_ok, CH)
            e.tensor_scalar(wm[:], wm[:], -1.0, None, ALU.mult).then_inc(w_ok, 1)
            e.wait_ge(w_ok, 2 * CH + 1)
            e.reciprocal(wsum[:], wsum[:]).then_inc(w_ok, 1)
            e.wait_ge(w_ok, 2 * CH + 2)
            for c in range(CH):
                e.tensor_scalar(wv[:, c, :], wv[:, c, :], wsum[:, c:c + 1], 1.0 / DIM, ALU.mult,
                                ALU.mult).then_inc(w_ok, 1)
            with e.Fori(0, BLOCKS) as i:
                d = Tally(e, dve, i, 2 * BT + 1 + Gate.STEPS)
                now = acc[:, bass.ds(i * BT, BT), :]
                one = [acc[:, bass.ds(i * BT + a, 1), :].rearrange("p t d -> p (t d)") for a in range(BT)]
                for a in range(BT):
                    e.bn_stats(st[:, a, :], one[a]).then_inc(dve, 1)
                    d.step()
                d.wait()
                e.sem_inc(passed, 1)
                for a in range(BT):
                    e.bn_aggr(mv[:, a, :], st[:, a, :]).then_inc(dve, 1)
                    d.step()
                d.wait()
                e.tensor_scalar(vs[:], mv[:, :, 1], 1e-5, None, ALU.add).then_inc(var_ok, 1)
                e.wait_ge(root_ok, i + 1)
                e.reciprocal(rs[:], sd[:]).then_inc(dve, 1)
                d.step()
                e.wait_ge(turned, i + 1)
                d.wait()
                for a in range(BT):
                    r = e.tensor_scalar(xn[:, a, :], one[a], mv[:, a, 0:1], rs[:, a:a + 1], ALU.subtract, ALU.mult)
                r.then_inc(xn_ok, 1)
                e.wait_ge(stored, 16 * NST * i + 16)
                e.wait_ge(v_ps, 2 * i + 1)
                e.tensor_copy(v[:], pV[:])
                e.tensor_tensor(now, now, pV[:], ALU.subtract).then_inc(v_ok, 1)
                e.wait_ge(logit, i + 1)
                gate.vector(e, i, d, passed, pT[:, 0, 0:BT * EXPERTS].rearrange("p (a x) -> p a x", a=BT), cb[:], False)
                e.tensor_copy(comb[:, bass.ds(i * BT, BT), 1:1 + EXPERTS], cb[:]).then_inc(cb_ok, 1)
                e.wait_ge(v_ps, 2 * i + 2)
                e.wait_ge(v_ok, 2 * i + 3)
                e.tensor_tensor(now, now, pV[:], ALU.add).then_inc(v_ok, 1)
                d.close()

        @b.gpsimd
        def _(e):
            e.sem_inc(xT_ok, 1)
            with e.Fori(0, BLOCKS) as i:
                e.wait_ge(xnT_ok, i + 1)
                e.sem_inc(passed, 1)
                e.tensor_copy(xT[:, :, bass.ds(i * BLK, BLK)], xnT[:]).then_inc(xT_ok, 1)


def attend1(nc, scr, acc):
    with Stage(nc, "a1") as s:
        qT, kT = s.sb("qT", [P, CH, SEQ]), s.sb("kT", [P, CH, SEQ])
        v, vn = s.sb("v", [P, QT, DIM]), s.sb("vn", [P, QT, DIM])
        w = s.sb("w", [P, QT, SEQ])
        top, negm, sums, rsum = (s.sb(n, [P, QT]) for n in ("top", "negm", "sums", "rsum"))
        pS = s.ps("pS", [P, 2, SEQ])
        pO = s.ps("pO", [P, 4, BANK])
        qk_in, v_in = s.sem("qk_in"), s.sem("v_in")
        scored = s.sem("scored")
        max_ok = s.sem("max_ok")
        neg_ok = s.sem("neg_ok")
        exped = s.sem("exped")
        inv_ok = s.sem("inv_ok")
        vn_ok = s.sem("vn_ok")
        av = s.sem("av")
        added = s.sem("added")
        SCALE = SEQ ** -0.5
        b = s.block()

        @b.sync
        def _(e):
            with e.Fori(0, BATCH) as i:
                now = bass.ds(i * SEQ, SEQ)
                e.wait_ge(scored, QT * i + 1)
                e.dma_start(kT[:], chunked(scr["k1T"])[:, :, now]).then_inc(qk_in, 16)
                e.dma_start(qT[:], chunked(scr["q1T"])[:, :, now]).then_inc(qk_in, 16)
                e.wait_ge(av, QT * i + 1)
                e.dma_start(v[:], tiled(scr["v1"], i, QT)).then_inc(v_in, 16)

        @b.tensor
        def _(e):
            e.sem_inc(scored, 1)
            e.sem_inc(av, 1)
            with e.Fori(0, BATCH) as i:
                e.wait_ge(qk_in, 32 * i + 32)
                for m in range(QT):
                    e.wait_ge(exped, QT * i + m + 1)
                    for half in range(2):
                        for c in range(CH):
                            r = e.matmul(pS[:, m % 2, half * BANK:(half + 1) * BANK], kT[:, c, m * P:(m + 1) * P],
                                         qT[:, c, half * BANK:(half + 1) * BANK], start=(c == 0), stop=(c == CH - 1))
                    r.then_inc(scored, 1)
                for n in range(QT):
                    e.wait_ge(added, QT * i + n + 1)
                    for m in range(QT):
                        if n == 0:
                            e.wait_ge(vn_ok, QT * i + m + 1)
                        r = e.matmul(pO[:, n % 4, 0:DIM], w[:, m, n * P:(n + 1) * P], vn[:, m, :],
                                     start=(m == 0), stop=(m == QT - 1))
                    r.then_inc(av, 1)

        @b.scalar
        def _(e):
            e.sem_inc(exped, 2)
            with e.Fori(0, BATCH) as i:
                for m in range(QT):
                    e.wait_ge(neg_ok, QT * i + m + 1)
                    if m == 0:
                        e.wait_ge(av, QT * i + 1)
                    e.activation(w[:, m, :], pS[:, m % 2, :], ACT.Exp, bias=negm[:, m:m + 1], scale=SCALE,
                                 accum_out=sums[:, m:m + 1]).then_inc(exped, 1)

        @b.vector
        def _(e):
            e.sem_inc(added, 4)
            with e.Fori(0, BATCH) as i:
                def divide(m):
                    n = QT * i + m
                    e.wait_ge(exped, n + 1 + 2)
                    e.reciprocal(rsum[:, m:m + 1], sums[:, m:m + 1]).then_inc(inv_ok, 1)
                    if m == 0:
                        e.wait_ge(v_in, 16 * i + 16)
                        e.wait_ge(av, QT * i + 1)
                    e.wait_ge(inv_ok, n + 1)
                    e.tensor_scalar(vn[:, m, :], v[:, m, :], rsum[:, m:m + 1], None, ALU.mult).then_inc(vn_ok, 1)

                for m in range(QT):
                    n = QT * i + m
                    e.wait_ge(scored, n + 1 + 1)
                    e.reduce_max(top[:, m:m + 1], pS[:, m % 2, :], AX_X).then_inc(max_ok, 1)
                    e.wait_ge(max_ok, n + 1)
                    e.tensor_scalar(negm[:, m:m + 1], top[:, m:m + 1], -SCALE, None, ALU.mult).then_inc(neg_ok, 1)
                    if m:
                        divide(m - 1)
                divide(QT - 1)
                for n in range(QT):
                    e.wait_ge(av, QT * i + n + 1 + 1)
                    now = acc[:, bass.ds(i * QT + n, 1), :].rearrange("p t d -> p (t d)")
                    e.tensor_tensor(now, now, pO[:, n % 4, 0:DIM], ALU.add).then_inc(added, 1)


def build(nc, I, out, upto=99, dbg=None):
    kind = "ExternalOutput" if dbg else "Internal"
    def dram(name, shape):
        return nc.dram_tensor(f"scr_{name}", shape, F32, kind=kind).ap()
    scr = {n: dram(n, sh) for n, sh in (
        ("xn", (TOK, DIM)), ("qT", (DIM, TOK)), ("kT", (DIM, TOK)), ("v", (TOK, DIM)), ("q2T", (DIM, TOK)),
        ("kcT", (P, TOK)), ("vc", (TOK, HD1)), ("o0", (TOK, DIM)), ("o1", (TOK, DIM)),
        ("q1T", (DIM, TOK)), ("k1T", (DIM, TOK)), ("v1", (TOK, DIM)))}
    with ExitStack() as ctx:
        ident = ctx.enter_context(nc.sbuf_tensor("ident", [P, P], F32))
        project0(nc, I, scr, ident)
        attend(nc, scr, ident, "t16", HEADS0, HD0, True)
        attend(nc, scr, ident, "rms", HEADS1, HD1, False)
        acc = ctx.enter_context(nc.sbuf_tensor("acc", [P, TILES, DIM], F32))
        xT = ctx.enter_context(nc.sbuf_tensor("xT", [P, CH, TOK], F32))
        comb = ctx.enter_context(nc.sbuf_tensor("comb", [P, TILES, 1 + EXPERTS], F32))
        route0(nc, I, scr, ident, acc, xT, comb)
        experts(nc, I, "e0", acc, xT, comb, 1 + EXPERTS, FF0, True, 0)
        project1(nc, I, scr, ident, acc, xT, comb)
        attend1(nc, scr, acc)
        experts(nc, I, "e1", acc, xT, comb, EXPERTS, FF1, False, 1, out)


def spread(w):
    import numpy as np
    rows = w.shape[0]
    wide = np.zeros((rows, GROUPS, GROUP, P // GROUP), w.dtype)
    wide[..., :HD0] = w.reshape(rows, GROUPS, GROUP, HD0)
    return wide.reshape(rows, GROUPS * P)


def columns(a):
    return a.reshape(-1, P).T


def kernel(**inputs):
    import numpy as np
    import concourse.bacc as bacc
    from concourse.bass_utils import run_bass_kernel_spmd as run

    a = {k: np.asarray(v) for k, v in inputs.items()}
    L0, F0, L1, F1 = "L0_attn_", "L0_ffn_", "L1_attn_", "L1_ffn_"
    arrays = {
        "x": a[L0 + "x"].reshape(TOK, DIM),
        "wq": spread(a[L0 + "Wq"]), "wk": spread(a[L0 + "Wk"]), "wv": a[L0 + "Wv"],
        "bq": columns(spread(a[L0 + "bq"][None])[0]), "bk": columns(spread(a[L0 + "bk"][None])[0]),
        "bv": a[L0 + "bv"], "wo": a[L0 + "Wo"], "bo": a[L0 + "bo"],
        "g1": columns(a[F0 + "g1"]), "g2": columns(a[F0 + "g2"]),
        "wq2": a[F0 + "Wq"].T, "wkc": np.concatenate([a[F0 + "Wkc"].T] * 2, axis=1), "wvc": a[F0 + "Wvc"].T,
        "wo2": a[F0 + "Wo"].T, "wr": a[F0 + "Wr"].T, "ebias": a[F0 + "expert_bias"],
        "e0_w1": np.concatenate([a[F0 + "sW1"].T[None], a[F0 + "eW1"].transpose(0, 2, 1)]).reshape(-1, FF0),
        "e0_w3": np.concatenate([a[F0 + "sW3"].T[None], a[F0 + "eW3"].transpose(0, 2, 1)]).reshape(-1, FF0),
        "e0_w2": np.concatenate([a[F0 + "sW2"].T[None], a[F0 + "eW2"].transpose(0, 2, 1)]).reshape(-1, DIM),
        "l1wq": a[L1 + "wq"], "l1wk": a[L1 + "wk"], "l1wvT": a[L1 + "wv"].T,
        "gate_w": a[F1 + "gate_w"], "gate_b": a[F1 + "gate_b"],
        "e1_w1": a[F1 + "w1"].reshape(-1, FF1), "e1_w2": a[F1 + "w2"].reshape(-1, DIM),
        "b1": a[F1 + "b1"].reshape(EXPERTS, FF1 // P, P).transpose(2, 0, 1), "b2": a[F1 + "b2"],
        "ident": np.eye(P, dtype=np.float32), "iota": np.arange(EXPERTS, dtype=np.float32),
    }
    arrays = {f"in_{k}": np.ascontiguousarray(v) for k, v in arrays.items()}
    nc = bacc.Bacc("TRN2", target_bir_lowering=False, num_devices=1)
    I = {k[3:]: nc.dram_tensor(k, v.shape, mybir.dt.from_np(v.dtype), kind="ExternalInput").ap()
         for k, v in arrays.items()}
    out = nc.dram_tensor("out", (TOK, DIM), F32, kind="ExternalOutput").ap()
    build(nc, I, out)
    r = run(nc, [arrays], core_ids=[0])
    return r.results[0]["out"].reshape(BATCH, SEQ, DIM)
```

```python
from contextlib import ExitStack

import concourse.bass as bass
from concourse import mybir

F32 = mybir.dt.float32
BF16 = mybir.dt.bfloat16
F32R = mybir.dt.float32r
U32 = mybir.dt.uint32
ALU = mybir.AluOpType
ACT = mybir.ActivationFunctionType
AX_X = mybir.AxisListType.X

P = 128
BATCH, SEQ, DIM = 4, 1024, 256
TOK = BATCH * SEQ
TILES = TOK // P
CH = DIM // P
BLK = 512
BT = BLK // P
BLOCKS = TOK // BLK
BANK = 512
HEADS0, HD0 = 16, 16
GROUP = 4
GROUPS = HEADS0 // GROUP
TOPK = 16
PARTS = 3
HI, LO = 0, 1
PRODUCTS = ((HI, HI), (HI, LO), (LO, HI))
HEADS1, HD1 = 4, 64
EXPERTS = 8
FF0, FF1 = 256, 512
NEG = -3.0e38
QT = SEQ // P
ROUNDS = QT // 2


class Stage:

    def __init__(self, nc, name):
        self.nc, self.name, self.ctx = nc, name, ExitStack()

    def __enter__(self):
        self.ctx.__enter__()
        return self

    def __exit__(self, *e):
        return self.ctx.__exit__(*e)

    def sb(self, name, shape, dt=F32):
        return self.ctx.enter_context(self.nc.sbuf_tensor(f"{self.name}_{name}", shape, dt))

    def ps(self, name, shape):
        return self.ctx.enter_context(self.nc.psum_tensor(f"{self.name}_{name}", shape, F32))

    def sem(self, name):
        return self.ctx.enter_context(self.nc.semaphore(f"{self.name}_{name}"))

    def block(self):
        return self.ctx.enter_context(self.nc.Block())


def tiled(ap, i, n=BT):
    return ap.rearrange("(t p) d -> p t d", p=P)[:, bass.ds(i * n, n), :]


def chunked(ap, c=CH):
    return ap.rearrange("(c p) n -> p c n", p=P)


def ticks(e, outer, rounds, units, steps):
    drain = max(lag for lag, _ in steps)
    assert drain <= units
    with e.Fori(0, outer) as b:
        for k in range(units):
            for lag, step in steps:
                if k >= lag:
                    step(b, 0, k - lag, "open")
        with e.Fori(1, rounds) as r:
            for k in range(units):
                for lag, step in steps:
                    if k >= lag:
                        step(b, r, k - lag, "loop")
                    else:
                        step(b, r - 1, k - lag + units, "loop")
        for k in range(drain):
            for lag, step in steps:
                if k < lag:
                    step(b, rounds - 1, units + k - lag, "drain")


class Tally:

    def __init__(self, eng, sem, round_, per):
        self.eng, self.sem, self.base, self.per, self.n = eng, sem, round_ * per, per, 0

    def step(self, k=1):
        self.n += k

    def wait(self):
        self.eng.wait_ge(self.sem, self.base + self.n)

    def close(self):
        assert self.n == self.per, (self.n, self.per)



def project0(nc, I, scr, ident):
    with Stage(nc, "pj") as s:
        wq = s.sb("wq", [P, CH, DIM])
        wk = s.sb("wk", [P, CH, DIM])
        wv = s.sb("wv", [P, CH, DIM])
        wq2 = s.sb("wq2", [P, CH, DIM])
        wkc = s.sb("wkc", [P, CH, P])
        wvc = s.sb("wvc", [P, CH, HD1])
        bq = s.sb("bq", [P, CH])
        bqs = s.sb("bqs", [P, CH])
        bk = s.sb("bk", [P, CH])
        bv = s.sb("bv", [P, DIM])
        g1 = s.sb("g1", [P, CH])
        x = s.sb("x", [P, BT, DIM])
        xn = s.sb("xn", [P, BT, DIM])
        nx = s.sb("nx", [P, BT, DIM])
        sq = s.sb("sq", [P, DIM])
        st = s.sb("st", [P, BT, 6])
        mv = s.sb("mv", [P, BT, 2])
        vs = s.sb("vs", [P, BT])
        ms = s.sb("ms", [P, BT])
        sd = s.sb("sd", [P, BT])
        rs = s.sb("rs", [P, BT])
        xnT = s.sb("xnT", [P, CH, BLK])
        nxT = s.sb("nxT", [P, CH, BLK])
        qT = s.sb("qT", [P, CH, BLK])
        kT = s.sb("kT", [P, CH, BLK])
        qP = s.sb("qP", [P, PARTS, CH, BLK], BF16)
        kP = s.sb("kP", [P, PARTS, CH, BLK], BF16)
        v = s.sb("v", [P, BT, DIM])
        q2T = s.sb("q2T", [P, CH, BLK])
        kcT = s.sb("kcT", [P, BLK])
        vc = s.sb("vc", [P, BT, HD1])
        pT = s.ps("pT", [P, CH, BLK])
        pP = s.ps("pP", [P, 4, BLK])
        pV = s.ps("pV", [P, BT, DIM])

        loaded = s.sem("loaded")
        x_in = s.sem("x_in")
        xn_ok = s.sem("xn_ok")
        nx_ok = s.sem("nx_ok")
        dve = s.sem("dve")
        var_ok = s.sem("var_ok")
        root_ok = s.sem("root_ok")
        sq_ok = s.sem("sq_ok")
        turned = s.sem("turned")
        xnT_ok = s.sem("xnT_ok")
        nxT_ok = s.sem("nxT_ok")
        proj = s.sem("proj")
        proj_out = s.sem("proj_out")
        q_split = s.sem("q_split")
        k_split = s.sem("k_split")
        pv_ok = s.sem("pv_ok")
        pv_out = s.sem("pv_out")
        stored = s.sem("stored")
        passed = s.sem("passed")
        NW, NP = 11, 3 * CH + 1
        NST = 5 + 2 * PARTS
        b = s.block()

        @b.sync
        def _(e):
            for dst, src in ((wq[:], chunked(I["wq"])), (wk[:], chunked(I["wk"])), (wv[:], chunked(I["wv"])),
                             (wq2[:], chunked(I["wq2"])), (wkc[:], chunked(I["wkc"])), (wvc[:], chunked(I["wvc"])),
                             (bq[:], I["bq"]), (bk[:], I["bk"]), (bv[:], I["bv"].partition_broadcast(P)),
                             (g1[:], I["g1"]), (ident[:], I["ident"])):
                e.dma_start(dst, src).then_inc(loaded, 16)
            e.sem_inc(stored, 16)
            with e.Fori(0, BLOCKS) as i:
                now = bass.ds(i * BLK, BLK)
                e.wait_ge(xn_ok, i + 1)
                e.dma_start(x[:], tiled(I["x"], i)).then_inc(x_in, 16)
                e.wait_ge(xn_ok, i + 2)
                e.dma_start(tiled(scr["xn"], i), xn[:]).then_inc(stored, 16)
                e.wait_ge(pv_out, 2 * i + 2)
                e.dma_start(tiled(scr["v"], i), v[:]).then_inc(stored, 16)
                for t, name, split in ((qP, "qP", q_split), (kP, "kP", k_split)):
                    e.wait_ge(split, 4 * i + 4 + 4)
                    for p in range(PARTS):
                        e.dma_start(chunked(scr[name][p])[:, :, now], t[:, p]).then_inc(stored, 16)
                e.wait_ge(proj_out, NP * i + NP + 4)
                e.sem_inc(passed, 1)
                e.dma_start(chunked(scr["q2T"])[:, :, now], q2T[:]).then_inc(stored, 16)
                e.dma_start(scr["kcT"][:, now], kcT[:]).then_inc(stored, 16)
                e.wait_ge(pv_out, 2 * i + 3)
                e.dma_start(tiled(scr["vc"], i), vc[:]).then_inc(stored, 16)
            e.wait_ge(stored, 16 * NST * BLOCKS + 16)

        def split(e, i, t, parts, done):
            e.tensor_copy(parts[:, 0], t[:]).then_inc(done, 1)
            e.wait_ge(done, 4 * i + 1 + 4)
            e.tensor_tensor(t[:], t[:], parts[:, 0], ALU.subtract).then_inc(done, 1)
            e.wait_ge(done, 4 * i + 2 + 4)
            e.sem_inc(passed, 1)
            e.tensor_copy(parts[:, 1], t[:]).then_inc(done, 1)
            e.wait_ge(done, 4 * i + 3 + 4)
            e.tensor_tensor(parts[:, 2], t[:], parts[:, 1], ALU.subtract).then_inc(done, 1)

        @b.gpsimd
        def _(e):
            e.sem_inc(k_split, 4)
            with e.Fori(0, BLOCKS) as i:
                e.wait_ge(stored, 16 * NST * i + 16)
                e.wait_ge(proj_out, NP * i + 2 * CH + 4)
                e.sem_inc(passed, 1)
                split(e, i, kT, kP, k_split)

        @b.vector
        def _(e):
            e.wait_ge(loaded, 16 * NW)
            e.sem_inc(xn_ok, 1)
            e.sem_inc(pv_out, 1)
            e.sem_inc(q_split, 4)
            with e.Fori(0, BLOCKS) as i:
                d = Tally(e, dve, i, 2 * BT + 2)
                e.wait_ge(x_in, 16 * i + 16)
                for a in range(BT):
                    e.bn_stats(st[:, a, :], x[:, a, :]).then_inc(dve, 1)
                    d.step()
                d.wait()
                e.sem_inc(passed, 1)
                for a in range(BT):
                    e.bn_aggr(mv[:, a, :], st[:, a, :]).then_inc(dve, 1)
                    d.step()
                d.wait()
                e.tensor_scalar(vs[:], mv[:, :, 1], 1e-5, None, ALU.add).then_inc(var_ok, 1)
                e.wait_ge(root_ok, 2 * i + 1)
                e.reciprocal(rs[:], sd[:]).then_inc(dve, 1)
                d.step()
                e.wait_ge(turned, 2 * i + 1)
                e.wait_ge(stored, 16 * NST * i + 16)
                d.wait()
                for a in range(BT):
                    r = e.tensor_scalar(xn[:, a, :], x[:, a, :], mv[:, a, 0:1], rs[:, a:a + 1],
                                        ALU.subtract, ALU.mult)
                r.then_inc(xn_ok, 1)
                e.wait_ge(sq_ok, BT * i + BT)
                e.tensor_scalar(vs[:], ms[:], 1.0 / DIM, 1e-6, ALU.mult, ALU.add).then_inc(var_ok, 1)
                e.wait_ge(root_ok, 2 * i + 2)
                e.reciprocal(rs[:], sd[:]).then_inc(dve, 1)
                d.step()
                e.wait_ge(turned, 2 * i + 2)
                d.wait()
                for a in range(BT):
                    r = e.tensor_scalar(nx[:, a, :], xn[:, a, :], rs[:, a:a + 1], None, ALU.mult)
                r.then_inc(nx_ok, 1)
                e.wait_ge(turned, 2 * i + 4)
                for c in range(CH):
                    r = e.tensor_scalar(nxT[:, c, :], pT[:, c, :], g1[:, c:c + 1], None, ALU.mult)
                r.then_inc(nxT_ok, 1)
                e.wait_ge(pv_ok, 2 * i + 1)
                for a in range(BT):
                    r = e.tensor_tensor(v[:, a, :], pV[:, a, :], bv[:], ALU.add)
                r.then_inc(pv_out, 1)
                e.wait_ge(pv_ok, 2 * i + 2)
                e.tensor_copy(vc[:], pV[:, :, 0:HD1]).then_inc(pv_out, 1)
                e.wait_ge(proj_out, NP * i + CH + 4)
                split(e, i, qT, qP, q_split)
                d.close()

        @b.scalar
        def _(e):
            e.wait_ge(loaded, 16 * NW)
            e.sem_inc(proj_out, 4)
            e.activation(bqs[:], bq[:], ACT.Copy, scale=HD0 ** -0.5)
            with e.Fori(0, BLOCKS) as i:
                e.wait_ge(var_ok, 2 * i + 1)
                e.activation(sd[:], vs[:], ACT.Sqrt).then_inc(root_ok, 1)
                e.wait_ge(xn_ok, i + 2)
                for a in range(BT):
                    e.activation(sq[:], xn[:, a, :], ACT.Square, accum_out=ms[:, a:a + 1]).then_inc(sq_ok, 1)
                    e.wait_ge(sq_ok, BT * i + a + 1)
                e.wait_ge(var_ok, 2 * i + 2)
                e.activation(sd[:], vs[:], ACT.Sqrt).then_inc(root_ok, 1)
                e.wait_ge(turned, 2 * i + 3)
                for c in range(CH):
                    r = e.activation(xnT[:, c, :], pT[:, c, :], ACT.Copy)
                r.then_inc(xnT_ok, 1)
                e.wait_ge(stored, 16 * NST * i + 16)
                e.wait_ge(q_split, 4 * i + 4)
                e.wait_ge(k_split, 4 * i + 4)
                k = 0
                for dst, bias, scale in ((qT, bqs, HD0 ** -0.5), (kT, bk, 1.0), (q2T, None, HD1 ** -0.5)):
                    for c in range(CH):
                        k += 1
                        e.wait_ge(proj, NP * i + k)
                        if bias is None:
                            r = e.activation(dst[:, c, :], pP[:, (k - 1) % 4, :], ACT.Copy, scale=scale)
                        else:
                            r = e.activation(dst[:, c, :], pP[:, (k - 1) % 4, :], ACT.Identity,
                                             bias=bias[:, c:c + 1], scale=scale)
                        r.then_inc(proj_out, 1)
                e.wait_ge(proj, NP * i + NP)
                e.activation(kcT[:], pP[:, k % 4, :], ACT.Copy).then_inc(proj_out, 1)

        @b.tensor
        def _(e):
            e.wait_ge(loaded, 16 * NW)
            e.sem_inc(turned, 2)

            def turn(src):
                for c in range(CH):
                    for a in range(BT):
                        r = e.transpose(pT[:, c, a * P:(a + 1) * P], src[:, a, c * P:(c + 1) * P], ident[:])
                return r

            def project(i, k, w, m, srcT):
                e.wait_ge(proj_out, NP * i + k + 1)
                for c in range(CH):
                    r = e.matmul(pP[:, k % 4, :], w[:, c, m * P:(m + 1) * P], srcT[:, c, :],
                                 start=(c == 0), stop=(c == CH - 1))
                r.then_inc(proj, 1)

            with e.Fori(0, BLOCKS) as i:
                e.wait_ge(xn_ok, i + 2)
                turn(xn).then_inc(turned, 1)
                e.wait_ge(xnT_ok, i + 1)
                e.wait_ge(nx_ok, i + 1)
                turn(nx).then_inc(turned, 1)
                for k in range(2 * CH):
                    if k == 0:
                        e.wait_ge(proj_out, NP * i + 4)
                    project(i, k, wq if k < CH else wk, k % CH, xnT)
                e.wait_ge(pv_out, 2 * i + 1)
                for a in range(BT):
                    for c in range(CH):
                        r = e.matmul(pV[:, a, :], xnT[:, c, a * P:(a + 1) * P], wv[:, c, :],
                                     start=(c == 0), stop=(c == CH - 1))
                r.then_inc(pv_ok, 1)
                e.wait_ge(nxT_ok, i + 1)
                for k in range(2 * CH, NP):
                    project(i, k, wq2 if k < 3 * CH else wkc, k % CH if k < 3 * CH else 0, nxT)
                e.wait_ge(pv_out, 2 * i + 2)
                for a in range(BT):
                    for c in range(CH):
                        r = e.matmul(pV[:, a, 0:HD1], nxT[:, c, a * P:(a + 1) * P], wvc[:, c, :],
                                     start=(c == 0), stop=(c == CH - 1))
                r.then_inc(pv_ok, 1)


def attend(nc, scr, ident):
    with Stage(nc, "at") as s:
        BLKU = GROUP + 1
        TU = GROUPS * BLKU
        U = 2 * TU
        BU = QT * TU
        WIDE = P // GROUP
        SLOTS = 2 * PARTS
        KQ = SLOTS * HD0
        R, RT = 5, 10
        Q_PART = (0, 0, 1, 1, 0, 2)
        K_PART = (0, 1, 0, 1, 2, 0)
        q = s.sb("q", [KQ, HEADS0, SEQ], BF16)
        k = s.sb("k", [KQ, HEADS0, SEQ], BF16)
        v = s.sb("v", [P, QT, DIM + HD0])
        q2 = s.sb("q2", [P, HEADS1 // 2, P])
        kc = s.sb("kc", [P, SEQ])
        vc = s.sb("vc", [P, QT, HD1])
        sb = s.sb("sb", [P, R, SEQ])
        cut = s.sb("cut", [P, SEQ])
        w = s.sb("w", [P, R, SEQ])
        wT = s.sb("wT", [P, RT, SEQ])
        m8 = s.sb("m8", [P, R, TOPK])
        negm = s.sb("negm", [P, R])
        sums = s.sb("sums", [P, 2, TU])
        rsum = s.sb("rsum", [P, 2, TU])
        oT = s.sb("oT", [P, 2, BANK])
        o = [s.sb(f"o{j}", [P, 2, DIM]) for j in range(2)]
        pS = s.ps("pS", [P, 2, SEQ])
        pT = s.ps("pT", [P, 2, BANK])
        pO = s.ps("pO", [P, 2, BANK])

        kq_in = [s.sem(f"kq_in{g}") for g in range(GROUPS)]
        kc_in, v_in = s.sem("kc_in"), s.sem("v_in")
        q2_in = [s.sem(f"q2_in{g}") for g in range(2)]
        scored = s.sem("scored")
        copied = s.sem("copied")
        thr_ok = s.sem("thr_ok")
        dmask = s.sem("dmask")
        pmask = s.sem("pmask")
        exped = s.sem("exped")
        turned = s.sem("turned")
        pT_free = [s.sem(f"pT_free{j}") for j in range(2)]
        av = s.sem("av")
        oT_ok = s.sem("oT_ok")
        back = s.sem("back")
        divided = s.sem("divided")
        o_ok = s.sem("o_ok")
        stored = [s.sem(f"stored{j}") for j in range(2)]
        dve = s.sem("dve")
        passed = s.sem("passed")
        pad = s.sem("pad")
        CUT = 288
        b = s.block()

        def dense(k):
            return k % BLKU == GROUP

        closers = [k for k in range(U) if k % BLKU == GROUP - 1 or k % (2 * BLKU) == 2 * BLKU - 1]
        GR = len(closers)

        def group_of(k):
            return closers.index(k // (2 * BLKU) * 2 * BLKU + 2 * BLKU - 1 if dense(k) else k // BLKU * BLKU + GROUP - 1)

        def unit(bi, r, k):
            return (bi * ROUNDS + r) * U + k

        def tile(bi, r, k):
            return (bi * ROUNDS + r) * 2 + k // TU

        def turns_before(bi, r, k, phase):
            n = (bi * ROUNDS + r) * (U + 2) + k + (k > TU + 3)
            return n if phase == "open" or k > 3 else n - 1

        def pT_uses(bi, r, k, phase):
            return (bi * ROUNDS + r) * (U + 2) + (TU + 4 if k < TU else U + 1 if phase == "drain" else U + 1 + 4)

        def sparse_no(bi, r, k):
            return (bi * ROUNDS + r) * (2 * HEADS0) + k // BLKU * GROUP + k % BLKU

        @b.sync
        def _(e):
            def load_stacks(bi, g):
                now, heads = bass.ds(bi * SEQ, SEQ), slice(g * GROUP, (g + 1) * GROUP)
                e.wait_ge(scored, bi * BU + BLKU * g + GROUP)
                e.sem_inc(passed, 1)
                for dst, name, part in ((q, "qP", Q_PART), (k, "kP", K_PART)):
                    for slot in range(SLOTS):
                        src = scr[name][part[slot]].rearrange("(h d) n -> d h n", d=HD0)
                        e.dma_start(dst[slot * HD0:(slot + 1) * HD0, heads, :], src[:, heads, now]
                                    ).then_inc(kq_in[g], 16)

            def load_q2(t, g):
                e.wait_ge(scored, t * TU + 2 * BLKU * (g + 1))
                e.sem_inc(passed, 1)
                e.dma_start(q2[:, g, :], chunked(scr["q2T"])[:, g, bass.ds(t * P, P)]).then_inc(q2_in[g], 16)

            with e.Fori(0, BATCH) as bi:
                load_stacks(bi, 0)
                load_stacks(bi, 1)
                load_q2(bi * QT, 0)
                load_stacks(bi, 2)
                load_stacks(bi, 3)
                load_q2(bi * QT, 1)
                e.wait_ge(scored, bi * BU + TU)
                e.sem_inc(passed, 1)
                e.dma_start(kc[:], scr["kcT"][:, bass.ds(bi * SEQ, SEQ)]).then_inc(kc_in, 16)
                e.wait_ge(av, bi * (GR * ROUNDS) + GR)
                e.sem_inc(passed, 1)
                e.dma_start(v[:, :, 0:DIM], tiled(scr["v"], bi, QT)).then_inc(v_in, 16)
                e.dma_start(vc[:], tiled(scr["vc"], bi, QT)).then_inc(v_in, 16)
                with e.Fori(1, QT) as t:
                    load_q2(bi * QT + t, 0)
                    load_q2(bi * QT + t, 1)

        @b.tensor
        def _(e):
            e.sem_inc(scored, TU)
            e.sem_inc(turned, 2 * R)
            e.sem_inc(av, GR)
            e.sem_inc(back, 1)

            def scores(bi, r, u, phase):
                n = unit(bi, r, u)
                blk = u % TU // BLKU
                h = blk * GROUP + u % BLKU
                if phase == "open" and u < TU:
                    if u % BLKU == 0:
                        e.wait_ge(kq_in[blk], 16 * 2 * SLOTS * (bi + 1))
                    if u == GROUP:
                        e.wait_ge(kc_in, 16 * (bi + 1))
                if dense(u) and blk % 2 == 0:
                    e.wait_ge(q2_in[blk // 2], 16 * (tile(bi, r, u) + 1))
                e.wait_ge(copied, n + 1)
                for c in range(SEQ // BANK):
                    keys = slice(c * BANK, (c + 1) * BANK)
                    if dense(u):
                        rows = slice(HD1 * (blk % 2), HD1 * (blk % 2) + HD1)
                        m = e.matmul(pS[:, u % 2, keys], q2[rows, blk // 2, :], kc[rows, keys], start=True, stop=True)
                    else:
                        m = e.matmul(pS[:, u % 2, keys], q[:, h, bass.ds((r * 2 + u // TU) * P, P)], k[:, h, keys],
                                     start=True, stop=True)
                m.then_inc(scored, 1)

            def turn(bi, r, u, phase):
                n, before = unit(bi, r, u), turns_before(bi, r, u, phase)
                e.wait_ge(exped, n + 1 + R)
                for j in range(2):
                    e.wait_ge(pT_free[j], before + 1)
                    for c in range(4 * j, 4 * j + 4):
                        m = e.transpose(pT[:, j, (c % 4) * P:(c % 4 + 1) * P], w[:, u % R, c * P:(c + 1) * P], ident[:])
                    m.then_inc(turned, 1)

            def outputs(bi, r, u, phase, half):
                if u not in closers:
                    return
                if phase == "open" and u == closers[0] and half == 0:
                    e.wait_ge(v_in, 32 * (bi + 1))
                    e.wait_ge(pad, 1)
                if u % TU in (GROUP - 1, 2 * BLKU - 1) and half == 0:
                    e.wait_ge(oT_ok, tile(bi, r, u) + 1)
                e.wait_ge(pT_free[half], turns_before(bi, r, u, phase) + 2)
                blk = u % TU // BLKU
                for c in range(half * QT // 2, (half + 1) * QT // 2):
                    for j in range(2 if dense(u) else GROUP):
                        if dense(u):
                            slot = (u - BLKU * (1 - j)) % RT
                            out = pO[HD1 * j:HD1 * (j + 1), 1, blk // 2 * P:(blk // 2 + 1) * P]
                            vals = vc[:, c, :]
                        else:
                            slot, h = (u - (GROUP - 1) + j) % RT, blk * GROUP + j
                            out = pO[WIDE * j:WIDE * (j + 1), 0, blk * P:(blk + 1) * P]
                            vals = v[:, c, h * HD0:h * HD0 + WIDE]
                        m = e.matmul(out, vals, wT[:, slot, c * P:(c + 1) * P], start=(c == 0), stop=(c == QT - 1),
                                     skip_group_check=True)
                if half == 1:
                    m.then_inc(av, 1)

            def outputs0(bi, r, u, phase):
                outputs(bi, r, u, phase, 0)

            def outputs1(bi, r, u, phase):
                outputs(bi, r, u, phase, 1)

            def turn_back(bi, r, u, phase):
                if u % TU != TU - 1:
                    return
                t = tile(bi, r, u)
                before = pT_uses(bi, r, u, phase)
                e.wait_ge(oT_ok, t + 1 + 1)
                for j in range(2):
                    e.wait_ge(pT_free[j], before + 1)
                    for g in range((GROUPS, 2)[j]):
                        m = e.transpose(pT[:, j, g * P:(g + 1) * P], oT[:, j, g * P:(g + 1) * P], ident[:])
                m.then_inc(back, 1)

            ticks(e, BATCH, ROUNDS, U, [(0, scores), (4, turn), (7, outputs1), (6, outputs0), (8, turn_back)])

        @b.scalar
        def _(e):
            e.sem_inc(copied, 2)
            e.sem_inc(exped, R)
            e.sem_inc(oT_ok, 1)
            for j in range(2):
                e.sem_inc(pT_free[j], 1)
                e.sem_inc(stored[j], 32)

            def copy(bi, r, u, phase):
                n = unit(bi, r, u)
                e.wait_ge(scored, n + 1 + TU)
                e.wait_ge(dmask, n + 1)
                e.wait_ge(pmask, 2 * n + 2)
                e.wait_ge(exped, n + 1)
                e.activation(sb[:, u % R, :], pS[:, u % 2, :], ACT.Copy).then_inc(copied, 1)

            def exp(bi, r, u, phase):
                n = unit(bi, r, u)
                e.wait_ge(dmask, n + 1 + R)
                e.wait_ge(pmask, 2 * n + 2 + 2 * R)
                if dense(u):
                    e.wait_ge(turned, 2 * n + 2)
                if u % TU == 0:
                    e.wait_ge(o_ok, tile(bi, r, u) + 1)
                e.activation(w[:, u % R, :], (sb if dense(u) else w)[:, u % R, :], ACT.Exp,
                             bias=negm[:, u % R:u % R + 1],
                             accum_out=sums[:, u // TU, u % TU:u % TU + 1]).then_inc(exped, 1)

            def copy_turned(bi, r, u, phase):
                n, g = unit(bi, r, u), (bi * ROUNDS + r) * GR
                e.wait_ge(av, g + group_of(u - RT) + 1 + GR if u >= RT else g + group_of(u - RT + U) + 1)
                for j in range(2):
                    e.wait_ge(turned, 2 * n + j + 1 + 2 * R)
                    e.activation(wT[:, u % RT, j * BANK:(j + 1) * BANK], pT[:, j, :], ACT.Copy).then_inc(pT_free[j], 1)

            def outputs_out(bi, r, u, phase):
                if u % TU != TU - 1:
                    return
                t = tile(bi, r, u)
                e.wait_ge(av, (bi * ROUNDS + r) * GR + group_of(u) + 1 + GR)
                e.wait_ge(back, t + 1)
                e.activation(oT[:, 0, :], pO[:, 0, :], ACT.Copy)
                e.activation(oT[:, 1, 0:2 * P], pO[:, 1, 0:2 * P], ACT.Copy).then_inc(oT_ok, 1)

            def store(bi, r, u, phase):
                if u % TU != TU - 1:
                    return
                t = tile(bi, r, u)
                e.wait_ge(o_ok, t + 1 + 2)
                for j in range(2):
                    e.dma_start(scr[f"o{j}"].rearrange("(t p) d -> p t d", p=P)[:, bass.ds(t, 1), :],
                                o[j][:, u // TU].unsqueeze(1)).then_inc(stored[u // TU], 16)

            ticks(e, BATCH, ROUNDS, U, [(0, copy), (3, exp), (4, copy_turned), (7, outputs_out), (11, store)])
            for j in range(2):
                e.wait_ge(stored[j], 32 * (BATCH * ROUNDS + 1))

        @b.vector
        def _(e):
            e.sem_inc(dmask, R)
            e.sem_inc(o_ok, 2)

            def largest(bi, r, u, phase):
                n, z = unit(bi, r, u), u % R
                e.wait_ge(copied, n + 1 + 2)
                e.sem_inc(passed, 1)
                if dense(u):
                    e.reduce_max(m8[:, z, 0:1], sb[:, z, :], AX_X).then_inc(thr_ok, 1)
                else:
                    e.max(m8[:, z, 0:8], sb[:, z, :]).then_inc(dve, 1)

            def mask(bi, r, u, phase):
                n, z = unit(bi, r, u), u % R
                e.wait_ge(turned, 2 * n + 2)
                e.wait_ge(thr_ok, n + 1)
                if dense(u):
                    e.tensor_scalar(negm[:, z:z + 1], m8[:, z, 0:1], -1.0, None, ALU.mult).then_inc(dmask, 1)
                else:
                    e.scalar_tensor_tensor(w[:, z, 0:CUT], sb[:, z, 0:CUT], m8[:, z, TOPK - 1:TOPK],
                                           sb[:, z, 0:CUT], ALU.is_ge, ALU.mult).then_inc(dmask, 1)

            def next_largest(bi, r, u, phase):
                if dense(u):
                    return
                n, sn, z = unit(bi, r, u), sparse_no(bi, r, u), u % R
                e.wait_ge(dve, 2 * sn + 1)
                e.sem_inc(passed, 1)
                e.match_replace(cut[:], m8[:, z, 0:8], sb[:, z, :], NEG).then_inc(dve, 1)
                e.tensor_scalar(negm[:, z:z + 1], m8[:, z, 0:1], 0.0, -1.0, ALU.max, ALU.mult)
                e.wait_ge(dve, 2 * sn + 2)
                e.sem_inc(passed, 1)
                e.max(m8[:, z, 8:16], cut[:]).then_inc(thr_ok, 1)

            def divide(bi, r, u, phase):
                if u % TU != TU - 1:
                    return
                t, half = tile(bi, r, u), u // TU
                e.wait_ge(back, t + 1 + 1)
                e.reciprocal(rsum[:, half, :], sums[:, half, :]).then_inc(divided, 1)
                e.wait_ge(stored[half], 32 * (bi * ROUNDS + r + 1))
                e.wait_ge(divided, t + 1)
                rb = rsum[:, half, :].rearrange("p (b u) -> p b u", u=BLKU)
                e.tensor_tensor(o[0][:, half, :].rearrange("p (b j d) -> p b j d", b=GROUPS, j=GROUP),
                                pT[:, 0, :].rearrange("p (b j d) -> p b j d", b=GROUPS, j=GROUP)[:, :, :, 0:HD0],
                                rb[:, :, 0:GROUP].unsqueeze(3).to_broadcast([P, GROUPS, GROUP, HD0]),
                                ALU.mult).then_inc(pT_free[0], 1)
                e.tensor_tensor(o[1][:, half, :].rearrange("p (h d) -> p h d", h=HEADS1),
                                pT[:, 1, 0:2 * P].rearrange("p (h d) -> p h d", h=HEADS1),
                                rb[:, :, GROUP].unsqueeze(2).to_broadcast([P, HEADS1, HD1]),
                                ALU.mult).then_inc(pT_free[1], 1)
                for j in range(2):
                    e.wait_ge(pT_free[j], pT_uses(bi, r, u, phase) + 2)
                e.sem_inc(o_ok, 1)

            ticks(e, BATCH, ROUNDS, U, [(0, largest), (1, mask), (0, next_largest), (8, divide)])

        @b.gpsimd
        def _(e):
            e.sem_inc(pmask, 2 * R)
            e.memset(v[:, :, DIM:], 0.0).then_inc(pad, 1)

            def mask(bi, r, u, phase):
                n, z = unit(bi, r, u), u % R
                if dense(u):
                    e.wait_ge(pmask, 2 * n + 2 * R)
                    e.sem_inc(pmask, 2)
                    return
                e.wait_ge(turned, 2 * n + 2)
                e.wait_ge(thr_ok, n + 1)
                e.sem_inc(passed, 1)
                e.tensor_scalar(w[:, z, CUT:], sb[:, z, CUT:], m8[:, z, TOPK - 1:TOPK], None,
                                ALU.is_ge).then_inc(pmask, 1)
                e.wait_ge(pmask, 2 * n + 1 + 2 * R)
                e.tensor_tensor(w[:, z, CUT:], w[:, z, CUT:], sb[:, z, CUT:], ALU.mult).then_inc(pmask, 1)

            ticks(e, BATCH, ROUNDS, U, [(0, mask)])


def split_xT(e, i, src, xT, hi_ok, ok, passed):
    now = bass.ds(i * BLK, BLK)
    e.sem_inc(passed, 1)
    e.tensor_copy(xT[:, HI, :, now], src[:]).then_inc(hi_ok, 1)
    e.wait_ge(hi_ok, i + 1)
    e.sem_inc(passed, 1)
    e.tensor_tensor(xT[:, LO, :, now], src[:], xT[:, HI, :, now], ALU.subtract).then_inc(ok, 1)


class Gate:

    def __init__(self, s, bias_in):
        t = [P, BT, EXPERTS]
        self.bias = s.sb("g_bias", [P, EXPERTS])
        self.bias_in = bias_in
        self.iota = s.sb("g_iota", [P, EXPERTS])
        self.lg, self.pr, self.oh = s.sb("g_lg", t), s.sb("g_pr", t), s.sb("g_oh", t)
        self.m8, self.ixf = s.sb("g_m8", t), s.sb("g_ixf", t)
        self.ix = s.sb("g_ix", t, U32)
        self.r = s.sb("g_r", [P, BT])
        self.c = s.sb("g_c", [P, 2, BT])
        self.exp_in = s.sem("g_exp_in")
        self.exp_out = s.sem("g_exp_out")

    def vector(self, e, i, d, passed, logits, comb, soft):
        t = [P, BT, EXPERTS]
        many = lambda a: a.unsqueeze(2).to_broadcast(t)
        n_exp = 2 if soft else 1
        def tt(out, a, b, op):
            e.tensor_tensor(out, a, b, op).then_inc(d.sem, 1)
            d.step()
            d.wait()
        tt(self.lg[:], logits, self.bias[:].unsqueeze(1).to_broadcast(t), ALU.add)
        e.reduce_max(self.r[:], self.lg[:], AX_X).then_inc(d.sem, 1)
        d.step()
        d.wait()
        e.tensor_tensor(self.lg[:], self.lg[:], many(self.r[:]), ALU.subtract).then_inc(self.exp_in, 1)
        e.wait_ge(self.exp_out, n_exp * i + 1)
        e.reduce_sum(self.r[:], self.pr[:], AX_X).then_inc(d.sem, 1)
        d.step()
        d.wait()
        e.reciprocal(self.r[:], self.r[:]).then_inc(d.sem, 1)
        d.step()
        d.wait()
        tt(self.pr[:], self.pr[:], many(self.r[:]), ALU.mult)
        e.sem_inc(passed, 1)
        for a in range(BT):
            e.max(self.m8[:, a, :], self.pr[:, a, :]).then_inc(d.sem, 1)
            d.step()
        d.wait()
        e.sem_inc(passed, 1)
        for a in range(BT):
            e.max_index(self.ix[:, a, :], self.m8[:, a, :], self.pr[:, a, :]).then_inc(d.sem, 1)
            d.step()
        d.wait()
        e.tensor_copy(self.ixf[:], self.ix[:]).then_inc(d.sem, 1)
        d.step()
        if soft:
            e.tensor_tensor(self.c[:, 1, :], self.m8[:, :, 1], self.m8[:, :, 0], ALU.subtract
                            ).then_inc(self.exp_in, 1)
            e.wait_ge(self.exp_out, n_exp * i + 2)
            e.tensor_scalar(self.r[:], self.c[:, 1, :], 1.0, None, ALU.add).then_inc(d.sem, 1)
            d.step()
        else:
            e.tensor_tensor(self.r[:], self.m8[:, :, 1], self.m8[:, :, 0], ALU.add).then_inc(d.sem, 1)
            d.step()
        d.wait()
        e.reciprocal(self.r[:], self.r[:]).then_inc(d.sem, 1)
        d.step()
        d.wait()
        if soft:
            e.tensor_copy(self.c[:, 0, :], self.r[:]).then_inc(d.sem, 1)
            d.step()
            tt(self.c[:, 1, :], self.c[:, 1, :], self.r[:], ALU.mult)
        else:
            for m in range(2):
                tt(self.c[:, m, :], self.m8[:, :, m], self.r[:], ALU.mult)
        iota = self.iota[:].unsqueeze(1).to_broadcast(t)
        tt(self.oh[:], iota, many(self.ixf[:, :, 0]), ALU.is_equal)
        tt(self.oh[:], self.oh[:], many(self.c[:, 0, :]), ALU.mult)
        tt(self.lg[:], iota, many(self.ixf[:, :, 1]), ALU.is_equal)
        tt(self.lg[:], self.lg[:], many(self.c[:, 1, :]), ALU.mult)
        tt(comb, self.lg[:], self.oh[:], ALU.add)

    STEPS = 1 + 1 + 1 + 1 + 1 + BT + BT + 1 + 1 + 1 + 2 + 5

    def scalar(self, e, i, soft):
        n = 2 if soft else 1
        e.wait_ge(self.exp_in, n * i + 1)
        e.activation(self.pr[:], self.lg[:], ACT.Exp).then_inc(self.exp_out, 1)
        if soft:
            e.wait_ge(self.exp_in, n * i + 2)
            e.activation(self.c[:, 1, :], self.c[:, 1, :], ACT.Exp).then_inc(self.exp_out, 1)


def route0(nc, I, scr, ident, acc, xT, comb):
    with Stage(nc, "rt") as s:
        wo = [s.sb(f"wo{j}", [P, CH, DIM]) for j in range(2)]
        wr = s.sb("wr", [P, CH, EXPERTS])
        bo = s.sb("bo", [P, DIM])
        g2 = s.sb("g2", [P, CH])
        o = [s.sb(f"o{j}", [P, BT, DIM]) for j in range(2)]
        x = s.sb("x", [P, BT, DIM])
        xn = s.sb("xn", [P, BT, DIM])
        nx = s.sb("nx", [P, BT, DIM])
        sq = s.sb("sq", [P, DIM])
        ms, vs, sd, rs = (s.sb(n, [P, BT]) for n in ("ms", "vs", "sd", "rs"))
        oT = [s.sb(f"oT{j}", [P, CH, BLK]) for j in range(2)]
        nxT = s.sb("nxT", [P, CH, BLK])
        pT = s.ps("pT", [P, CH, BLK])
        pP = s.ps("pP", [P, 2, BT, DIM])
        pL = s.ps("pL", [P, BT, EXPERTS])
        loaded = s.sem("loaded")
        o_in = s.sem("o_in")
        x_in = s.sem("x_in")
        turned = s.sem("turned")
        oT_ok = s.sem("oT_ok")
        proj = s.sem("proj")
        x2_ok = s.sem("x2_ok")
        sq_ok = s.sem("sq_ok")
        var_ok = s.sem("var_ok")
        root_ok = s.sem("root_ok")
        nx_ok = s.sem("nx_ok")
        nxT_ok = s.sem("nxT_ok")
        logit = s.sem("logit")
        xT_hi = s.sem("xT_hi")
        xT_ok = s.sem("xT_ok")
        done = s.sem("done")
        dve = s.sem("dve")
        passed = s.sem("passed")
        gate = Gate(s, I["ebias"])
        b = s.block()
        NW = 7

        @b.sync
        def _(e):
            for dst, src in ((wo[0][:], chunked(I["wo"])), (wo[1][:], chunked(I["wo2"])), (wr[:], chunked(I["wr"])),
                             (bo[:], I["bo"].partition_broadcast(P)), (g2[:], I["g2"]),
                             (gate.bias[:], I["ebias"].partition_broadcast(P)),
                             (gate.iota[:], I["iota"].partition_broadcast(P))):
                e.dma_start(dst, src).then_inc(loaded, 16)
            with e.Fori(0, BLOCKS) as i:
                e.wait_ge(turned, 3 * i + 3)
                for j in range(2):
                    e.dma_start(o[j][:], tiled(scr[f"o{j}"], i)).then_inc(o_in, 16)
                e.wait_ge(done, i + 1)
                e.dma_start(x[:], tiled(I["x"], i)).then_inc(x_in, 16)
                e.dma_start(xn[:], tiled(scr["xn"], i)).then_inc(x_in, 16)

        @b.tensor
        def _(e):
            e.wait_ge(loaded, 16 * NW)
            e.sem_inc(turned, 3)

            def turn(src):
                for c in range(CH):
                    for a in range(BT):
                        r = e.transpose(pT[:, c, a * P:(a + 1) * P], src[:, a, c * P:(c + 1) * P], ident[:])
                return r

            with e.Fori(0, BLOCKS) as i:
                e.wait_ge(o_in, 32 * i + 32)
                e.wait_ge(nxT_ok, i + 1)
                turn(o[0]).then_inc(turned, 1)
                e.wait_ge(oT_ok, 2 * i + 1)
                turn(o[1]).then_inc(turned, 1)
                e.wait_ge(done, i + 1)
                for j in range(2):
                    e.wait_ge(oT_ok, 2 * i + j + 1)
                    for a in range(BT):
                        for c in range(CH):
                            r = e.matmul(pP[:, j, a, :], oT[j][:, c, a * P:(a + 1) * P], wo[j][:, c, :],
                                         start=(c == 0), stop=(c == CH - 1))
                    r.then_inc(proj, 1)
                e.wait_ge(nx_ok, i + 1)
                turn(nx).then_inc(turned, 1)
                e.wait_ge(nxT_ok, i + 2)
                for a in range(BT):
                    for c in range(CH):
                        r = e.matmul(pL[:, a, :], nxT[:, c, a * P:(a + 1) * P], wr[:, c, :],
                                     start=(c == 0), stop=(c == CH - 1))
                r.then_inc(logit, 1)

        @b.scalar
        def _(e):
            with e.Fori(0, BLOCKS) as i:
                for j in range(2):
                    e.wait_ge(turned, 3 * i + j + 1 + 3)
                    for c in range(CH):
                        r = e.activation(oT[j][:, c, :], pT[:, c, :], ACT.Copy)
                    r.then_inc(oT_ok, 1)
                e.wait_ge(x2_ok, i + 1)
                for a in range(BT):
                    e.activation(sq[:], xn[:, a, :], ACT.Square, accum_out=ms[:, a:a + 1]).then_inc(sq_ok, 1)
                    e.wait_ge(sq_ok, BT * i + a + 1)
                e.wait_ge(var_ok, i + 1)
                e.activation(sd[:], vs[:], ACT.Sqrt).then_inc(root_ok, 1)
                gate.scalar(e, i, True)

        @b.vector
        def _(e):
            e.wait_ge(loaded, 16 * NW)
            e.sem_inc(done, 1)
            e.sem_inc(nxT_ok, 1)
            with e.Fori(0, BLOCKS) as i:
                d = Tally(e, dve, i, 3 + Gate.STEPS)
                e.wait_ge(x_in, 32 * i + 32)
                for a in range(BT):
                    r = e.tensor_tensor(x[:, a, :], x[:, a, :], bo[:], ALU.add)
                r.then_inc(dve, 1)
                d.step()
                e.wait_ge(proj, 2 * i + 1)
                d.wait()
                e.tensor_tensor(x[:], x[:], pP[:, 0], ALU.add).then_inc(dve, 1)
                d.step()
                e.wait_ge(proj, 2 * i + 2)
                e.tensor_tensor(xn[:], xn[:], pP[:, 1], ALU.add).then_inc(x2_ok, 1)
                e.wait_ge(x2_ok, i + 1)
                d.wait()
                e.tensor_tensor(acc[:, bass.ds(i * BT, BT), :], x[:], xn[:], ALU.add)
                e.wait_ge(sq_ok, BT * i + BT)
                e.tensor_scalar(vs[:], ms[:], 1.0 / DIM, 1e-6, ALU.mult, ALU.add).then_inc(var_ok, 1)
                e.wait_ge(root_ok, i + 1)
                e.reciprocal(rs[:], sd[:]).then_inc(dve, 1)
                d.step()
                d.wait()
                for a in range(BT):
                    r = e.tensor_scalar(nx[:, a, :], xn[:, a, :], rs[:, a:a + 1], None, ALU.mult)
                r.then_inc(nx_ok, 1)
                e.wait_ge(nx_ok, i + 1)
                e.sem_inc(done, 1)
                e.wait_ge(xT_ok, i + 1)
                e.wait_ge(turned, 3 * i + 6)
                for c in range(CH):
                    r = e.tensor_scalar(nxT[:, c, :], pT[:, c, :], g2[:, c:c + 1], None, ALU.mult)
                r.then_inc(nxT_ok, 1)
                e.wait_ge(logit, i + 1)
                gate.vector(e, i, d, passed, pL[:], comb[:, bass.ds(i * BT, BT), 1:1 + EXPERTS], True)
                d.close()

        @b.gpsimd
        def _(e):
            e.memset(comb[:, :, 0:1], 1.0)
            e.sem_inc(xT_ok, 1)
            with e.Fori(0, BLOCKS) as i:
                e.wait_ge(nxT_ok, i + 2)
                split_xT(e, i, nxT, xT, xT_hi, xT_ok, passed)


def experts(nc, I, name, acc, xT, comb, count, ff, swiglu, first, out=None):
    with Stage(nc, name) as s:
        FC = ff // P
        SIDES = 2 if swiglu else 1
        RH = 2 if swiglu else 4
        raw1 = s.sb("raw1", [P, SIDES, CH, ff])
        raw2 = s.sb("raw2", [P, FC, DIM])
        w1 = s.sb("w1", [P, 2, SIDES, CH, ff], F32R)
        w2 = s.sb("w2", [P, 2, FC, DIM], F32R)
        b1 = None if swiglu else s.sb("b1", [P, FC])
        sg = s.sb("sg", [P, 2, BLK]) if swiglu else None
        h32 = s.sb("h32", [P, 2, BLK])
        h = s.sb("h", [P, 2, 2, FC, BLK], F32R)
        pH = s.ps("pH", [P, RH, SIDES, BLK])
        pY = s.ps("pY", [P, 2, BT, DIM])
        w1_in, w2_in = s.sem("w1_in"), s.sem("w2_in")
        w_hi = s.sem("w_hi")
        w_ok = s.sem("w_ok")
        b1_in = s.sem("b1_in")
        hid = s.sem("hid")
        sg_ok = s.sem("sg_ok")
        h_hi = s.sem("h_hi")
        h_ok = s.sem("h_ok")
        y_ok = s.sem("y_ok")
        added = s.sem("added")
        stored = s.sem("stored")
        b = s.block()
        ROUNDS_T = BLOCKS // 2

        def unit(x, r, k):
            return (x * ROUNDS_T + r) * 2 + k

        @b.sync
        def _(e):
            with e.Fori(0, count) as x:
                if b1 is not None:
                    e.wait_ge(h_hi, x * (BLOCKS * FC) + RH)
                    e.dma_start(b1[:], I["b1"][:, bass.ds(x, 1), :].rearrange("p x f -> p (x f)")).then_inc(b1_in, 16)
                e.wait_ge(w_ok, 2 * x + 1)
                for side, wname in enumerate(("w1", "w3")[:SIDES]):
                    e.dma_start(raw1[:, side], I[f"{name}_{wname}"].rearrange("(x c p) f -> p x c f", c=CH, p=P)
                                [:, bass.ds(x, 1), :, :].rearrange("p x c f -> p (x c) f")).then_inc(w1_in, 16)
                e.wait_ge(w_ok, 2 * x + 2)
                e.dma_start(raw2[:], I[f"{name}_w2"].rearrange("(x c p) d -> p x c d", c=FC, p=P)
                            [:, bass.ds(x, 1), :, :].rearrange("p x c d -> p (x c) d")).then_inc(w2_in, 16)
            if out is not None:
                e.wait_ge(added, count * BLOCKS + 2)
                e.dma_start(out.rearrange("(t p) d -> p t d", p=P), acc[:]).then_inc(stored, 16)
                e.wait_ge(stored, 16)

        @b.tensor
        def _(e):
            e.sem_inc(hid, 1)
            e.sem_inc(y_ok, 2)

            def hidden(x, r, k, phase):
                n = unit(x, r, k)
                if phase == "open" and k == 0:
                    e.wait_ge(w_ok, 2 * x + 1 + 2)
                for f in range(FC):
                    e.wait_ge(h_hi, n * FC + f + 1)
                    for side in range(SIDES):
                        for j, (pw, px) in enumerate(PRODUCTS):
                            for c in range(CH):
                                m = e.matmul(pH[:, (k * FC + f) % RH, side, :], w1[:, pw, side, c, f * P:(f + 1) * P],
                                             xT[:, px, c, bass.ds((r * 2 + k) * BLK, BLK)],
                                             start=(j == 0 and c == 0), stop=(j == len(PRODUCTS) - 1 and c == CH - 1))
                    m.then_inc(hid, 1)

            def output(x, r, k, phase):
                n = unit(x, r, k)
                if phase == "open" and k == 0:
                    e.wait_ge(w_ok, 2 * x + 2 + 2)
                e.wait_ge(added, n + 1)
                e.wait_ge(h_ok, n * FC + FC + 2)
                for a in range(BT):
                    for f in range(FC):
                        for j, (ph, pw) in enumerate(PRODUCTS):
                            m = e.matmul(pY[:, k, a, :], h[:, k, ph, f, a * P:(a + 1) * P], w2[:, pw, f, :],
                                         start=(f == 0 and j == 0), stop=(f == FC - 1 and j == len(PRODUCTS) - 1))
                m.then_inc(y_ok, 1)

            ticks(e, count, ROUNDS_T, 2, [(0, hidden), (1, output)])

        @b.scalar
        def _(e):
            if not swiglu:
                e.sem_inc(h_hi, RH)

            def weights(x, r, k, phase):
                if phase == "open" and k == 0:
                    e.wait_ge(w1_in, 16 * SIDES * (x + 1))
                    e.wait_ge(hid, x * (BLOCKS * FC) + 1)
                    e.activation(w1[:, HI], raw1[:], ACT.Copy).then_inc(w_hi, 1)
                    e.wait_ge(w2_in, 16 * (x + 1))
                    e.wait_ge(y_ok, x * BLOCKS + 2)
                    e.activation(w2[:, HI], raw2[:], ACT.Copy).then_inc(w_hi, 1)

            def act(x, r, k, phase):
                n = unit(x, r, k)
                if not swiglu:
                    e.wait_ge(y_ok, n + 1)
                    if phase == "open" and k == 0:
                        e.wait_ge(b1_in, 16 * (x + 1))
                for f in range(FC):
                    e.wait_ge(hid, n * FC + f + 1 + 1)
                    if swiglu:
                        e.wait_ge(h_hi, n * FC + f + 1)
                        e.activation(sg[:, f % 2, :], pH[:, (k * FC + f) % RH, 0, :], ACT.Silu).then_inc(sg_ok, 1)
                    else:
                        e.wait_ge(h_ok, n * FC + f + 1)
                        for dst in (h32[:, f % 2, :], h[:, k, HI, f, :]):
                            m = e.activation(dst, pH[:, (k * FC + f) % RH, 0, :], ACT.Relu, bias=b1[:, f:f + 1])
                        m.then_inc(h_hi, 1)

            ticks(e, count, ROUNDS_T, 2, [(0, weights), (0, act)])

        @b.vector
        def _(e):
            if swiglu:
                e.sem_inc(h_hi, RH)
            e.sem_inc(added, 2)
            e.sem_inc(w_ok, 2)

            def weights(x, r, k, phase):
                if phase == "open" and k == 0:
                    for j, (w, raw) in enumerate(((w1, raw1), (w2, raw2))):
                        e.wait_ge(w_hi, 2 * x + j + 1)
                        e.tensor_tensor(w[:, LO], raw[:], w[:, HI], ALU.subtract).then_inc(w_ok, 1)

            def multiply(x, r, k, phase):
                n = unit(x, r, k)
                e.wait_ge(y_ok, n + 1)
                for f in range(FC):
                    e.wait_ge(sg_ok, n * FC + f + 1)
                    e.wait_ge(h_ok, n * FC + f + 1)
                    for dst in (h32[:, f % 2, :], h[:, k, HI, f, :]):
                        m = e.tensor_tensor(dst, sg[:, f % 2, :], pH[:, (k * FC + f) % RH, 1, :], ALU.mult)
                    m.then_inc(h_hi, 1)

            def add(x, r, k, phase):
                n = unit(x, r, k)
                e.wait_ge(y_ok, n + 1 + 2)
                if phase == "open" and k == 0:
                    e.wait_ge(added, x * BLOCKS + 2)
                for a in range(BT):
                    t = (r * 2 + k) * BT + a
                    now = acc[:, bass.ds(t, 1), :].rearrange("p t d -> p (t d)")
                    m = e.scalar_tensor_tensor(now, pY[:, k, a, :], comb[:, bass.ds(t, 1), bass.ds(x + first, 1)]
                                               .rearrange("p t x -> p (t x)"), now, ALU.mult, ALU.add)
                m.then_inc(added, 1)

            ticks(e, count, ROUNDS_T, 2, [(0, weights), (0, multiply), (1, add)] if swiglu else [(0, weights), (1, add)])

        @b.gpsimd
        def _(e):
            e.sem_inc(h_ok, 2)

            def rest(x, r, k, phase):
                for f in range(FC):
                    m = unit(x, r, k) * FC + f
                    e.wait_ge(h_hi, m + 1 + RH)
                    e.tensor_tensor(h[:, k, LO, f, :], h32[:, f % 2, :], h[:, k, HI, f, :], ALU.subtract).then_inc(h_ok, 1)

            ticks(e, count, ROUNDS_T, 2, [(0, rest)])


def project1(nc, I, scr, ident, acc, xT, comb):
    with Stage(nc, "p1") as s:
        wq = s.sb("wq", [P, CH, DIM])
        wk = s.sb("wk", [P, CH, DIM])
        wv = s.sb("wv", [P, CH, DIM])
        wg = s.sb("wg", [P, CH, EXPERTS])
        b2 = s.sb("b2", [EXPERTS, DIM])
        wm, wsum = s.sb("wm", [P, CH]), s.sb("wsum", [P, CH])
        xn = s.sb("xn", [P, BT, DIM])
        st, mv = s.sb("st", [P, BT, 6]), s.sb("mv", [P, BT, 2])
        vs, sd, rs = (s.sb(n, [P, BT]) for n in ("vs", "sd", "rs"))
        xnT = s.sb("xnT", [P, CH, BLK])
        qk = s.sb("qk", [P, 2 * CH, BLK])
        v = s.sb("v", [P, BT, DIM])
        cb = s.sb("cb", [P, BT, EXPERTS])
        cT = s.sb("cT", [EXPERTS, BLK])
        pT = s.ps("pT", [P, CH, BLK])
        pP = s.ps("pP", [P, 2 * CH, BLK])
        pV = s.ps("pV", [P, BT, DIM])
        loaded = s.sem("loaded")
        w_ok = s.sem("w_ok")
        var_ok, root_ok = s.sem("var_ok"), s.sem("root_ok")
        xn_ok = s.sem("xn_ok")
        turned = s.sem("turned")
        xnT_ok = s.sem("xnT_ok")
        xT_hi = s.sem("xT_hi")
        xT_ok = s.sem("xT_ok")
        logit = s.sem("logit")
        proj = s.sem("proj")
        qk_ok = s.sem("qk_ok")
        v_ps = s.sem("v_ps")
        v_ok = s.sem("v_ok")
        cb_ok = s.sem("cb_ok")
        cb_T = s.sem("cb_T")
        cT_ok = s.sem("cT_ok")
        stored = s.sem("stored")
        dve = s.sem("dve")
        passed = s.sem("passed")
        gate = Gate(s, I["gate_b"])
        NW, NST = 7, 3
        b = s.block()

        @b.sync
        def _(e):
            for dst, src in ((wq[:], chunked(I["l1wq"])), (wk[:], chunked(I["l1wk"])), (wv[:], chunked(I["l1wvT"])),
                             (wg[:], chunked(I["gate_w"])), (b2[:], I["b2"]),
                             (gate.bias[:], I["gate_b"].partition_broadcast(P)),
                             (gate.iota[:], I["iota"].partition_broadcast(P))):
                e.dma_start(dst, src).then_inc(loaded, 16)
            e.sem_inc(stored, 16)
            with e.Fori(0, BLOCKS) as i:
                now = bass.ds(i * BLK, BLK)
                e.wait_ge(v_ok, 2 * i + 3)
                e.dma_start(tiled(scr["v1"], i), v[:]).then_inc(stored, 16)
                e.wait_ge(qk_ok, 4 * i + 8)
                e.dma_start(chunked(scr["q1T"])[:, :, now], qk[:, 0:CH, :]).then_inc(stored, 16)
                e.dma_start(chunked(scr["k1T"])[:, :, now], qk[:, CH:, :]).then_inc(stored, 16)
            e.wait_ge(stored, 16 * NST * BLOCKS + 16)

        @b.tensor
        def _(e):
            e.wait_ge(loaded, 16 * NW)
            e.wait_ge(w_ok, 2 * CH + 4)
            e.sem_inc(turned, 1)
            with e.Fori(0, BLOCKS) as i:
                e.wait_ge(xn_ok, i + 1)
                e.wait_ge(cT_ok, i + 1)
                for c in range(CH):
                    for a in range(BT):
                        r = e.transpose(pT[:, c, a * P:(a + 1) * P], xn[:, a, c * P:(c + 1) * P], ident[:])
                r.then_inc(turned, 1)
                e.wait_ge(xnT_ok, i + 1)
                for a in range(BT):
                    for c in range(CH):
                        r = e.matmul(pT[:, 0, a * EXPERTS:(a + 1) * EXPERTS], xnT[:, c, a * P:(a + 1) * P],
                                     wg[:, c, :], start=(c == 0), stop=(c == CH - 1))
                r.then_inc(logit, 1)
                e.wait_ge(v_ok, 2 * i + 2)
                for a in range(BT):
                    for c in range(CH):
                        r = e.matmul(pV[:, a, :], xnT[:, c, a * P:(a + 1) * P], wv[:, c, :],
                                     start=(c == 0), stop=(c == CH - 1))
                r.then_inc(v_ps, 1)
                k = 0
                for w in (wq, wk):
                    for m in range(CH):
                        e.wait_ge(qk_ok, 4 * i + k + 1)
                        for c in range(CH):
                            r = e.matmul(pP[:, k, :], w[:, c, m * P:(m + 1) * P], xnT[:, c, :],
                                         start=(c == 0), stop=(c == CH - 1))
                        r.then_inc(proj, 1)
                        k += 1
                e.wait_ge(cb_ok, i + 1)
                for a in range(BT):
                    r = e.transpose(pT[0:EXPERTS, 1, a * P:(a + 1) * P], cb[:, a, :], ident[:])
                r.then_inc(cb_T, 1)
                e.wait_ge(v_ok, 2 * i + 3)
                e.wait_ge(cT_ok, i + 2)
                for a in range(BT):
                    r = e.matmul(pV[:, a, :], cT[:, a * P:(a + 1) * P], b2[:], start=True, stop=True)
                r.then_inc(v_ps, 1)

        @b.scalar
        def _(e):
            e.sem_inc(qk_ok, 4)
            e.sem_inc(cT_ok, 1)
            e.wait_ge(w_ok, CH + 1)
            for c in range(CH):
                e.activation(wv[:, c, :], wv[:, c, :], ACT.Exp, bias=wm[:, c:c + 1],
                             accum_out=wsum[:, c:c + 1]).then_inc(w_ok, 1)
                e.wait_ge(w_ok, CH + 1 + c + 1)
            with e.Fori(0, BLOCKS) as i:
                e.wait_ge(var_ok, i + 1)
                e.activation(sd[:], vs[:], ACT.Sqrt).then_inc(root_ok, 1)
                e.wait_ge(turned, i + 2)
                e.wait_ge(xT_ok, i + 1)
                for c in range(CH):
                    r = e.activation(xnT[:, c, :], pT[:, c, :], ACT.Copy)
                r.then_inc(xnT_ok, 1)
                gate.scalar(e, i, False)
                e.wait_ge(stored, 16 * NST * i + 16)
                for k in range(2 * CH):
                    e.wait_ge(proj, 2 * CH * i + k + 1)
                    e.activation(qk[:, k, :], pP[:, k, :], ACT.Copy).then_inc(qk_ok, 1)
                e.wait_ge(cb_T, i + 1)
                e.activation(cT[:], pT[0:EXPERTS, 1, :], ACT.Copy).then_inc(cT_ok, 1)

        @b.vector
        def _(e):
            e.wait_ge(loaded, 16 * NW)
            e.sem_inc(v_ok, 2)
            for c in range(CH):
                e.reduce_max(wm[:, c:c + 1], wv[:, c, :], AX_X).then_inc(w_ok, 1)
            e.wait_ge(w_ok, CH)
            e.tensor_scalar(wm[:], wm[:], -1.0, None, ALU.mult).then_inc(w_ok, 1)
            e.wait_ge(w_ok, 2 * CH + 1)
            e.reciprocal(wsum[:], wsum[:]).then_inc(w_ok, 1)
            e.wait_ge(w_ok, 2 * CH + 2)
            for c in range(CH):
                e.tensor_scalar(wv[:, c, :], wv[:, c, :], wsum[:, c:c + 1], 1.0 / DIM, ALU.mult,
                                ALU.mult).then_inc(w_ok, 1)
            with e.Fori(0, BLOCKS) as i:
                d = Tally(e, dve, i, 2 * BT + 1 + Gate.STEPS)
                now = acc[:, bass.ds(i * BT, BT), :]
                one = [acc[:, bass.ds(i * BT + a, 1), :].rearrange("p t d -> p (t d)") for a in range(BT)]
                for a in range(BT):
                    e.bn_stats(st[:, a, :], one[a]).then_inc(dve, 1)
                    d.step()
                d.wait()
                e.sem_inc(passed, 1)
                for a in range(BT):
                    e.bn_aggr(mv[:, a, :], st[:, a, :]).then_inc(dve, 1)
                    d.step()
                d.wait()
                e.tensor_scalar(vs[:], mv[:, :, 1], 1e-5, None, ALU.add).then_inc(var_ok, 1)
                e.wait_ge(root_ok, i + 1)
                e.reciprocal(rs[:], sd[:]).then_inc(dve, 1)
                d.step()
                e.wait_ge(turned, i + 1)
                d.wait()
                for a in range(BT):
                    r = e.tensor_scalar(xn[:, a, :], one[a], mv[:, a, 0:1], rs[:, a:a + 1], ALU.subtract, ALU.mult)
                r.then_inc(xn_ok, 1)
                e.wait_ge(stored, 16 * NST * i + 16)
                e.wait_ge(v_ps, 2 * i + 1)
                e.tensor_copy(v[:], pV[:])
                e.tensor_tensor(now, now, pV[:], ALU.subtract).then_inc(v_ok, 1)
                e.wait_ge(logit, i + 1)
                gate.vector(e, i, d, passed, pT[:, 0, 0:BT * EXPERTS].rearrange("p (a x) -> p a x", a=BT), cb[:], False)
                e.tensor_copy(comb[:, bass.ds(i * BT, BT), 1:1 + EXPERTS], cb[:]).then_inc(cb_ok, 1)
                e.wait_ge(v_ps, 2 * i + 2)
                e.wait_ge(v_ok, 2 * i + 3)
                e.tensor_tensor(now, now, pV[:], ALU.add).then_inc(v_ok, 1)
                d.close()

        @b.gpsimd
        def _(e):
            e.sem_inc(xT_ok, 1)
            with e.Fori(0, BLOCKS) as i:
                e.wait_ge(xnT_ok, i + 1)
                split_xT(e, i, xnT, xT, xT_hi, xT_ok, passed)


def attend1(nc, scr, acc):
    with Stage(nc, "a1") as s:
        qT, kT = s.sb("qT", [P, CH, SEQ]), s.sb("kT", [P, CH, SEQ])
        v, vn = s.sb("v", [P, QT, DIM]), s.sb("vn", [P, QT, DIM])
        w = s.sb("w", [P, QT, SEQ])
        top, negm, sums, rsum = (s.sb(n, [P, QT]) for n in ("top", "negm", "sums", "rsum"))
        pS = s.ps("pS", [P, 2, SEQ])
        pO = s.ps("pO", [P, 4, BANK])
        qk_in, v_in = s.sem("qk_in"), s.sem("v_in")
        scored = s.sem("scored")
        max_ok = s.sem("max_ok")
        neg_ok = s.sem("neg_ok")
        exped = s.sem("exped")
        inv_ok = s.sem("inv_ok")
        vn_ok = s.sem("vn_ok")
        av = s.sem("av")
        added = s.sem("added")
        SCALE = SEQ ** -0.5
        b = s.block()

        @b.sync
        def _(e):
            with e.Fori(0, BATCH) as i:
                now = bass.ds(i * SEQ, SEQ)
                e.wait_ge(scored, QT * i + 1)
                e.dma_start(kT[:], chunked(scr["k1T"])[:, :, now]).then_inc(qk_in, 16)
                e.dma_start(qT[:], chunked(scr["q1T"])[:, :, now]).then_inc(qk_in, 16)
                e.wait_ge(av, QT * i + 1)
                e.dma_start(v[:], tiled(scr["v1"], i, QT)).then_inc(v_in, 16)

        @b.tensor
        def _(e):
            e.sem_inc(scored, 1)
            e.sem_inc(av, 1)
            with e.Fori(0, BATCH) as i:
                e.wait_ge(qk_in, 32 * i + 32)
                for m in range(QT):
                    e.wait_ge(exped, QT * i + m + 1)
                    for half in range(2):
                        for c in range(CH):
                            r = e.matmul(pS[:, m % 2, half * BANK:(half + 1) * BANK], kT[:, c, m * P:(m + 1) * P],
                                         qT[:, c, half * BANK:(half + 1) * BANK], start=(c == 0), stop=(c == CH - 1))
                    r.then_inc(scored, 1)
                for n in range(QT):
                    e.wait_ge(added, QT * i + n + 1)
                    for m in range(QT):
                        if n == 0:
                            e.wait_ge(vn_ok, QT * i + m + 1)
                        r = e.matmul(pO[:, n % 4, 0:DIM], w[:, m, n * P:(n + 1) * P], vn[:, m, :],
                                     start=(m == 0), stop=(m == QT - 1))
                    r.then_inc(av, 1)

        @b.scalar
        def _(e):
            e.sem_inc(exped, 2)
            with e.Fori(0, BATCH) as i:
                for m in range(QT):
                    e.wait_ge(neg_ok, QT * i + m + 1)
                    if m == 0:
                        e.wait_ge(av, QT * i + 1)
                    e.activation(w[:, m, :], pS[:, m % 2, :], ACT.Exp, bias=negm[:, m:m + 1], scale=SCALE,
                                 accum_out=sums[:, m:m + 1]).then_inc(exped, 1)

        @b.vector
        def _(e):
            e.sem_inc(added, 4)
            with e.Fori(0, BATCH) as i:
                def divide(m):
                    n = QT * i + m
                    e.wait_ge(exped, n + 1 + 2)
                    e.reciprocal(rsum[:, m:m + 1], sums[:, m:m + 1]).then_inc(inv_ok, 1)
                    if m == 0:
                        e.wait_ge(v_in, 16 * i + 16)
                        e.wait_ge(av, QT * i + 1)
                    e.wait_ge(inv_ok, n + 1)
                    e.tensor_scalar(vn[:, m, :], v[:, m, :], rsum[:, m:m + 1], None, ALU.mult).then_inc(vn_ok, 1)

                for m in range(QT):
                    n = QT * i + m
                    e.wait_ge(scored, n + 1 + 1)
                    e.reduce_max(top[:, m:m + 1], pS[:, m % 2, :], AX_X).then_inc(max_ok, 1)
                    e.wait_ge(max_ok, n + 1)
                    e.tensor_scalar(negm[:, m:m + 1], top[:, m:m + 1], -SCALE, None, ALU.mult).then_inc(neg_ok, 1)
                    if m:
                        divide(m - 1)
                divide(QT - 1)
                for n in range(QT):
                    e.wait_ge(av, QT * i + n + 1 + 1)
                    now = acc[:, bass.ds(i * QT + n, 1), :].rearrange("p t d -> p (t d)")
                    e.tensor_tensor(now, now, pO[:, n % 4, 0:DIM], ALU.add).then_inc(added, 1)


def build(nc, I, out, upto=99, dbg=None):
    kind = "ExternalOutput" if dbg else "Internal"
    def dram(name, shape):
        return nc.dram_tensor(f"scr_{name}", shape, BF16 if len(shape) == 3 else F32, kind=kind).ap()
    scr = {n: dram(n, sh) for n, sh in (
        ("xn", (TOK, DIM)), ("qP", (PARTS, DIM, TOK)), ("kP", (PARTS, DIM, TOK)), ("v", (TOK, DIM)), ("q2T", (DIM, TOK)),
        ("kcT", (P, TOK)), ("vc", (TOK, HD1)), ("o0", (TOK, DIM)), ("o1", (TOK, DIM)),
        ("q1T", (DIM, TOK)), ("k1T", (DIM, TOK)), ("v1", (TOK, DIM)))}
    with ExitStack() as ctx:
        ident = ctx.enter_context(nc.sbuf_tensor("ident", [P, P], F32))
        project0(nc, I, scr, ident)
        attend(nc, scr, ident)
        acc = ctx.enter_context(nc.sbuf_tensor("acc", [P, TILES, DIM], F32))
        xT = ctx.enter_context(nc.sbuf_tensor("xT", [P, 2, CH, TOK], F32R))
        comb = ctx.enter_context(nc.sbuf_tensor("comb", [P, TILES, 1 + EXPERTS], F32))
        route0(nc, I, scr, ident, acc, xT, comb)
        experts(nc, I, "e0", acc, xT, comb, 1 + EXPERTS, FF0, True, 0)
        project1(nc, I, scr, ident, acc, xT, comb)
        attend1(nc, scr, acc)
        experts(nc, I, "e1", acc, xT, comb, EXPERTS, FF1, False, 1, out)


def columns(a):
    return a.reshape(-1, P).T


def kernel(**inputs):
    import numpy as np
    import concourse.bacc as bacc
    from concourse.bass_utils import run_bass_kernel_spmd as run

    a = {k: np.asarray(v) for k, v in inputs.items()}
    L0, F0, L1, F1 = "L0_attn_", "L0_ffn_", "L1_attn_", "L1_ffn_"
    arrays = {
        "x": a[L0 + "x"].reshape(TOK, DIM),
        "wq": a[L0 + "Wq"], "wk": a[L0 + "Wk"], "wv": a[L0 + "Wv"],
        "bq": columns(a[L0 + "bq"]), "bk": columns(a[L0 + "bk"]),
        "bv": a[L0 + "bv"], "wo": a[L0 + "Wo"], "bo": a[L0 + "bo"],
        "g1": columns(a[F0 + "g1"]), "g2": columns(a[F0 + "g2"]),
        "wq2": a[F0 + "Wq"].T, "wkc": np.concatenate([a[F0 + "Wkc"].T] * 2, axis=1), "wvc": a[F0 + "Wvc"].T,
        "wo2": a[F0 + "Wo"].T, "wr": a[F0 + "Wr"].T, "ebias": a[F0 + "expert_bias"],
        "e0_w1": np.concatenate([a[F0 + "sW1"].T[None], a[F0 + "eW1"].transpose(0, 2, 1)]).reshape(-1, FF0),
        "e0_w3": np.concatenate([a[F0 + "sW3"].T[None], a[F0 + "eW3"].transpose(0, 2, 1)]).reshape(-1, FF0),
        "e0_w2": np.concatenate([a[F0 + "sW2"].T[None], a[F0 + "eW2"].transpose(0, 2, 1)]).reshape(-1, DIM),
        "l1wq": a[L1 + "wq"], "l1wk": a[L1 + "wk"], "l1wvT": a[L1 + "wv"].T,
        "gate_w": a[F1 + "gate_w"], "gate_b": a[F1 + "gate_b"],
        "e1_w1": a[F1 + "w1"].reshape(-1, FF1), "e1_w2": a[F1 + "w2"].reshape(-1, DIM),
        "b1": a[F1 + "b1"].reshape(EXPERTS, FF1 // P, P).transpose(2, 0, 1), "b2": a[F1 + "b2"],
        "ident": np.eye(P, dtype=np.float32), "iota": np.arange(EXPERTS, dtype=np.float32),
    }
    arrays = {f"in_{k}": np.ascontiguousarray(v) for k, v in arrays.items()}
    nc = bacc.Bacc("TRN2", target_bir_lowering=False, num_devices=1)
    I = {k[3:]: nc.dram_tensor(k, v.shape, mybir.dt.from_np(v.dtype), kind="ExternalInput").ap()
         for k, v in arrays.items()}
    out = nc.dram_tensor("out", (TOK, DIM), F32, kind="ExternalOutput").ap()
    build(nc, I, out)
    r = run(nc, [arrays], core_ids=[0])
    return r.results[0]["out"].reshape(BATCH, SEQ, DIM)
```

```python
from contextlib import ExitStack

import concourse.bass as bass
from concourse import mybir

F32 = mybir.dt.float32
BF16 = mybir.dt.bfloat16
F32R = mybir.dt.float32r
U32 = mybir.dt.uint32
ALU = mybir.AluOpType
ACT = mybir.ActivationFunctionType
AX_X = mybir.AxisListType.X

P = 128
BATCH, SEQ, DIM = 4, 1024, 256
TOK = BATCH * SEQ
TILES = TOK // P
CH = DIM // P
BLK = 512
BT = BLK // P
BLOCKS = TOK // BLK
BANK = 512
HEADS0, HD0 = 16, 16
GROUP = 4
GROUPS = HEADS0 // GROUP
TOPK = 16
PARTS = 3
HI, LO = 0, 1
PRODUCTS = ((HI, HI), (HI, LO), (LO, HI))
HEADS1, HD1 = 4, 64
EXPERTS = 8
FF0, FF1 = 256, 512
NEG = -3.0e38
QT = SEQ // P
ROUNDS = QT // 2


class Stage:

    def __init__(self, nc, name):
        self.nc, self.name, self.ctx = nc, name, ExitStack()

    def __enter__(self):
        self.ctx.__enter__()
        return self

    def __exit__(self, *e):
        return self.ctx.__exit__(*e)

    def sb(self, name, shape, dt=F32):
        return self.ctx.enter_context(self.nc.sbuf_tensor(f"{self.name}_{name}", shape, dt))

    def ps(self, name, shape):
        return self.ctx.enter_context(self.nc.psum_tensor(f"{self.name}_{name}", shape, F32))

    def sem(self, name):
        return self.ctx.enter_context(self.nc.semaphore(f"{self.name}_{name}"))

    def block(self):
        return self.ctx.enter_context(self.nc.Block())


def tiled(ap, i, n=BT):
    return ap.rearrange("(t p) d -> p t d", p=P)[:, bass.ds(i * n, n), :]


def chunked(ap, c=CH):
    return ap.rearrange("(c p) n -> p c n", p=P)


def ticks(e, outer, rounds, units, steps):
    drain = max(lag for lag, _ in steps)
    assert drain <= units
    with e.Fori(0, outer) as b:
        for k in range(units):
            for lag, step in steps:
                if k >= lag:
                    step(b, 0, k - lag, "open")
        with e.Fori(1, rounds) as r:
            for k in range(units):
                for lag, step in steps:
                    if k >= lag:
                        step(b, r, k - lag, "loop")
                    else:
                        step(b, r - 1, k - lag + units, "loop")
        for k in range(drain):
            for lag, step in steps:
                if k < lag:
                    step(b, rounds - 1, units + k - lag, "drain")


def long_ticks(e, outer, rounds, units, steps):
    drain = max(lag for lag, _ in steps)
    assert drain <= units

    def loop(b):
        with e.Fori(1, rounds) as r:
            for k in range(units):
                for lag, step in steps:
                    if k >= lag:
                        step(b, r, k - lag, "loop")
                    else:
                        step(b, r - 1, k - lag + units, "loop")

    for k in range(units):
        for lag, step in steps:
            if k >= lag:
                step(0, 0, k - lag, "first")
    with e.Fori(0, outer - 1) as b:
        loop(b)
        for k in range(units):
            for lag, step in steps:
                if k >= lag:
                    step(b + 1, 0, k - lag, "open")
                else:
                    step(b, rounds - 1, k - lag + units, "loop")
    loop(outer - 1)
    for k in range(drain):
        for lag, step in steps:
            if k < lag:
                step(outer - 1, rounds - 1, units + k - lag, "drain")


def one_ahead(e, ahead, rest):
    ahead(0)
    with e.Fori(0, BLOCKS - 1) as i:
        rest(i, False)
    rest(BLOCKS - 1, True)


class Tally:

    def __init__(self, eng, sem, round_, per):
        self.eng, self.sem, self.base, self.per, self.n = eng, sem, round_ * per, per, 0

    def step(self, k=1):
        self.n += k

    def wait(self):
        self.eng.wait_ge(self.sem, self.base + self.n)

    def close(self):
        assert self.n == self.per, (self.n, self.per)


def project0(nc, I, scr, ident):
    with Stage(nc, "pj") as s:
        wq = s.sb("wq", [P, CH, DIM])
        wk = s.sb("wk", [P, CH, DIM])
        wv = s.sb("wv", [P, CH, DIM])
        wq2 = s.sb("wq2", [P, CH, DIM])
        wkc = s.sb("wkc", [P, CH, P])
        wvc = s.sb("wvc", [P, CH, HD1])
        bq = s.sb("bq", [P, CH])
        bqs = s.sb("bqs", [P, CH])
        bk = s.sb("bk", [P, CH])
        bv = s.sb("bv", [P, DIM])
        g1 = s.sb("g1", [P, CH])
        x = s.sb("x", [P, BT, DIM])
        xn = s.sb("xn", [P, BT, DIM])
        nx = s.sb("nx", [P, BT, DIM])
        sq = s.sb("sq", [P, DIM])
        st = s.sb("st", [P, BT, 6])
        mv = s.sb("mv", [P, BT, 2])
        vs = s.sb("vs", [P, BT])
        ms = s.sb("ms", [P, BT])
        sd = s.sb("sd", [P, BT])
        rs = s.sb("rs", [P, BT])
        xnT = s.sb("xnT", [P, CH, BLK])
        nxT = s.sb("nxT", [P, CH, BLK])
        qT = s.sb("qT", [P, CH, BLK])
        kT = s.sb("kT", [P, CH, BLK])
        qP = s.sb("qP", [P, PARTS, CH, BLK], BF16)
        kP = s.sb("kP", [P, PARTS, CH, BLK], BF16)
        v = s.sb("v", [P, BT, DIM])
        q2T = s.sb("q2T", [P, CH, BLK])
        kcT = s.sb("kcT", [P, BLK])
        vc = s.sb("vc", [P, BT, HD1])
        pT = s.ps("pT", [P, CH, BLK])
        pP = s.ps("pP", [P, 4, BLK])
        pV = s.ps("pV", [P, BT, DIM])

        loaded = s.sem("loaded")
        x_in = s.sem("x_in")
        xn_ok = s.sem("xn_ok")
        nx_ok = s.sem("nx_ok")
        dve = s.sem("dve")
        var_ok = s.sem("var_ok")
        root_ok = s.sem("root_ok")
        sq_ok = s.sem("sq_ok")
        turned = s.sem("turned")
        xnT_ok = s.sem("xnT_ok")
        nxT_ok = s.sem("nxT_ok")
        proj = s.sem("proj")
        proj_out = s.sem("proj_out")
        q_split = s.sem("q_split")
        k_split = s.sem("k_split")
        pv_ok = s.sem("pv_ok")
        pv_out = s.sem("pv_out")
        stored = s.sem("stored")
        xn_stored = s.sem("xn_stored")
        passed = s.sem("passed")
        NW, NP = 11, 3 * CH + 1
        NST = 4 + 2 * PARTS
        b = s.block()

        @b.sync
        def _(e):
            for dst, src in ((wq[:], chunked(I["wq"])), (wk[:], chunked(I["wk"])), (wv[:], chunked(I["wv"])),
                             (wq2[:], chunked(I["wq2"])), (wkc[:], chunked(I["wkc"])), (wvc[:], chunked(I["wvc"])),
                             (bq[:], I["bq"]), (bk[:], I["bk"]), (bv[:], I["bv"].partition_broadcast(P)),
                             (g1[:], I["g1"]), (ident[:], I["ident"])):
                e.dma_start(dst, src).then_inc(loaded, 16)
            e.sem_inc(stored, 16)
            with e.Fori(0, BLOCKS) as i:
                now = bass.ds(i * BLK, BLK)
                e.wait_ge(pv_out, 2 * i + 2)
                e.dma_start(tiled(scr["v"], i), v[:]).then_inc(stored, 16)
                for t, name, split in ((qP, "qP", q_split), (kP, "kP", k_split)):
                    e.wait_ge(split, 4 * i + 4 + 4)
                    for p in range(PARTS):
                        e.dma_start(chunked(scr[name][p])[:, :, now], t[:, p]).then_inc(stored, 16)
                e.wait_ge(proj_out, NP * i + NP + 4)
                e.sem_inc(passed, 1)
                e.dma_start(chunked(scr["q2T"])[:, :, now], q2T[:]).then_inc(stored, 16)
                e.dma_start(scr["kcT"][:, now], kcT[:]).then_inc(stored, 16)
                e.wait_ge(pv_out, 2 * i + 3)
                e.dma_start(tiled(scr["vc"], i), vc[:]).then_inc(stored, 16)

            e.wait_ge(stored, 16 * NST * BLOCKS + 16)

        def split(e, i, t, parts, done):
            e.tensor_copy(parts[:, 0], t[:]).then_inc(done, 1)
            e.wait_ge(done, 4 * i + 1 + 4)
            e.tensor_tensor(t[:], t[:], parts[:, 0], ALU.subtract).then_inc(done, 1)
            e.wait_ge(done, 4 * i + 2 + 4)
            e.sem_inc(passed, 1)
            e.tensor_copy(parts[:, 1], t[:]).then_inc(done, 1)
            e.wait_ge(done, 4 * i + 3 + 4)
            e.tensor_tensor(parts[:, 2], t[:], parts[:, 1], ALU.subtract).then_inc(done, 1)

        @b.gpsimd
        def _(e):
            e.sem_inc(k_split, 4)
            with e.Fori(0, BLOCKS) as i:
                e.wait_ge(stored, 16 * NST * i + 16)
                e.wait_ge(proj_out, NP * i + 2 * CH + 4)
                e.sem_inc(passed, 1)
                split(e, i, kT, kP, k_split)

        @b.vector
        def _(e):
            e.wait_ge(loaded, 16 * NW)
            e.sem_inc(xn_ok, 1)
            e.sem_inc(nx_ok, 1)
            e.sem_inc(pv_out, 1)
            e.sem_inc(q_split, 4)

            def layernorm(i):
                d = Tally(e, dve, i, 2 * BT + 2)
                e.wait_ge(x_in, 16 * i + 16)
                for a in range(BT):
                    e.bn_stats(st[:, a, :], x[:, a, :]).then_inc(dve, 1)
                    d.step()
                d.wait()
                e.sem_inc(passed, 1)
                for a in range(BT):
                    e.bn_aggr(mv[:, a, :], st[:, a, :]).then_inc(dve, 1)
                    d.step()
                d.wait()
                e.tensor_scalar(vs[:], mv[:, :, 1], 1e-5, None, ALU.add).then_inc(var_ok, 1)
                e.wait_ge(root_ok, 2 * i + 1)
                e.reciprocal(rs[:], sd[:]).then_inc(dve, 1)
                d.step()
                e.wait_ge(turned, 2 * i + 1)
                e.wait_ge(nx_ok, i + 1)
                e.wait_ge(xn_stored, 16 * i + 16)
                d.wait()
                for a in range(BT):
                    r = e.tensor_scalar(xn[:, a, :], x[:, a, :], mv[:, a, 0:1], rs[:, a:a + 1],
                                        ALU.subtract, ALU.mult)
                r.then_inc(xn_ok, 1)

            def rest(i, last, first=False):
                d = Tally(e, dve, i, 2 * BT + 2)
                d.step(2 * BT + 1)
                e.wait_ge(sq_ok, BT * i + BT)
                e.tensor_scalar(vs[:], ms[:], 1.0 / DIM, 1e-6, ALU.mult, ALU.add).then_inc(var_ok, 1)
                e.wait_ge(root_ok, 2 * i + 2)
                e.reciprocal(rs[:], sd[:]).then_inc(dve, 1)
                d.step()
                e.wait_ge(turned, 2 * i + 2)
                d.wait()
                for a in range(BT):
                    r = e.tensor_scalar(nx[:, a, :], xn[:, a, :], rs[:, a:a + 1], None, ALU.mult)
                r.then_inc(nx_ok, 1)
                if not first:
                    split_q(i - 1)
                e.wait_ge(turned, 2 * i + 4)
                for c in range(CH):
                    r = e.tensor_scalar(nxT[:, c, :], pT[:, c, :], g1[:, c:c + 1], None, ALU.mult)
                r.then_inc(nxT_ok, 1)
                d.close()
                if not last:
                    layernorm(i + 1)
                e.wait_ge(stored, 16 * NST * i + 16)
                e.wait_ge(pv_ok, 2 * i + 1)
                for a in range(BT):
                    r = e.tensor_tensor(v[:, a, :], pV[:, a, :], bv[:], ALU.add)
                r.then_inc(pv_out, 1)
                e.wait_ge(pv_ok, 2 * i + 2)
                e.tensor_copy(vc[:], pV[:, :, 0:HD1]).then_inc(pv_out, 1)

            def split_q(i):
                e.wait_ge(proj_out, NP * i + CH + 4)
                e.wait_ge(stored, 16 * NST * i + 16)
                e.sem_inc(passed, 1)
                split(e, i, qT, qP, q_split)

            layernorm(0)
            rest(0, False, True)
            with e.Fori(1, BLOCKS - 1) as i:
                rest(i, False)
            rest(BLOCKS - 1, True)
            split_q(BLOCKS - 1)

        @b.scalar
        def _(e):
            e.dma_start(x[:], tiled(I["x"], 0)).then_inc(x_in, 16)
            e.sem_inc(xn_stored, 16)
            e.wait_ge(loaded, 16 * NW)
            e.sem_inc(proj_out, 4)
            e.activation(bqs[:], bq[:], ACT.Copy, scale=HD0 ** -0.5)

            def root(i):
                e.wait_ge(var_ok, 2 * i + 1)
                e.activation(sd[:], vs[:], ACT.Sqrt).then_inc(root_ok, 1)

            def rest(i, last):
                e.wait_ge(xn_ok, i + 2)
                e.dma_start(tiled(scr["xn"], i), xn[:]).then_inc(xn_stored, 16)
                if not last:
                    e.dma_start(x[:], tiled(I["x"], i + 1)).then_inc(x_in, 16)
                for a in range(BT):
                    e.activation(sq[:], xn[:, a, :], ACT.Square, accum_out=ms[:, a:a + 1]).then_inc(sq_ok, 1)
                    e.wait_ge(sq_ok, BT * i + a + 1)
                e.wait_ge(var_ok, 2 * i + 2)
                e.activation(sd[:], vs[:], ACT.Sqrt).then_inc(root_ok, 1)
                e.wait_ge(turned, 2 * i + 3)
                for c in range(CH):
                    r = e.activation(xnT[:, c, :], pT[:, c, :], ACT.Copy)
                r.then_inc(xnT_ok, 1)
                if not last:
                    root(i + 1)
                e.wait_ge(stored, 16 * NST * i + 16)
                e.wait_ge(q_split, 4 * i + 4)
                e.wait_ge(k_split, 4 * i + 4)
                k = 0
                for dst, bias, scale in ((qT, bqs, HD0 ** -0.5), (kT, bk, 1.0), (q2T, None, HD1 ** -0.5)):
                    for c in range(CH):
                        k += 1
                        e.wait_ge(proj, NP * i + k)
                        if bias is None:
                            r = e.activation(dst[:, c, :], pP[:, (k - 1) % 4, :], ACT.Copy, scale=scale)
                        else:
                            r = e.activation(dst[:, c, :], pP[:, (k - 1) % 4, :], ACT.Identity,
                                             bias=bias[:, c:c + 1], scale=scale)
                        r.then_inc(proj_out, 1)
                e.wait_ge(proj, NP * i + NP)
                e.activation(kcT[:], pP[:, k % 4, :], ACT.Copy).then_inc(proj_out, 1)

            one_ahead(e, root, rest)
            e.wait_ge(xn_stored, 16 * BLOCKS + 16)

        @b.tensor
        def _(e):
            e.wait_ge(loaded, 16 * NW)
            e.sem_inc(turned, 2)

            def turn(src):
                for c in range(CH):
                    for a in range(BT):
                        r = e.transpose(pT[:, c, a * P:(a + 1) * P], src[:, a, c * P:(c + 1) * P], ident[:])
                return r

            def project(i, k, w, m, srcT):
                e.wait_ge(proj_out, NP * i + k + 1)
                for c in range(CH):
                    r = e.matmul(pP[:, k % 4, :], w[:, c, m * P:(m + 1) * P], srcT[:, c, :],
                                 start=(c == 0), stop=(c == CH - 1))
                r.then_inc(proj, 1)

            with e.Fori(0, BLOCKS) as i:
                e.wait_ge(xn_ok, i + 2)
                turn(xn).then_inc(turned, 1)
                e.wait_ge(xnT_ok, i + 1)
                e.wait_ge(nx_ok, i + 2)
                turn(nx).then_inc(turned, 1)
                for k in range(2 * CH):
                    if k == 0:
                        e.wait_ge(proj_out, NP * i + 4)
                    project(i, k, wq if k < CH else wk, k % CH, xnT)
                e.wait_ge(pv_out, 2 * i + 1)
                for a in range(BT):
                    for c in range(CH):
                        r = e.matmul(pV[:, a, :], xnT[:, c, a * P:(a + 1) * P], wv[:, c, :],
                                     start=(c == 0), stop=(c == CH - 1))
                r.then_inc(pv_ok, 1)
                e.wait_ge(nxT_ok, i + 1)
                for k in range(2 * CH, NP):
                    project(i, k, wq2 if k < 3 * CH else wkc, k % CH if k < 3 * CH else 0, nxT)
                e.wait_ge(pv_out, 2 * i + 2)
                for a in range(BT):
                    for c in range(CH):
                        r = e.matmul(pV[:, a, 0:HD1], nxT[:, c, a * P:(a + 1) * P], wvc[:, c, :],
                                     start=(c == 0), stop=(c == CH - 1))
                r.then_inc(pv_ok, 1)


def attend(nc, scr, ident):
    with Stage(nc, "at") as s:
        BLKU = GROUP + 1
        TU = GROUPS * BLKU
        U = 2 * TU
        BU = QT * TU
        WIDE = P // GROUP
        SLOTS = 2 * PARTS
        KQ = SLOTS * HD0
        R, RT = 5, 10
        Q_PART = (0, 0, 1, 1, 0, 2)
        K_PART = (0, 1, 0, 1, 2, 0)
        q = s.sb("q", [KQ, HEADS0, SEQ], BF16)
        k = s.sb("k", [KQ, HEADS0, SEQ], BF16)
        v = s.sb("v", [P, QT, DIM + HD0])
        q2 = s.sb("q2", [P, HEADS1 // 2, P])
        kc = s.sb("kc", [P, SEQ])
        vc = s.sb("vc", [P, QT, HD1])
        sb = s.sb("sb", [P, R, SEQ])
        cut = s.sb("cut", [P, SEQ])
        w = s.sb("w", [P, R, SEQ])
        wT = s.sb("wT", [P, RT, SEQ])
        m8 = s.sb("m8", [P, R, TOPK])
        negm = s.sb("negm", [P, R])
        sums = s.sb("sums", [P, 2, TU])
        rsum = s.sb("rsum", [P, 2, TU])
        oT = s.sb("oT", [P, 2, BANK])
        o = [s.sb(f"o{j}", [P, 2, DIM]) for j in range(2)]
        pS = s.ps("pS", [P, 2, SEQ])
        pT = s.ps("pT", [P, 2, BANK])
        pO = s.ps("pO", [P, 2, BANK])

        kq_in = [s.sem(f"kq_in{g}") for g in range(GROUPS)]
        kc_in, v_in = s.sem("kc_in"), s.sem("v_in")
        q2_in = [s.sem(f"q2_in{g}") for g in range(2)]
        scored = s.sem("scored")
        copied = s.sem("copied")
        thr_ok = s.sem("thr_ok")
        dmask = s.sem("dmask")
        pmask = s.sem("pmask")
        exped = s.sem("exped")
        turned = s.sem("turned")
        pT_free = [s.sem(f"pT_free{j}") for j in range(2)]
        av = s.sem("av")
        oT_ok = s.sem("oT_ok")
        back = s.sem("back")
        divided = s.sem("divided")
        o_ok = s.sem("o_ok")
        stored = [s.sem(f"stored{j}") for j in range(2)]
        dve = s.sem("dve")
        passed = s.sem("passed")
        pad = s.sem("pad")
        CUT = 240
        b = s.block()

        def dense(k):
            return k % BLKU == GROUP

        closers = [k for k in range(U) if k % BLKU == GROUP - 1 or k % (2 * BLKU) == 2 * BLKU - 1]
        GR = len(closers)

        def group_of(k):
            return closers.index(k // (2 * BLKU) * 2 * BLKU + 2 * BLKU - 1 if dense(k) else k // BLKU * BLKU + GROUP - 1)

        def unit(bi, r, k):
            return (bi * ROUNDS + r) * U + k

        def tile(bi, r, k):
            return (bi * ROUNDS + r) * 2 + k // TU

        def turns_before(bi, r, k, phase):
            n = (bi * ROUNDS + r) * (U + 2) + k + (k > TU + 3)
            return n if phase == "first" or k > 3 else n - 1

        def pT_uses(bi, r, k, phase):
            return (bi * ROUNDS + r) * (U + 2) + (TU + 4 if k < TU else U + 1 if phase == "drain" else U + 1 + 4)

        def sparse_no(bi, r, k):
            return (bi * ROUNDS + r) * (2 * HEADS0) + k // BLKU * GROUP + k % BLKU

        @b.sync
        def _(e):
            def load_stacks(bi, g):
                now, heads = bass.ds(bi * SEQ, SEQ), slice(g * GROUP, (g + 1) * GROUP)
                e.wait_ge(scored, bi * BU + BLKU * g + GROUP)
                e.sem_inc(passed, 1)
                for dst, name, part in ((q, "qP", Q_PART), (k, "kP", K_PART)):
                    for slot in range(SLOTS):
                        src = scr[name][part[slot]].rearrange("(h d) n -> d h n", d=HD0)
                        e.dma_start(dst[slot * HD0:(slot + 1) * HD0, heads, :], src[:, heads, now]
                                    ).then_inc(kq_in[g], 16)

            def load_q2(t, g):
                e.wait_ge(scored, t * TU + 2 * BLKU * (g + 1))
                e.sem_inc(passed, 1)
                e.dma_start(q2[:, g, :], chunked(scr["q2T"])[:, g, bass.ds(t * P, P)]).then_inc(q2_in[g], 16)

            with e.Fori(0, BATCH) as bi:
                load_stacks(bi, 0)
                load_stacks(bi, 1)
                load_q2(bi * QT, 0)
                load_stacks(bi, 2)
                e.wait_ge(scored, bi * BU + TU)
                e.sem_inc(passed, 1)
                e.dma_start(kc[:], scr["kcT"][:, bass.ds(bi * SEQ, SEQ)]).then_inc(kc_in, 16)
                load_stacks(bi, 3)
                load_q2(bi * QT, 1)
                e.wait_ge(av, bi * (GR * ROUNDS) + GR)
                e.sem_inc(passed, 1)
                e.dma_start(v[:, :, 0:DIM], tiled(scr["v"], bi, QT)).then_inc(v_in, 16)
                e.dma_start(vc[:], tiled(scr["vc"], bi, QT)).then_inc(v_in, 16)
                with e.Fori(1, QT) as t:
                    load_q2(bi * QT + t, 0)
                    load_q2(bi * QT + t, 1)

        @b.tensor
        def _(e):
            e.sem_inc(scored, TU)
            e.sem_inc(turned, 2 * R)
            e.sem_inc(av, GR)
            e.sem_inc(back, 1)

            def scores(bi, r, u, phase):
                n = unit(bi, r, u)
                blk = u % TU // BLKU
                h = blk * GROUP + u % BLKU
                if phase in ("first", "open") and u < TU:
                    if u % BLKU == 0:
                        e.wait_ge(kq_in[blk], 16 * 2 * SLOTS * (bi + 1))
                    if u == GROUP:
                        e.wait_ge(kc_in, 16 * (bi + 1))
                if dense(u) and blk % 2 == 0:
                    e.wait_ge(q2_in[blk // 2], 16 * (tile(bi, r, u) + 1))
                e.wait_ge(copied, n + 1)
                for c in range(SEQ // BANK):
                    keys = slice(c * BANK, (c + 1) * BANK)
                    if dense(u):
                        rows = slice(HD1 * (blk % 2), HD1 * (blk % 2) + HD1)
                        m = e.matmul(pS[:, u % 2, keys], q2[rows, blk // 2, :], kc[rows, keys], start=True, stop=True)
                    else:
                        m = e.matmul(pS[:, u % 2, keys], q[:, h, bass.ds((r * 2 + u // TU) * P, P)], k[:, h, keys],
                                     start=True, stop=True)
                m.then_inc(scored, 1)

            def turn(bi, r, u, phase):
                n, before = unit(bi, r, u), turns_before(bi, r, u, phase)
                e.wait_ge(exped, n + 1 + R)
                for j in range(2):
                    e.wait_ge(pT_free[j], before + 1)
                    for c in range(4 * j, 4 * j + 4):
                        m = e.transpose(pT[:, j, (c % 4) * P:(c % 4 + 1) * P], w[:, u % R, c * P:(c + 1) * P], ident[:])
                    m.then_inc(turned, 1)

            def outputs(bi, r, u, phase, half):
                if u not in closers:
                    return
                if phase in ("first", "open") and u == closers[0] and half == 0:
                    e.wait_ge(v_in, 32 * (bi + 1))
                    e.wait_ge(pad, 1)
                if u % TU in (GROUP - 1, 2 * BLKU - 1) and half == 0:
                    e.wait_ge(oT_ok, tile(bi, r, u) + 1)
                e.wait_ge(pT_free[half], turns_before(bi, r, u, phase) + 2)
                blk = u % TU // BLKU
                for c in range(half * QT // 2, (half + 1) * QT // 2):
                    for j in range(2 if dense(u) else GROUP):
                        if dense(u):
                            slot = (u - BLKU * (1 - j)) % RT
                            out = pO[HD1 * j:HD1 * (j + 1), 1, blk // 2 * P:(blk // 2 + 1) * P]
                            vals = vc[:, c, :]
                        else:
                            slot, h = (u - (GROUP - 1) + j) % RT, blk * GROUP + j
                            out = pO[WIDE * j:WIDE * (j + 1), 0, blk * P:(blk + 1) * P]
                            vals = v[:, c, h * HD0:h * HD0 + WIDE]
                        m = e.matmul(out, vals, wT[:, slot, c * P:(c + 1) * P], start=(c == 0), stop=(c == QT - 1),
                                     skip_group_check=True)
                if half == 1:
                    m.then_inc(av, 1)

            def outputs0(bi, r, u, phase):
                outputs(bi, r, u, phase, 0)

            def outputs1(bi, r, u, phase):
                outputs(bi, r, u, phase, 1)

            def turn_back(bi, r, u, phase):
                if u % TU != TU - 1:
                    return
                t = tile(bi, r, u)
                before = pT_uses(bi, r, u, phase)
                e.wait_ge(oT_ok, t + 1 + 1)
                for j in range(2):
                    e.wait_ge(pT_free[j], before + 1)
                    for g in range((GROUPS, 2)[j]):
                        m = e.transpose(pT[:, j, g * P:(g + 1) * P], oT[:, j, g * P:(g + 1) * P], ident[:])
                m.then_inc(back, 1)

            long_ticks(e, BATCH, ROUNDS, U, [(0, scores), (5, turn), (8, outputs1), (7, outputs0), (9, turn_back)])

        @b.scalar
        def _(e):
            e.sem_inc(copied, 2)
            e.sem_inc(exped, R)
            e.sem_inc(oT_ok, 1)
            for j in range(2):
                e.sem_inc(pT_free[j], 1)
                e.sem_inc(stored[j], 32)

            def copy(bi, r, u, phase):
                n = unit(bi, r, u)
                e.wait_ge(scored, n + 1 + TU)
                e.wait_ge(dmask, n + 1)
                e.wait_ge(pmask, 2 * n + 2)
                e.wait_ge(exped, n + 1)
                e.activation(sb[:, u % R, :], pS[:, u % 2, :], ACT.Copy).then_inc(copied, 1)

            def exp(bi, r, u, phase):
                n = unit(bi, r, u)
                e.wait_ge(dmask, n + 1 + R)
                e.wait_ge(pmask, 2 * n + 2 + 2 * R)
                if dense(u):
                    e.wait_ge(turned, 2 * n + 2)
                if u % TU == 0:
                    e.wait_ge(o_ok, tile(bi, r, u) + 1)
                e.activation(w[:, u % R, :], (sb if dense(u) else w)[:, u % R, :], ACT.Exp,
                             bias=negm[:, u % R:u % R + 1],
                             accum_out=sums[:, u // TU, u % TU:u % TU + 1]).then_inc(exped, 1)

            def copy_turned(bi, r, u, phase):
                n, g = unit(bi, r, u), (bi * ROUNDS + r) * GR
                e.wait_ge(av, g + group_of(u - RT) + 1 + GR if u >= RT else g + group_of(u - RT + U) + 1)
                for j in range(2):
                    e.wait_ge(turned, 2 * n + j + 1 + 2 * R)
                    e.activation(wT[:, u % RT, j * BANK:(j + 1) * BANK], pT[:, j, :], ACT.Copy).then_inc(pT_free[j], 1)

            def outputs_out(bi, r, u, phase):
                if u % TU != TU - 1:
                    return
                t = tile(bi, r, u)
                e.wait_ge(av, (bi * ROUNDS + r) * GR + group_of(u) + 1 + GR)
                e.wait_ge(back, t + 1)
                e.activation(oT[:, 0, :], pO[:, 0, :], ACT.Copy)
                e.activation(oT[:, 1, 0:2 * P], pO[:, 1, 0:2 * P], ACT.Copy).then_inc(oT_ok, 1)

            def store(bi, r, u, phase):
                if u % TU != TU - 1:
                    return
                t = tile(bi, r, u)
                e.wait_ge(o_ok, t + 1 + 2)
                for j in range(2):
                    e.dma_start(scr[f"o{j}"].rearrange("(t p) d -> p t d", p=P)[:, bass.ds(t, 1), :],
                                o[j][:, u // TU].unsqueeze(1)).then_inc(stored[u // TU], 16)

            long_ticks(e, BATCH, ROUNDS, U, [(0, copy), (4, exp), (5, copy_turned), (8, outputs_out), (12, store)])
            for j in range(2):
                e.wait_ge(stored[j], 32 * (BATCH * ROUNDS + 1))

        @b.vector
        def _(e):
            e.sem_inc(dmask, R)
            e.sem_inc(o_ok, 2)

            def largest(bi, r, u, phase):
                n, z = unit(bi, r, u), u % R
                e.wait_ge(copied, n + 1 + 2)
                e.sem_inc(passed, 1)
                if dense(u):
                    e.reduce_max(m8[:, z, 0:1], sb[:, z, :], AX_X).then_inc(thr_ok, 1)
                else:
                    e.max(m8[:, z, 0:8], sb[:, z, :]).then_inc(dve, 1)

            def mask(bi, r, u, phase):
                n, z = unit(bi, r, u), u % R
                e.wait_ge(turned, 2 * n + 2)
                e.wait_ge(thr_ok, n + 1)
                if dense(u):
                    e.tensor_scalar(negm[:, z:z + 1], m8[:, z, 0:1], -1.0, None, ALU.mult).then_inc(dmask, 1)
                else:
                    e.scalar_tensor_tensor(w[:, z, 0:CUT], sb[:, z, 0:CUT], m8[:, z, TOPK - 1:TOPK],
                                           sb[:, z, 0:CUT], ALU.is_ge, ALU.mult).then_inc(dmask, 1)

            def next_largest(bi, r, u, phase):
                if dense(u):
                    return
                n, sn, z = unit(bi, r, u), sparse_no(bi, r, u), u % R
                e.wait_ge(dve, 2 * sn + 1)
                e.sem_inc(passed, 1)
                e.match_replace(cut[:], m8[:, z, 0:8], sb[:, z, :], NEG).then_inc(dve, 1)
                e.tensor_scalar(negm[:, z:z + 1], m8[:, z, 0:1], 0.0, -1.0, ALU.max, ALU.mult)
                e.wait_ge(dve, 2 * sn + 2)
                e.sem_inc(passed, 1)
                e.max(m8[:, z, 8:16], cut[:]).then_inc(thr_ok, 1)

            def divide(bi, r, u, phase):
                if u % TU != TU - 1:
                    return
                t, half = tile(bi, r, u), u // TU
                e.wait_ge(back, t + 1 + 1)
                e.reciprocal(rsum[:, half, :], sums[:, half, :]).then_inc(divided, 1)
                e.wait_ge(stored[half], 32 * (bi * ROUNDS + r + 1))
                e.wait_ge(divided, t + 1)
                rb = rsum[:, half, :].rearrange("p (b u) -> p b u", u=BLKU)
                e.tensor_tensor(o[0][:, half, :].rearrange("p (b j d) -> p b j d", b=GROUPS, j=GROUP),
                                pT[:, 0, :].rearrange("p (b j d) -> p b j d", b=GROUPS, j=GROUP)[:, :, :, 0:HD0],
                                rb[:, :, 0:GROUP].unsqueeze(3).to_broadcast([P, GROUPS, GROUP, HD0]),
                                ALU.mult).then_inc(pT_free[0], 1)
                e.tensor_tensor(o[1][:, half, :].rearrange("p (h d) -> p h d", h=HEADS1),
                                pT[:, 1, 0:2 * P].rearrange("p (h d) -> p h d", h=HEADS1),
                                rb[:, :, GROUP].unsqueeze(2).to_broadcast([P, HEADS1, HD1]),
                                ALU.mult).then_inc(pT_free[1], 1)
                for j in range(2):
                    e.wait_ge(pT_free[j], pT_uses(bi, r, u, phase) + 2)
                e.sem_inc(o_ok, 1)

            long_ticks(e, BATCH, ROUNDS, U, [(0, largest), (1, mask), (9, divide), (0, next_largest)])

        @b.gpsimd
        def _(e):
            e.sem_inc(pmask, 2 * R)
            e.memset(v[:, :, DIM:], 0.0).then_inc(pad, 1)

            def mask(bi, r, u, phase):
                n, z = unit(bi, r, u), u % R
                if dense(u):
                    e.wait_ge(pmask, 2 * n + 2 * R)
                    e.sem_inc(pmask, 2)
                    return
                e.wait_ge(turned, 2 * n + 2)
                e.wait_ge(thr_ok, n + 1)
                e.sem_inc(passed, 1)
                e.tensor_scalar(w[:, z, CUT:], sb[:, z, CUT:], m8[:, z, TOPK - 1:TOPK], None,
                                ALU.is_ge).then_inc(pmask, 1)
                e.wait_ge(pmask, 2 * n + 1 + 2 * R)
                e.tensor_tensor(w[:, z, CUT:], w[:, z, CUT:], sb[:, z, CUT:], ALU.mult).then_inc(pmask, 1)

            long_ticks(e, BATCH, ROUNDS, U, [(0, mask)])


def split_xT(e, i, src, xT, hi_ok, ok, passed):
    now = bass.ds(i * BLK, BLK)
    e.sem_inc(passed, 1)
    e.tensor_copy(xT[:, HI, :, now], src[:]).then_inc(hi_ok, 1)
    e.wait_ge(hi_ok, i + 1)
    e.sem_inc(passed, 1)
    e.tensor_tensor(xT[:, LO, :, now], src[:], xT[:, HI, :, now], ALU.subtract).then_inc(ok, 1)


class Gate:

    def __init__(self, s):
        t = [P, TILES, EXPERTS]
        self.bias = s.sb("g_bias", [P, EXPERTS])
        self.iota = s.sb("g_iota", [P, EXPERTS])
        self.lg, self.pr, self.oh = s.sb("g_lg", t), s.sb("g_pr", t), s.sb("g_oh", t)
        self.m8, self.ixf = s.sb("g_m8", t), s.sb("g_ixf", t)
        self.ix = s.sb("g_ix", t, U32)
        self.r = s.sb("g_r", [P, TILES])
        self.c = s.sb("g_c", [P, 2, TILES])
        self.exp_in = s.sem("g_exp_in")
        self.exp_out = s.sem("g_exp_out")

    def logits(self, e, i, d, logits):
        e.tensor_tensor(self.lg[:, bass.ds(i * BT, BT), :], logits,
                        self.bias[:].unsqueeze(1).to_broadcast([P, BT, EXPERTS]), ALU.add).then_inc(d.sem, 1)
        d.step()

    def vector(self, e, d, passed, comb, soft):
        t = [P, TILES, EXPERTS]
        many = lambda a: a.unsqueeze(2).to_broadcast(t)
        def tt(out, a, b, op):
            e.tensor_tensor(out, a, b, op).then_inc(d.sem, 1)
            d.step()
            d.wait()
        d.wait()
        e.reduce_max(self.r[:], self.lg[:], AX_X).then_inc(d.sem, 1)
        d.step()
        d.wait()
        e.tensor_tensor(self.lg[:], self.lg[:], many(self.r[:]), ALU.subtract).then_inc(self.exp_in, 1)
        e.wait_ge(self.exp_out, 1)
        e.reduce_sum(self.r[:], self.pr[:], AX_X).then_inc(d.sem, 1)
        d.step()
        d.wait()
        e.reciprocal(self.r[:], self.r[:]).then_inc(d.sem, 1)
        d.step()
        d.wait()
        tt(self.pr[:], self.pr[:], many(self.r[:]), ALU.mult)
        for a in range(TILES):
            e.max(self.m8[:, a, :], self.pr[:, a, :]).then_inc(d.sem, 1)
            d.step()
        d.wait()
        for a in range(TILES):
            e.max_index(self.ix[:, a, :], self.m8[:, a, :], self.pr[:, a, :]).then_inc(d.sem, 1)
            d.step()
        d.wait()
        e.tensor_copy(self.ixf[:], self.ix[:]).then_inc(d.sem, 1)
        d.step()
        if soft:
            e.tensor_tensor(self.c[:, 1, :], self.m8[:, :, 1], self.m8[:, :, 0], ALU.subtract
                            ).then_inc(self.exp_in, 1)
            e.wait_ge(self.exp_out, 2)
            e.tensor_scalar(self.r[:], self.c[:, 1, :], 1.0, None, ALU.add).then_inc(d.sem, 1)
            d.step()
        else:
            e.tensor_tensor(self.r[:], self.m8[:, :, 1], self.m8[:, :, 0], ALU.add).then_inc(d.sem, 1)
            d.step()
        d.wait()
        e.reciprocal(self.r[:], self.r[:]).then_inc(d.sem, 1)
        d.step()
        d.wait()
        if soft:
            e.tensor_copy(self.c[:, 0, :], self.r[:]).then_inc(d.sem, 1)
            d.step()
            tt(self.c[:, 1, :], self.c[:, 1, :], self.r[:], ALU.mult)
        else:
            for m in range(2):
                tt(self.c[:, m, :], self.m8[:, :, m], self.r[:], ALU.mult)
        iota = self.iota[:].unsqueeze(1).to_broadcast(t)
        tt(self.oh[:], iota, many(self.ixf[:, :, 0]), ALU.is_equal)
        tt(self.oh[:], self.oh[:], many(self.c[:, 0, :]), ALU.mult)
        tt(self.lg[:], iota, many(self.ixf[:, :, 1]), ALU.is_equal)
        tt(self.lg[:], self.lg[:], many(self.c[:, 1, :]), ALU.mult)
        tt(comb[:, :, 1:1 + EXPERTS], self.lg[:], self.oh[:], ALU.add)

    def scalar(self, e, soft):
        e.wait_ge(self.exp_in, 1)
        e.activation(self.pr[:], self.lg[:], ACT.Exp).then_inc(self.exp_out, 1)
        if soft:
            e.wait_ge(self.exp_in, 2)
            e.activation(self.c[:, 1, :], self.c[:, 1, :], ACT.Exp).then_inc(self.exp_out, 1)


def route0(nc, I, scr, ident, acc, xT, comb):
    with Stage(nc, "rt") as s:
        wo = [s.sb(f"wo{j}", [P, CH, DIM]) for j in range(2)]
        wr = s.sb("wr", [P, CH, EXPERTS])
        bo = s.sb("bo", [P, DIM])
        g2 = s.sb("g2", [P, CH])
        o = [s.sb(f"o{j}", [P, BT, DIM]) for j in range(2)]
        x = s.sb("x", [P, BT, DIM])
        xn = s.sb("xn", [P, BT, DIM])
        nx = s.sb("nx", [P, BT, DIM])
        sq = s.sb("sq", [P, DIM])
        ms, vs, sd, rs = (s.sb(n, [P, BT]) for n in ("ms", "vs", "sd", "rs"))
        oT = [s.sb(f"oT{j}", [P, CH, BLK]) for j in range(2)]
        nxT = s.sb("nxT", [P, CH, BLK])
        pT = s.ps("pT", [P, CH, BLK])
        pP = s.ps("pP", [P, 2, BT, DIM])
        pL = s.ps("pL", [P, BT, EXPERTS])
        loaded = s.sem("loaded")
        o_in = s.sem("o_in")
        x_in = s.sem("x_in")
        o_T = s.sem("o_T")
        nx_T = s.sem("nx_T")
        oT_ok = s.sem("oT_ok")
        proj = s.sem("proj")
        x2_ok = s.sem("x2_ok")
        sq_ok = s.sem("sq_ok")
        var_ok = s.sem("var_ok")
        root_ok = s.sem("root_ok")
        nx_ok = s.sem("nx_ok")
        nxT_ok = s.sem("nxT_ok")
        logit = s.sem("logit")
        xT_hi = s.sem("xT_hi")
        xT_ok = s.sem("xT_ok")
        done = s.sem("done")
        dve = s.sem("dve")
        passed = s.sem("passed")
        gate = Gate(s)
        b = s.block()
        NW, STEPS = 7, 4

        @b.sync
        def _(e):
            for dst, src in ((wo[0][:], chunked(I["wo"])), (wo[1][:], chunked(I["wo2"])), (wr[:], chunked(I["wr"])),
                             (bo[:], I["bo"].partition_broadcast(P)), (g2[:], I["g2"]),
                             (gate.bias[:], I["ebias"].partition_broadcast(P)),
                             (gate.iota[:], I["iota"].partition_broadcast(P))):
                e.dma_start(dst, src).then_inc(loaded, 16)
            with e.Fori(0, BLOCKS) as i:
                e.wait_ge(o_T, 2 * i + 2)
                for j in range(2):
                    e.dma_start(o[j][:], tiled(scr[f"o{j}"], i)).then_inc(o_in, 16)
                e.wait_ge(done, i + 1)
                e.dma_start(x[:], tiled(I["x"], i)).then_inc(x_in, 16)
                e.dma_start(xn[:], tiled(scr["xn"], i)).then_inc(x_in, 16)

        @b.tensor
        def _(e):
            e.wait_ge(loaded, 16 * NW)
            e.sem_inc(o_T, 2)

            def turn(src):
                for c in range(CH):
                    for a in range(BT):
                        r = e.transpose(pT[:, c, a * P:(a + 1) * P], src[:, a, c * P:(c + 1) * P], ident[:])
                return r

            def front(i):
                e.wait_ge(o_in, 32 * i + 32)
                e.wait_ge(nxT_ok, i + 1)
                turn(o[0]).then_inc(o_T, 1)
                e.wait_ge(oT_ok, 2 * i + 1)
                turn(o[1]).then_inc(o_T, 1)
                e.wait_ge(x2_ok, i + 1)
                for j in range(2):
                    e.wait_ge(oT_ok, 2 * i + j + 1)
                    for a in range(BT):
                        for c in range(CH):
                            r = e.matmul(pP[:, j, a, :], oT[j][:, c, a * P:(a + 1) * P], wo[j][:, c, :],
                                         start=(c == 0), stop=(c == CH - 1))
                    r.then_inc(proj, 1)

            def rest(i, last):
                if not last:
                    front(i + 1)
                e.wait_ge(nx_ok, i + 1)
                turn(nx).then_inc(nx_T, 1)
                e.wait_ge(nxT_ok, i + 1 + 2)
                for a in range(BT):
                    for c in range(CH):
                        r = e.matmul(pL[:, a, :], nxT[:, c, a * P:(a + 1) * P], wr[:, c, :],
                                     start=(c == 0), stop=(c == CH - 1))
                r.then_inc(logit, 1)

            one_ahead(e, front, rest)

        @b.scalar
        def _(e):
            def copy(i):
                for j in range(2):
                    e.wait_ge(o_T, 2 * i + j + 1 + 2)
                    for c in range(CH):
                        r = e.activation(oT[j][:, c, :], pT[:, c, :], ACT.Copy)
                    r.then_inc(oT_ok, 1)

            def rest(i, last):
                if not last:
                    copy(i + 1)
                e.wait_ge(x2_ok, i + 1 + 1)
                for a in range(BT):
                    e.activation(sq[:], xn[:, a, :], ACT.Square, accum_out=ms[:, a:a + 1]).then_inc(sq_ok, 1)
                    e.wait_ge(sq_ok, BT * i + a + 1)
                e.wait_ge(var_ok, i + 1)
                e.activation(sd[:], vs[:], ACT.Sqrt).then_inc(root_ok, 1)

            one_ahead(e, copy, rest)
            gate.scalar(e, True)

        @b.vector
        def _(e):
            e.wait_ge(loaded, 16 * NW)
            e.sem_inc(done, 1)
            e.sem_inc(nxT_ok, 2)
            e.sem_inc(x2_ok, 1)
            with e.Fori(0, BLOCKS) as i:
                d = Tally(e, dve, i, STEPS)
                e.wait_ge(x_in, 32 * i + 32)
                for a in range(BT):
                    r = e.tensor_tensor(x[:, a, :], x[:, a, :], bo[:], ALU.add)
                r.then_inc(dve, 1)
                d.step()
                e.wait_ge(proj, 2 * i + 1)
                d.wait()
                e.tensor_tensor(x[:], x[:], pP[:, 0], ALU.add).then_inc(dve, 1)
                d.step()
                e.wait_ge(proj, 2 * i + 2)
                e.tensor_tensor(xn[:], xn[:], pP[:, 1], ALU.add).then_inc(x2_ok, 1)
                e.wait_ge(x2_ok, i + 1 + 1)
                d.wait()
                e.tensor_tensor(acc[:, bass.ds(i * BT, BT), :], x[:], xn[:], ALU.add)
                e.wait_ge(sq_ok, BT * i + BT)
                e.tensor_scalar(vs[:], ms[:], 1.0 / DIM, 1e-6, ALU.mult, ALU.add).then_inc(var_ok, 1)
                e.wait_ge(root_ok, i + 1)
                e.reciprocal(rs[:], sd[:]).then_inc(dve, 1)
                d.step()
                d.wait()
                for a in range(BT):
                    r = e.tensor_scalar(nx[:, a, :], xn[:, a, :], rs[:, a:a + 1], None, ALU.mult)
                r.then_inc(nx_ok, 1)
                e.wait_ge(nx_ok, i + 1)
                e.sem_inc(done, 1)
                e.wait_ge(xT_ok, i + 1)
                e.wait_ge(nx_T, i + 1)
                for c in range(CH):
                    r = e.tensor_scalar(nxT[:, c, :], pT[:, c, :], g2[:, c:c + 1], None, ALU.mult)
                r.then_inc(nxT_ok, 1)
                e.wait_ge(logit, i + 1)
                gate.logits(e, i, d, pL[:])
                d.close()
            gate.vector(e, Tally(e, dve, BLOCKS, STEPS), passed, comb, True)

        @b.gpsimd
        def _(e):
            e.memset(comb[:, :, 0:1], 1.0)
            e.sem_inc(xT_ok, 1)
            with e.Fori(0, BLOCKS) as i:
                e.wait_ge(nxT_ok, i + 1 + 2)
                split_xT(e, i, nxT, xT, xT_hi, xT_ok, passed)


def experts(nc, I, name, acc, xT, comb, count, ff, swiglu, first, out=None):
    with Stage(nc, name) as s:
        FC = ff // P
        SIDES = 2 if swiglu else 1
        RH = 2 if swiglu else 4
        raw1 = s.sb("raw1", [P, SIDES, CH, ff])
        raw2 = s.sb("raw2", [P, FC, DIM])
        w1 = s.sb("w1", [P, 2, SIDES, CH, ff], F32R)
        w2 = s.sb("w2", [P, 2, FC, DIM], F32R)
        b1 = None if swiglu else s.sb("b1", [P, FC])
        sg = s.sb("sg", [P, 2, BLK]) if swiglu else None
        h32 = s.sb("h32", [P, 2, BLK])
        h = s.sb("h", [P, 2, 2, FC, BLK], F32R)
        pH = s.ps("pH", [P, RH, SIDES, BLK])
        pY = s.ps("pY", [P, 2, BT, DIM])
        w1_in, w2_in = s.sem("w1_in"), s.sem("w2_in")
        w_hi = s.sem("w_hi")
        w1_ok = s.sem("w1_ok")
        w2_ok = s.sem("w2_ok")
        b1_in = s.sem("b1_in")
        hid = s.sem("hid")
        sg_ok = s.sem("sg_ok")
        h_hi = s.sem("h_hi")
        h_ok = s.sem("h_ok")
        y_ok = s.sem("y_ok")
        added = s.sem("added")
        stored = s.sem("stored")
        b = s.block()
        ROUNDS_T = BLOCKS // 2

        def unit(x, r, k):
            return (x * ROUNDS_T + r) * 2 + k

        @b.sync
        def _(e):
            with e.Fori(0, count) as x:
                if b1 is not None:
                    e.wait_ge(h_hi, x * (BLOCKS * FC) + RH)
                    e.dma_start(b1[:], I["b1"][:, bass.ds(x, 1), :].rearrange("p x f -> p (x f)")).then_inc(b1_in, 16)
                e.wait_ge(w1_ok, x + 1)
                for side, wname in enumerate(("w1", "w3")[:SIDES]):
                    e.dma_start(raw1[:, side], I[f"{name}_{wname}"].rearrange("(x c p) f -> p x c f", c=CH, p=P)
                                [:, bass.ds(x, 1), :, :].rearrange("p x c f -> p (x c) f")).then_inc(w1_in, 16)
                e.wait_ge(w2_ok, x + 1)
                e.dma_start(raw2[:], I[f"{name}_w2"].rearrange("(x c p) d -> p x c d", c=FC, p=P)
                            [:, bass.ds(x, 1), :, :].rearrange("p x c d -> p (x c) d")).then_inc(w2_in, 16)
            if out is not None:
                for i in range(BLOCKS):
                    e.wait_ge(added, (count - 1) * BLOCKS + i + 1 + 2)
                    e.dma_start(tiled(out, i), acc[:, i * BT:(i + 1) * BT, :]).then_inc(stored, 16)
                e.wait_ge(stored, 16 * BLOCKS)

        @b.tensor
        def _(e):
            e.sem_inc(hid, 1)
            e.sem_inc(y_ok, 2)

            def hidden(x, r, k, phase):
                n = unit(x, r, k)
                if phase == "open" and k == 0:
                    e.wait_ge(w1_ok, x + 1 + 1)
                for f in range(FC):
                    e.wait_ge(h_hi, n * FC + f + 1)
                    for side in range(SIDES):
                        for j, (pw, px) in enumerate(PRODUCTS):
                            for c in range(CH):
                                m = e.matmul(pH[:, (k * FC + f) % RH, side, :], w1[:, pw, side, c, f * P:(f + 1) * P],
                                             xT[:, px, c, bass.ds((r * 2 + k) * BLK, BLK)],
                                             start=(j == 0 and c == 0), stop=(j == len(PRODUCTS) - 1 and c == CH - 1))
                    m.then_inc(hid, 1)

            def output(x, r, k, phase):
                n = unit(x, r, k)
                if phase == "open" and k == 0:
                    e.wait_ge(w2_ok, x + 1 + 1)
                e.wait_ge(added, n + 1)
                e.wait_ge(h_ok, n * FC + FC + 2)
                for a in range(BT):
                    for f in range(FC):
                        for j, (ph, pw) in enumerate(PRODUCTS):
                            m = e.matmul(pY[:, k, a, :], h[:, k, ph, f, a * P:(a + 1) * P], w2[:, pw, f, :],
                                         start=(f == 0 and j == 0), stop=(f == FC - 1 and j == len(PRODUCTS) - 1))
                m.then_inc(y_ok, 1)

            ticks(e, count, ROUNDS_T, 2, [(0, hidden), (1, output)])

        @b.scalar
        def _(e):
            if not swiglu:
                e.sem_inc(h_hi, RH)

            def weights(x, r, k, phase):
                if phase == "open" and k == 0:
                    e.wait_ge(w1_in, 16 * SIDES * (x + 1))
                    e.wait_ge(hid, x * (BLOCKS * FC) + 1)
                    e.activation(w1[:, HI], raw1[:], ACT.Copy).then_inc(w_hi, 1)
                    e.wait_ge(w2_in, 16 * (x + 1))
                    e.wait_ge(y_ok, x * BLOCKS + 2)
                    e.activation(w2[:, HI], raw2[:], ACT.Copy).then_inc(w_hi, 1)

            def act(x, r, k, phase):
                n = unit(x, r, k)
                if not swiglu:
                    e.wait_ge(y_ok, n + 1)
                    if phase == "open" and k == 0:
                        e.wait_ge(b1_in, 16 * (x + 1))
                for f in range(FC):
                    e.wait_ge(hid, n * FC + f + 1 + 1)
                    if swiglu:
                        e.wait_ge(h_hi, n * FC + f + 1)
                        e.activation(sg[:, f % 2, :], pH[:, (k * FC + f) % RH, 0, :], ACT.Silu).then_inc(sg_ok, 1)
                    else:
                        e.wait_ge(h_ok, n * FC + f + 1)
                        for dst in (h32[:, f % 2, :], h[:, k, HI, f, :]):
                            m = e.activation(dst, pH[:, (k * FC + f) % RH, 0, :], ACT.Relu, bias=b1[:, f:f + 1])
                        m.then_inc(h_hi, 1)

            ticks(e, count, ROUNDS_T, 2, [(0, weights), (0, act)])

        @b.vector
        def _(e):
            if swiglu:
                e.sem_inc(h_hi, RH)
            e.sem_inc(added, 2)
            e.sem_inc(w2_ok, 1)

            def weights(x, r, k, phase):
                if phase == "open" and k == 0:
                    e.wait_ge(w_hi, 2 * x + 2)
                    e.tensor_tensor(w2[:, LO], raw2[:], w2[:, HI], ALU.subtract).then_inc(w2_ok, 1)

            def multiply(x, r, k, phase):
                n = unit(x, r, k)
                e.wait_ge(y_ok, n + 1)
                for f in range(FC):
                    e.wait_ge(sg_ok, n * FC + f + 1)
                    e.wait_ge(h_ok, n * FC + f + 1)
                    for dst in (h32[:, f % 2, :], h[:, k, HI, f, :]):
                        m = e.tensor_tensor(dst, sg[:, f % 2, :], pH[:, (k * FC + f) % RH, 1, :], ALU.mult)
                    m.then_inc(h_hi, 1)

            def add(x, r, k, phase):
                n = unit(x, r, k)
                e.wait_ge(y_ok, n + 1 + 2)
                if phase == "open" and k == 0:
                    e.wait_ge(added, x * BLOCKS + 2)
                for a in range(BT):
                    t = (r * 2 + k) * BT + a
                    now = acc[:, bass.ds(t, 1), :].rearrange("p t d -> p (t d)")
                    m = e.scalar_tensor_tensor(now, pY[:, k, a, :], comb[:, bass.ds(t, 1), bass.ds(x + first, 1)]
                                               .rearrange("p t x -> p (t x)"), now, ALU.mult, ALU.add)
                m.then_inc(added, 1)

            ticks(e, count, ROUNDS_T, 2, [(0, weights), (0, multiply), (1, add)] if swiglu else [(0, weights), (1, add)])

        @b.gpsimd
        def _(e):
            e.sem_inc(h_ok, 2)
            e.sem_inc(w1_ok, 1)

            def weights(x, r, k, phase):
                if phase == "open" and k == 0:
                    e.wait_ge(w_hi, 2 * x + 1)
                    e.tensor_tensor(w1[:, LO], raw1[:], w1[:, HI], ALU.subtract).then_inc(w1_ok, 1)

            def rest(x, r, k, phase):
                for f in range(FC):
                    m = unit(x, r, k) * FC + f
                    e.wait_ge(h_hi, m + 1 + RH)
                    e.tensor_tensor(h[:, k, LO, f, :], h32[:, f % 2, :], h[:, k, HI, f, :], ALU.subtract).then_inc(h_ok, 1)

            ticks(e, count, ROUNDS_T, 2, [(0, weights), (0, rest)])


def project1(nc, I, scr, ident, acc, xT, comb):
    with Stage(nc, "p1") as s:
        wq = s.sb("wq", [P, CH, DIM])
        wk = s.sb("wk", [P, CH, DIM])
        wv = s.sb("wv", [P, CH, DIM])
        wg = s.sb("wg", [P, CH, EXPERTS])
        b2 = s.sb("b2", [EXPERTS, DIM])
        wm, wsum = s.sb("wm", [P, CH]), s.sb("wsum", [P, CH])
        xn = s.sb("xn", [P, BT, DIM])
        st, mv = s.sb("st", [P, BT, 6]), s.sb("mv", [P, BT, 2])
        vs, sd, rs = (s.sb(n, [P, BT]) for n in ("vs", "sd", "rs"))
        xnT = s.sb("xnT", [P, CH, BLK])
        qk = s.sb("qk", [P, 2 * CH, BLK])
        v = s.sb("v", [P, BT, DIM])
        cb = s.sb("cb", [P, 2, BT, EXPERTS])
        cT = s.sb("cT", [EXPERTS, 2, BLK])
        pT = s.ps("pT", [P, CH, BLK])
        pP = s.ps("pP", [P, 2 * CH, BLK])
        pV = s.ps("pV", [P, BT, DIM])
        loaded = s.sem("loaded")
        w_ok = s.sem("w_ok")
        var_ok, root_ok = s.sem("var_ok"), s.sem("root_ok")
        xn_ok = s.sem("xn_ok")
        turned = s.sem("turned")
        xnT_ok = s.sem("xnT_ok")
        xT_hi = s.sem("xT_hi")
        xT_ok = s.sem("xT_ok")
        logit = s.sem("logit")
        proj = s.sem("proj")
        qk_ok = s.sem("qk_ok")
        v_ps = s.sem("v_ps")
        v_ok = s.sem("v_ok")
        cb_ok = s.sem("cb_ok")
        cb_T = s.sem("cb_T")
        cT_ok = s.sem("cT_ok")
        b2_ps = s.sem("b2_ps")
        b2_ok = s.sem("b2_ok")
        stored = s.sem("stored")
        dve = s.sem("dve")
        passed = s.sem("passed")
        gate = Gate(s)
        NW, NST, STEPS = 7, 3, 2 * BT + 2

        def biases(e, *steps):
            ticks(e, 1, BLOCKS // 2, 2, steps)

        b = s.block()

        @b.sync
        def _(e):
            for dst, src in ((wq[:], chunked(I["l1wq"])), (wk[:], chunked(I["l1wk"])), (wv[:], chunked(I["l1wvT"])),
                             (wg[:], chunked(I["gate_w"])), (b2[:], I["b2"]),
                             (gate.bias[:], I["gate_b"].partition_broadcast(P)),
                             (gate.iota[:], I["iota"].partition_broadcast(P))):
                e.dma_start(dst, src).then_inc(loaded, 16)
            e.sem_inc(stored, 16)
            with e.Fori(0, BLOCKS) as i:
                now = bass.ds(i * BLK, BLK)
                e.wait_ge(v_ok, i + 2)
                e.dma_start(tiled(scr["v1"], i), v[:]).then_inc(stored, 16)
                e.wait_ge(qk_ok, 4 * i + 8)
                e.dma_start(chunked(scr["q1T"])[:, :, now], qk[:, 0:CH, :]).then_inc(stored, 16)
                e.dma_start(chunked(scr["k1T"])[:, :, now], qk[:, CH:, :]).then_inc(stored, 16)
            e.wait_ge(stored, 16 * NST * BLOCKS + 16)

        @b.tensor
        def _(e):
            e.wait_ge(loaded, 16 * NW)
            e.wait_ge(w_ok, 2 * CH + 4)
            e.sem_inc(turned, 1)
            e.sem_inc(cb_T, 2)
            e.sem_inc(b2_ps, 2)
            with e.Fori(0, BLOCKS) as i:
                e.wait_ge(xn_ok, i + 1)
                for c in range(CH):
                    for a in range(BT):
                        r = e.transpose(pT[:, c, a * P:(a + 1) * P], xn[:, a, c * P:(c + 1) * P], ident[:])
                r.then_inc(turned, 1)
                e.wait_ge(xnT_ok, i + 1)
                for a in range(BT):
                    for c in range(CH):
                        r = e.matmul(pT[:, 0, a * EXPERTS:(a + 1) * EXPERTS], xnT[:, c, a * P:(a + 1) * P],
                                     wg[:, c, :], start=(c == 0), stop=(c == CH - 1))
                r.then_inc(logit, 1)
                e.wait_ge(v_ok, i + 1)
                for a in range(BT):
                    for c in range(CH):
                        r = e.matmul(pV[:, a, :], xnT[:, c, a * P:(a + 1) * P], wv[:, c, :],
                                     start=(c == 0), stop=(c == CH - 1))
                r.then_inc(v_ps, 1)
                k = 0
                for w in (wq, wk):
                    for m in range(CH):
                        e.wait_ge(qk_ok, 4 * i + k + 1)
                        for c in range(CH):
                            r = e.matmul(pP[:, k, :], w[:, c, m * P:(m + 1) * P], xnT[:, c, :],
                                         start=(c == 0), stop=(c == CH - 1))
                        r.then_inc(proj, 1)
                        k += 1

            def turn(_, r, k, phase):
                n = r * 2 + k
                e.wait_ge(cb_ok, n + 1)
                e.wait_ge(cT_ok, n + 1)
                for a in range(BT):
                    m = e.transpose(pT[0:EXPERTS, k, a * P:(a + 1) * P], cb[:, k, a, :], ident[:])
                m.then_inc(cb_T, 1)

            def product(_, r, k, phase):
                n = r * 2 + k
                e.wait_ge(cT_ok, n + 1 + 2)
                e.wait_ge(b2_ok, n + 1)
                for a in range(BT):
                    m = e.matmul(pP[:, 2 * k + a // 2, a % 2 * DIM:(a % 2 + 1) * DIM], cT[:, k, a * P:(a + 1) * P],
                                 b2[:], start=True, stop=True)
                m.then_inc(b2_ps, 1)

            e.wait_ge(qk_ok, 4 * BLOCKS + 4)
            biases(e, (0, turn), (1, product))

        @b.scalar
        def _(e):
            e.sem_inc(qk_ok, 4)
            e.sem_inc(cT_ok, 2)
            e.wait_ge(w_ok, CH + 1)
            for c in range(CH):
                e.activation(wv[:, c, :], wv[:, c, :], ACT.Exp, bias=wm[:, c:c + 1],
                             accum_out=wsum[:, c:c + 1]).then_inc(w_ok, 1)
                e.wait_ge(w_ok, CH + 1 + c + 1)

            def root(i):
                e.wait_ge(var_ok, i + 1)
                e.activation(sd[:], vs[:], ACT.Sqrt).then_inc(root_ok, 1)

            def rest(i, last):
                e.wait_ge(turned, i + 2)
                e.wait_ge(xT_ok, i + 1)
                for c in range(CH):
                    r = e.activation(xnT[:, c, :], pT[:, c, :], ACT.Copy)
                r.then_inc(xnT_ok, 1)
                if not last:
                    root(i + 1)
                e.wait_ge(stored, 16 * NST * i + 16)
                for k in range(2 * CH):
                    e.wait_ge(proj, 2 * CH * i + k + 1)
                    e.activation(qk[:, k, :], pP[:, k, :], ACT.Copy).then_inc(qk_ok, 1)

            one_ahead(e, root, rest)
            gate.scalar(e, False)

            def copy(_, r, k, phase):
                n = r * 2 + k
                e.wait_ge(cb_T, n + 1 + 2)
                e.wait_ge(b2_ps, n + 1)
                e.activation(cT[:, k], pT[0:EXPERTS, k, :], ACT.Copy).then_inc(cT_ok, 1)

            biases(e, (0, copy))

        @b.vector
        def _(e):
            e.wait_ge(loaded, 16 * NW)
            e.sem_inc(v_ok, 1)
            e.sem_inc(b2_ok, 2)
            for c in range(CH):
                e.reduce_max(wm[:, c:c + 1], wv[:, c, :], AX_X).then_inc(w_ok, 1)
            e.wait_ge(w_ok, CH)
            e.tensor_scalar(wm[:], wm[:], -1.0, None, ALU.mult).then_inc(w_ok, 1)
            e.wait_ge(w_ok, 2 * CH + 1)
            e.reciprocal(wsum[:], wsum[:]).then_inc(w_ok, 1)
            e.wait_ge(w_ok, 2 * CH + 2)
            for c in range(CH):
                e.tensor_scalar(wv[:, c, :], wv[:, c, :], wsum[:, c:c + 1], 1.0 / DIM, ALU.mult,
                                ALU.mult).then_inc(w_ok, 1)

            def layernorm(i):
                d = Tally(e, dve, i, STEPS)
                one = [acc[:, bass.ds(i * BT + a, 1), :].rearrange("p t d -> p (t d)") for a in range(BT)]
                for a in range(BT):
                    e.bn_stats(st[:, a, :], one[a]).then_inc(dve, 1)
                    d.step()
                d.wait()
                e.sem_inc(passed, 1)
                for a in range(BT):
                    e.bn_aggr(mv[:, a, :], st[:, a, :]).then_inc(dve, 1)
                    d.step()
                d.wait()
                e.tensor_scalar(vs[:], mv[:, :, 1], 1e-5, None, ALU.add).then_inc(var_ok, 1)
                e.wait_ge(root_ok, i + 1)
                e.reciprocal(rs[:], sd[:]).then_inc(dve, 1)
                d.step()
                e.wait_ge(turned, i + 1)
                d.wait()
                for a in range(BT):
                    r = e.tensor_scalar(xn[:, a, :], one[a], mv[:, a, 0:1], rs[:, a:a + 1], ALU.subtract, ALU.mult)
                r.then_inc(xn_ok, 1)

            def rest(i, last):
                d = Tally(e, dve, i, STEPS)
                d.step(2 * BT + 1)
                e.wait_ge(logit, i + 1)
                gate.logits(e, i, d, pT[:, 0, 0:BT * EXPERTS].rearrange("p (a x) -> p a x", a=BT))
                d.close()
                if not last:
                    layernorm(i + 1)
                now = acc[:, bass.ds(i * BT, BT), :]
                e.wait_ge(stored, 16 * NST * i + 16)
                e.wait_ge(v_ps, i + 1)
                e.tensor_copy(v[:], pV[:])
                e.tensor_tensor(now, now, pV[:], ALU.subtract).then_inc(v_ok, 1)

            one_ahead(e, layernorm, rest)
            gate.vector(e, Tally(e, dve, BLOCKS, STEPS), passed, comb, False)
            e.wait_ge(v_ok, BLOCKS + 1)

            def pick(_, r, k, phase):
                n = r * 2 + k
                e.wait_ge(cb_T, n + 1)
                e.tensor_copy(cb[:, k], comb[:, bass.ds(n * BT, BT), 1:1 + EXPERTS]).then_inc(cb_ok, 1)

            def add(_, r, k, phase):
                n = r * 2 + k
                now = acc[:, bass.ds(n * BT, BT), :]
                e.wait_ge(b2_ps, n + 1 + 2)
                e.tensor_tensor(now, now, pP[:, 2 * k:2 * k + 2, :].rearrange("p b (a d) -> p (b a) d", a=2),
                                ALU.add).then_inc(b2_ok, 1)

            biases(e, (0, pick), (2, add))

        @b.gpsimd
        def _(e):
            e.sem_inc(xT_ok, 1)
            with e.Fori(0, BLOCKS) as i:
                e.wait_ge(xnT_ok, i + 1)
                split_xT(e, i, xnT, xT, xT_hi, xT_ok, passed)


def attend1(nc, scr, acc):
    with Stage(nc, "a1") as s:
        qT, kT = s.sb("qT", [P, CH, SEQ]), s.sb("kT", [P, CH, SEQ])
        v, vn = s.sb("v", [P, QT, DIM]), s.sb("vn", [P, QT, DIM])
        w = s.sb("w", [P, QT, SEQ])
        top, negm, sums, rsum = (s.sb(n, [P, QT]) for n in ("top", "negm", "sums", "rsum"))
        pS = s.ps("pS", [P, 2, SEQ])
        pO = s.ps("pO", [P, 4, BANK])
        qk_in, v_in = s.sem("qk_in"), s.sem("v_in")
        scored = s.sem("scored")
        max_ok = s.sem("max_ok")
        neg_ok = s.sem("neg_ok")
        exped = s.sem("exped")
        inv_ok = s.sem("inv_ok")
        vn_ok = s.sem("vn_ok")
        av = s.sem("av")
        added = s.sem("added")
        SCALE = SEQ ** -0.5
        b = s.block()

        @b.sync
        def _(e):
            with e.Fori(0, BATCH) as i:
                now = bass.ds(i * SEQ, SEQ)
                e.wait_ge(scored, QT * i + 1)
                e.dma_start(kT[:], chunked(scr["k1T"])[:, :, now]).then_inc(qk_in, 16)
                e.dma_start(qT[:], chunked(scr["q1T"])[:, :, now]).then_inc(qk_in, 16)
                e.wait_ge(av, QT * i + 1)
                e.dma_start(v[:], tiled(scr["v1"], i, QT)).then_inc(v_in, 16)

        @b.tensor
        def _(e):
            e.sem_inc(scored, 1)
            e.sem_inc(av, 1)
            with e.Fori(0, BATCH) as i:
                e.wait_ge(qk_in, 32 * i + 32)
                for m in range(QT):
                    e.wait_ge(exped, QT * i + m + 1)
                    for half in range(2):
                        for c in range(CH):
                            r = e.matmul(pS[:, m % 2, half * BANK:(half + 1) * BANK], kT[:, c, m * P:(m + 1) * P],
                                         qT[:, c, half * BANK:(half + 1) * BANK], start=(c == 0), stop=(c == CH - 1))
                    r.then_inc(scored, 1)
                for n in range(QT):
                    e.wait_ge(added, QT * i + n + 1)
                    for m in range(QT):
                        if n == 0:
                            e.wait_ge(vn_ok, QT * i + m + 1)
                        r = e.matmul(pO[:, n % 4, 0:DIM], w[:, m, n * P:(n + 1) * P], vn[:, m, :],
                                     start=(m == 0), stop=(m == QT - 1))
                    r.then_inc(av, 1)

        @b.scalar
        def _(e):
            e.sem_inc(exped, 2)
            with e.Fori(0, BATCH) as i:
                for m in range(QT):
                    e.wait_ge(neg_ok, QT * i + m + 1)
                    if m == 0:
                        e.wait_ge(av, QT * i + 1)
                    e.activation(w[:, m, :], pS[:, m % 2, :], ACT.Exp, bias=negm[:, m:m + 1], scale=SCALE,
                                 accum_out=sums[:, m:m + 1]).then_inc(exped, 1)

        @b.vector
        def _(e):
            e.sem_inc(added, 4)
            with e.Fori(0, BATCH) as i:
                def divide(m):
                    n = QT * i + m
                    e.wait_ge(exped, n + 1 + 2)
                    e.reciprocal(rsum[:, m:m + 1], sums[:, m:m + 1]).then_inc(inv_ok, 1)
                    if m == 0:
                        e.wait_ge(v_in, 16 * i + 16)
                        e.wait_ge(av, QT * i + 1)
                    e.wait_ge(inv_ok, n + 1)
                    e.tensor_scalar(vn[:, m, :], v[:, m, :], rsum[:, m:m + 1], None, ALU.mult).then_inc(vn_ok, 1)

                for m in range(QT):
                    n = QT * i + m
                    e.wait_ge(scored, n + 1 + 1)
                    e.reduce_max(top[:, m:m + 1], pS[:, m % 2, :], AX_X).then_inc(max_ok, 1)
                    e.wait_ge(max_ok, n + 1)
                    e.tensor_scalar(negm[:, m:m + 1], top[:, m:m + 1], -SCALE, None, ALU.mult).then_inc(neg_ok, 1)
                    if m:
                        divide(m - 1)
                divide(QT - 1)
                for n in range(QT):
                    e.wait_ge(av, QT * i + n + 1 + 1)
                    now = acc[:, bass.ds(i * QT + n, 1), :].rearrange("p t d -> p (t d)")
                    e.tensor_tensor(now, now, pO[:, n % 4, 0:DIM], ALU.add).then_inc(added, 1)


def build(nc, I, out, upto=99, dbg=None):
    kind = "ExternalOutput" if dbg else "Internal"
    def dram(name, shape):
        return nc.dram_tensor(f"scr_{name}", shape, BF16 if len(shape) == 3 else F32, kind=kind).ap()
    scr = {n: dram(n, sh) for n, sh in (
        ("xn", (TOK, DIM)), ("qP", (PARTS, DIM, TOK)), ("kP", (PARTS, DIM, TOK)), ("v", (TOK, DIM)), ("q2T", (DIM, TOK)),
        ("kcT", (P, TOK)), ("vc", (TOK, HD1)), ("o0", (TOK, DIM)), ("o1", (TOK, DIM)),
        ("q1T", (DIM, TOK)), ("k1T", (DIM, TOK)), ("v1", (TOK, DIM)))}
    with ExitStack() as ctx:
        ident = ctx.enter_context(nc.sbuf_tensor("ident", [P, P], F32))
        project0(nc, I, scr, ident)
        attend(nc, scr, ident)
        acc = ctx.enter_context(nc.sbuf_tensor("acc", [P, TILES, DIM], F32))
        xT = ctx.enter_context(nc.sbuf_tensor("xT", [P, 2, CH, TOK], F32R))
        comb = ctx.enter_context(nc.sbuf_tensor("comb", [P, TILES, 1 + EXPERTS], F32))
        route0(nc, I, scr, ident, acc, xT, comb)
        experts(nc, I, "e0", acc, xT, comb, 1 + EXPERTS, FF0, True, 0)
        project1(nc, I, scr, ident, acc, xT, comb)
        attend1(nc, scr, acc)
        experts(nc, I, "e1", acc, xT, comb, EXPERTS, FF1, False, 1, out)


def columns(a):
    return a.reshape(-1, P).T


def kernel(**inputs):
    import numpy as np
    import concourse.bacc as bacc
    from concourse.bass_utils import run_bass_kernel_spmd as run

    a = {k: np.asarray(v) for k, v in inputs.items()}
    L0, F0, L1, F1 = "L0_attn_", "L0_ffn_", "L1_attn_", "L1_ffn_"
    arrays = {
        "x": a[L0 + "x"].reshape(TOK, DIM),
        "wq": a[L0 + "Wq"], "wk": a[L0 + "Wk"], "wv": a[L0 + "Wv"],
        "bq": columns(a[L0 + "bq"]), "bk": columns(a[L0 + "bk"]),
        "bv": a[L0 + "bv"], "wo": a[L0 + "Wo"], "bo": a[L0 + "bo"],
        "g1": columns(a[F0 + "g1"]), "g2": columns(a[F0 + "g2"]),
        "wq2": a[F0 + "Wq"].T, "wkc": np.concatenate([a[F0 + "Wkc"].T] * 2, axis=1), "wvc": a[F0 + "Wvc"].T,
        "wo2": a[F0 + "Wo"].T, "wr": a[F0 + "Wr"].T, "ebias": a[F0 + "expert_bias"],
        "e0_w1": np.concatenate([a[F0 + "sW1"].T[None], a[F0 + "eW1"].transpose(0, 2, 1)]).reshape(-1, FF0),
        "e0_w3": np.concatenate([a[F0 + "sW3"].T[None], a[F0 + "eW3"].transpose(0, 2, 1)]).reshape(-1, FF0),
        "e0_w2": np.concatenate([a[F0 + "sW2"].T[None], a[F0 + "eW2"].transpose(0, 2, 1)]).reshape(-1, DIM),
        "l1wq": a[L1 + "wq"], "l1wk": a[L1 + "wk"], "l1wvT": a[L1 + "wv"].T,
        "gate_w": a[F1 + "gate_w"], "gate_b": a[F1 + "gate_b"],
        "e1_w1": a[F1 + "w1"].reshape(-1, FF1), "e1_w2": a[F1 + "w2"].reshape(-1, DIM),
        "b1": a[F1 + "b1"].reshape(EXPERTS, FF1 // P, P).transpose(2, 0, 1), "b2": a[F1 + "b2"],
        "ident": np.eye(P, dtype=np.float32), "iota": np.arange(EXPERTS, dtype=np.float32),
    }
    arrays = {f"in_{k}": np.ascontiguousarray(v) for k, v in arrays.items()}
    nc = bacc.Bacc("TRN2", target_bir_lowering=False, num_devices=1)
    I = {k[3:]: nc.dram_tensor(k, v.shape, mybir.dt.from_np(v.dtype), kind="ExternalInput").ap()
         for k, v in arrays.items()}
    out = nc.dram_tensor("out", (TOK, DIM), F32, kind="ExternalOutput").ap()
    build(nc, I, out)
    r = run(nc, [arrays], core_ids=[0])
    return r.results[0]["out"].reshape(BATCH, SEQ, DIM)
```
